# Optimizing a Trainium2 kernel written in Bass

```python
import numpy as np
import jax
import jax.numpy as jnp

def _softmax(x, axis=-1):
    return jax.nn.softmax(x, axis=axis)

def _gelu(x):
    return jax.nn.gelu(x, approximate=True)

def _silu(x):
    return jax.nn.silu(x)

def _sigmoid(x):
    return jax.nn.sigmoid(x)

def _layernorm(x, axis=-1, eps=1e-05):
    m = jnp.mean(x, axis=axis, keepdims=True)
    v = jnp.var(x, axis=axis, keepdims=True)
    return (x - m) / jnp.sqrt(v + eps)

def _scatter_add(tgt, idx, src, axis=0):
    return tgt.at[idx].add(src)

def _segment_sum(src, seg, n):
    return jax.ops.segment_sum(src, seg, n)
kernel_name = 'mk_gps_d1_gnn_r8_977a46'

def setup_inputs(seed: int=0):
    np.random.seed(seed)
    _w = jnp.asarray

    def _rec_inputs():
        import jax
        import jax.numpy as jnp
        _gk = jax.random.key(seed)
        x = -0.0003713 + 1 * jax.random.normal(jax.random.fold_in(_gk, 1), (6250, 256), jnp.float32)
        _s = jax.random.randint(jax.random.fold_in(_gk, 2), (100000,), 0, 6250, jnp.int32)
        _d = jax.random.randint(jax.random.fold_in(_gk, 3), (100000,), 0, 6250, jnp.int32)
        _loop = jnp.arange(6250, dtype=jnp.int32)
        src = jnp.concatenate([_s, _d, _loop])
        dst = jnp.concatenate([_d, _s, _loop])
        _o = jnp.argsort(dst, stable=True)
        src = src[_o]
        dst = dst[_o]
        return (x, src, dst)
    x, src, dst = _rec_inputs()

    def _L0_gnn_setup():
        import jax, jax.numpy as jnp
        import numpy as np
        N_NODES = 6250
        N_EDGES = 100000
        IN_DIM = 256
        HEADS = 4
        F_HEAD = 64
        NEG_SLOPE = 0.2
        key = jax.random.key(seed)
        k1, k2, k3, k4, k5 = jax.random.split(key, 5)
        x = jax.random.normal(k1, (N_NODES, IN_DIM), dtype=jnp.float32)
        edge_index = jax.random.randint(k2, (2, N_EDGES), 0, N_NODES, dtype=jnp.int64)
        scale = 1.0 / np.sqrt(IN_DIM)
        W = jax.random.normal(k3, (HEADS, IN_DIM, F_HEAD), dtype=jnp.float32) * scale
        att_src = jax.random.normal(k4, (HEADS, F_HEAD), dtype=jnp.float32) * scale
        att_dst = jax.random.normal(k5, (HEADS, F_HEAD), dtype=jnp.float32) * scale
        bias = jnp.zeros((HEADS * F_HEAD,), dtype=jnp.float32)
        return {'x': x, 'edge_index': edge_index, 'W': W, 'att_src': att_src, 'att_dst': att_dst, 'bias': bias}
    _L0_gnn_all = _L0_gnn_setup()
    _L0_gnn_in = {k: v for k, v in _L0_gnn_all.items() if k in ('W', 'att_src', 'att_dst', 'bias')}
    del _L0_gnn_all

    def _L0_mix_setup():
        import jax, jax.numpy as jnp
        import numpy as np
        DIM = 256
        HEADS = 4
        DIM_HEAD = 32
        NUM_MEM = 4
        HIDDEN = HEADS * DIM_HEAD
        SCALE = DIM_HEAD ** (-0.5)

        def rmsnorm(x, g):
            n = jnp.linalg.norm(x, axis=-1, keepdims=True)
            return x / jnp.maximum(n, 1e-12) * g * x.shape[-1] ** 0.5
        key = jax.random.key(seed)
        ks = jax.random.split(key, 8)
        B, N = (4, 2048)
        return {'x': jax.random.normal(ks[0], (B, N, DIM), jnp.float32), 't': jax.random.normal(ks[1], (B,), jnp.float32), 'w_qkv': jax.random.normal(ks[2], (DIM, 3 * HIDDEN), jnp.float32) * 0.02, 'mem_kv': jax.random.normal(ks[3], (2, HEADS, DIM_HEAD, NUM_MEM), jnp.float32), 'w_out': jax.random.normal(ks[4], (HIDDEN, DIM), jnp.float32) * 0.02, 'b_out': jnp.zeros((DIM,), jnp.float32), 'g_out': jnp.ones((DIM,), jnp.float32), 'g_pre': jnp.ones((DIM,), jnp.float32)}
    _L0_mix_all = _L0_mix_setup()
    _L0_mix_in = {k: v for k, v in _L0_mix_all.items() if k in ('t', 'w_qkv', 'mem_kv', 'w_out', 'b_out', 'g_out', 'g_pre')}
    del _L0_mix_all

    def _L0_ffn_setup():
        import jax, jax.numpy as jnp
        import numpy as np
        E = 8
        K = 2
        D = 256
        H = 512
        DOUT = 256
        EPS = 1e-05
        key = jax.random.key(seed)
        ks = jax.random.split(key, 9)
        s = 0.02
        return {'x': jax.random.normal(ks[0], (4, 1024, D), jnp.float32), 'gamma': 1.0 + 0.05 * jax.random.normal(ks[1], (D,), jnp.float32), 'beta': 0.05 * jax.random.normal(ks[2], (D,), jnp.float32), 'Wr': 0.01 * jax.random.normal(ks[3], (D, E), jnp.float32), 'br': jnp.zeros((E,), jnp.float32), 'W1': s * jax.random.normal(ks[4], (E, D, H), jnp.float32), 'b1': s * jax.random.normal(ks[5], (E, H), jnp.float32), 'W2': s * jax.random.normal(ks[6], (E, H, DOUT), jnp.float32), 'b2': s * jax.random.normal(ks[7], (E, DOUT), jnp.float32)}
    _L0_ffn_all = _L0_ffn_setup()
    _L0_ffn_in = {k: v for k, v in _L0_ffn_all.items() if k in ('gamma', 'beta', 'Wr', 'br', 'W1', 'b1', 'W2', 'b2')}
    del _L0_ffn_all
    return {'x': x, 'src': src, 'dst': dst, 'L0_gnn_W': _L0_gnn_in['W'], 'L0_gnn_att_src': _L0_gnn_in['att_src'], 'L0_gnn_att_dst': _L0_gnn_in['att_dst'], 'L0_gnn_bias': _L0_gnn_in['bias'], 'L0_mix_t': _L0_mix_in['t'], 'L0_mix_w_qkv': _L0_mix_in['w_qkv'], 'L0_mix_mem_kv': _L0_mix_in['mem_kv'], 'L0_mix_w_out': _L0_mix_in['w_out'], 'L0_mix_b_out': _L0_mix_in['b_out'], 'L0_mix_g_out': _L0_mix_in['g_out'], 'L0_mix_g_pre': _L0_mix_in['g_pre'], 'L0_ffn_gamma': _L0_ffn_in['gamma'], 'L0_ffn_beta': _L0_ffn_in['beta'], 'L0_ffn_Wr': _L0_ffn_in['Wr'], 'L0_ffn_br': _L0_ffn_in['br'], 'L0_ffn_W1': _L0_ffn_in['W1'], 'L0_ffn_b1': _L0_ffn_in['b1'], 'L0_ffn_W2': _L0_ffn_in['W2'], 'L0_ffn_b2': _L0_ffn_in['b2']}

def reference(x, src, dst, L0_gnn_W, L0_gnn_att_src, L0_gnn_att_dst, L0_gnn_bias, L0_mix_t, L0_mix_w_qkv, L0_mix_mem_kv, L0_mix_w_out, L0_mix_b_out, L0_mix_g_out, L0_mix_g_pre, L0_ffn_gamma, L0_ffn_beta, L0_ffn_Wr, L0_ffn_br, L0_ffn_W1, L0_ffn_b1, L0_ffn_W2, L0_ffn_b2):
    import jax
    import jax.numpy as jnp

    def _L0_gnn_ref(x, edge_index, W, att_src, att_dst, bias):
        import jax, jax.numpy as jnp
        import numpy as np
        N_NODES = 6250
        N_EDGES = 100000
        IN_DIM = 256
        HEADS = 4
        F_HEAD = 64
        NEG_SLOPE = 0.2
        N = x.shape[0]
        H, Fh = att_src.shape
        loops = jnp.arange(N, dtype=edge_index.dtype)
        src = jnp.concatenate([edge_index[0], loops])
        dst = jnp.concatenate([edge_index[1], loops])
        h = jnp.einsum('nd,hdf->nhf', x, W)
        a_src = jnp.einsum('nhf,hf->nh', h, att_src)
        a_dst = jnp.einsum('nhf,hf->nh', h, att_dst)
        e = jax.nn.leaky_relu(a_src[src] + a_dst[dst], NEG_SLOPE)
        emax = jax.lax.stop_gradient(jax.ops.segment_max(e, dst, num_segments=N))
        ex = jnp.exp(e - emax[dst])
        denom = jax.ops.segment_sum(ex, dst, num_segments=N)
        alpha = ex / denom[dst]
        msg = h[src] * alpha[:, :, None]
        out = jax.ops.segment_sum(msg, dst, num_segments=N)
        return out.reshape(N, H * Fh) + bias

    def _L0_mix_ref(x, t, w_qkv, mem_kv, w_out, b_out, g_out, g_pre):
        import jax, jax.numpy as jnp
        import numpy as np
        DIM = 256
        HEADS = 4
        DIM_HEAD = 32
        NUM_MEM = 4
        HIDDEN = HEADS * DIM_HEAD
        SCALE = DIM_HEAD ** (-0.5)

        def rmsnorm(x, g):
            n = jnp.linalg.norm(x, axis=-1, keepdims=True)
            return x / jnp.maximum(n, 1e-12) * g * x.shape[-1] ** 0.5
        b, n, c = x.shape
        xn = rmsnorm(x, g_pre)
        qkv = xn @ w_qkv
        q, k, v = jnp.split(qkv, 3, axis=-1)

        def to_heads(z):
            return z.reshape(b, n, HEADS, DIM_HEAD).transpose(0, 2, 3, 1)
        q, k, v = map(to_heads, (q, k, v))
        mk = jnp.broadcast_to(mem_kv[0], (b, HEADS, DIM_HEAD, NUM_MEM))
        mv = jnp.broadcast_to(mem_kv[1], (b, HEADS, DIM_HEAD, NUM_MEM))
        k = jnp.concatenate([mk, k], axis=-1)
        v = jnp.concatenate([mv, v], axis=-1)
        q = jax.nn.softmax(q, axis=-2) * SCALE
        k = jax.nn.softmax(k, axis=-1)
        context = jnp.einsum('bhdn,bhen->bhde', k, v)
        out = jnp.einsum('bhde,bhdn->bhen', context, q)
        out = out.transpose(0, 3, 1, 2).reshape(b, n, HIDDEN)
        out = rmsnorm(out @ w_out + b_out, g_out)
        return out + x

    def _L0_ffn_ref(x, gamma, beta, Wr, br, W1, b1, W2, b2):
        import jax, jax.numpy as jnp
        import numpy as np
        E = 8
        K = 2
        D = 256
        H = 512
        DOUT = 256
        EPS = 1e-05
        mu = jnp.mean(x, axis=-1, keepdims=True)
        var = jnp.mean(jnp.square(x - mu), axis=-1, keepdims=True)
        xn = (x - mu) * jax.lax.rsqrt(var + EPS) * gamma + beta
        logits = jnp.einsum('bsd,de->bse', xn, Wr) + br
        top_vals, top_idx = jax.lax.top_k(logits, K)
        w = jax.nn.softmax(top_vals, axis=-1)
        w_full = jnp.einsum('bsk,bske->bse', w, jax.nn.one_hot(top_idx, E, dtype=w.dtype))
        y = jnp.zeros(x.shape[:-1] + (DOUT,), x.dtype)
        for e in range(E):
            h = jax.nn.gelu(jnp.einsum('bsd,dh->bsh', xn, W1[e]) + b1[e], approximate=False)
            y_e = jnp.einsum('bsh,hd->bsd', h, W2[e]) + b2[e]
            y = y + y_e * w_full[..., e, None]
        return y
    edge_index = jnp.stack([src, dst])
    xn = _layernorm(x, axis=-1)
    x = x + _L0_gnn_ref(xn, edge_index, L0_gnn_W, L0_gnn_att_src, L0_gnn_att_dst, L0_gnn_bias) + _L0_mix_ref(xn[None], L0_mix_t, L0_mix_w_qkv, L0_mix_mem_kv, L0_mix_w_out, L0_mix_b_out, L0_mix_g_out, L0_mix_g_pre)[0]
    x = x + _L0_ffn_ref(_layernorm(x, axis=-1)[None], L0_ffn_gamma, L0_ffn_beta, L0_ffn_Wr, L0_ffn_br, L0_ffn_W1, L0_ffn_b1, L0_ffn_W2, L0_ffn_b2)[0]
    return x

_drawn_inputs = setup_inputs


def setup_inputs(seed=0):
    import zlib

    import numpy as np

    out = dict(_drawn_inputs(seed))
    spreads = {'L0_gnn_bias': (0.0, 0.1),
     'L0_mix_b_out': (0.0, 0.1),
     'L0_mix_g_out': (1.0, 0.2),
     'L0_mix_g_pre': (1.0, 0.6),
     'L0_ffn_br': (0.0, 0.372)}
    factors = {'L0_gnn_att_dst': 4.807,
     'L0_mix_w_qkv': 8.0,
     'L0_mix_mem_kv': 8.0,
     'L0_mix_w_out': 8.0,
     'L0_ffn_gamma': 8.0,
     'L0_ffn_beta': 8.0,
     'L0_ffn_Wr': 3.463,
     'L0_ffn_b1': 22.9,
     'L0_ffn_b2': 8.0}
    for name, (base, spread) in spreads.items():
        noise = np.random.default_rng([zlib.crc32(name.encode()), seed]).standard_normal(out[name].shape)
        drawn = base * np.exp(spread * noise) if base else spread * noise
        out[name] = jnp.asarray(drawn.astype(out[name].dtype))
    for name, factor in factors.items():
        out[name] = (out[name] * factor).astype(out[name].dtype)
    return out
```

```python
from contextlib import ExitStack

import concourse.bass as bass
from concourse import mybir

ALU = mybir.AluOpType
ACT = mybir.ActivationFunctionType
AX = mybir.AxisListType
F32 = mybir.dt.float32
I32 = mybir.dt.int32

P = 128
N_NODES = 6250
DIM = 256
TILES = -(-N_NODES // P)
N_PAD = TILES * P
LAST = N_NODES - (TILES - 1) * P
KC = DIM // P

G_HEADS = 4
F_HEAD = DIM // G_HEADS
ROW = DIM + G_HEADS
SLOPE = 0.2
LN_EPS = 1e-5

N_EDGES = 206250
SUB = 4
BLOCK = SUB * P
BLOCKS = -(-N_EDGES // BLOCK)
WIN = 32
ACC_W = N_PAD + WIN
WINDOWS = -(-N_NODES // WIN)
GUARD = 40.0

M_HEADS = 4
D_HEAD = 32
HID = M_HEADS * D_HEAD
N_MEM = 4
QKV_W = 3 * HID + 4

EXPERTS = 8
FF = 512
FC = FF // P
MOE_TILES = (2 * N_NODES + EXPERTS * (P - 1)) // P
SLOTS = MOE_TILES * P


class Own:

    def __init__(self, eng, sem):
        self.eng, self.sem, self.base, self.k = eng, sem, 0, 0

    def step(self, ins):
        ins.then_inc(self.sem, 1)
        self.k += 1
        return ins

    def wait(self):
        self.eng.wait_ge(self.sem, self.base + self.k)

    def do(self, ins):
        self.step(ins)
        self.wait()


def repeat(eng, own, first, total, unroll, per, body):
    full = (total - first) // unroll
    start = own.base + own.k
    if full:
        with eng.Fori(0, full) as it:
            for u in range(unroll):
                n = it * unroll + (first + u)
                own.base, own.k = start + (it * unroll + u) * per, 0
                body(n, (first + u) % unroll)
                assert own.k == per, (own.k, per)
    for n in range(first + full * unroll, total):
        own.base, own.k = start + (n - first) * per, 0
        body(n, n % unroll)
        assert own.k == per, (own.k, per)
    own.base, own.k = start + (total - first) * per, 0


def bcast(ap, axis, n):
    v = ap.unsqueeze(axis)
    shape = list(v.shape)
    shape[axis] = n
    return v.to_broadcast(shape)


def at(n, size=1):
    return bass.ds(n * size, size)


def gps_layer(nc, x, src, dst, g_W, g_asrc, g_adst, g_bias, w_qkv, mem_kv, w_out, b_out, g_out, g_pre,
              gamma, beta, Wr, br, W1, b1, W2, b2, out):
    table = nc.dram_tensor("node_table", [N_PAD, ROW], F32)
    dst_table = nc.dram_tensor("dst_table", [ACC_W, 2 * G_HEADS], F32)
    base_rows = nc.dram_tensor("base_rows", [N_PAD, DIM], F32)
    expert_in = nc.dram_tensor("expert_in", [SLOTS, DIM], F32)
    expert_out = nc.dram_tensor("expert_out", [SLOTS, DIM], F32)

    ctx = ExitStack()
    with ctx:
        def sb(name, shape, dt=F32, stack=ctx):
            return stack.enter_context(nc.sbuf_tensor(name, shape, dt))

        acc = sb("acc", [P, ACC_W * 4])
        region = sb("region", [P, TILES * QKV_W])
        ident = sb("ident", [P, P])
        ones = sb("ones", [P, P])
        valid = sb("valid", [P, TILES])
        sd = sb("sd", [P, TILES * 8])
        w_self = sb("w_self", [P, TILES * G_HEADS])
        spans = sb("spans", [1, 2], I32)

        node_stage(nc, ctx, locals())
        edge_buffers = {}
        edge_stage(nc, locals())
        any_order_stage(nc, locals())

        W = EXPERTS * KC * FF
        w1_sb = region[:, 0:W].rearrange("p (e c f) -> p e c f", e=EXPERTS, c=KC)
        w2_sb = region[:, W:2 * W].rearrange("p (e c f) -> p e c f", e=EXPERTS, c=FC)
        b2_sb = region[:, 2 * W:2 * W + EXPERTS * DIM]
        ye_sb = region[:, 2 * W + EXPERTS * DIM:2 * W + (EXPERTS + 2) * DIM]
        logits = sb("logits", [P, TILES * EXPERTS])
        wr = sb("wr", [P, KC * EXPERTS])
        place = sb("place", [P, 2 * TILES], I32)
        gate = sb("gate", [P, 2 * TILES])
        tile_expert = sb("tile_expert", [1, MOE_TILES], I32)
        weights_in = ctx.enter_context(nc.semaphore("weights_in"))
        rows_stage(nc, locals())
        route_stage(nc, locals())
        expert_stage(nc, locals())


def node_stage(nc, ctx0, g):
    acc, region, ident, ones, valid, sd, w_self = (g[k] for k in ("acc", "region", "ident", "ones", "valid", "sd", "w_self"))
    table, dst_table, base_rows = g["table"], g["dst_table"], g["base_rows"]
    x_all = acc[:, 0:TILES * DIM].rearrange("p (t d) -> p t d", d=DIM)
    qkv = region[:, :].rearrange("p (t c) -> p t c", c=QKV_W)
    sd3 = sd[:, :].rearrange("p (t c) -> p t c", c=8)
    X_GROUPS = 7
    XG = TILES // X_GROUPS

    used = [TILES * DIM]

    def carve(*shape):
        size = 1
        for d in shape:
            size *= d
        v = acc[:, used[0]:used[0] + size]
        used[0] += size
        return v if len(shape) == 1 else v.rearrange("p (a b) -> p a b", b=shape[1])

    with ExitStack() as ctx:
        def sb(name, shape, dt=F32):
            return ctx.enter_context(nc.sbuf_tensor(name, shape, dt))

        def pb(name, shape):
            return ctx.enter_context(nc.psum_tensor(name, shape, F32))

        def sem(name):
            return ctx.enter_context(nc.semaphore(name))

        w_h = carve(KC, DIM + 8)
        w_q = carve(KC, 3 * HID)
        gpre = sb("gpre", [P, KC])
        att = carve(2, DIM)
        rows = carve(3, DIM)
        w_o = sb("w_o", [P, DIM])
        mem_k = sb("mem_k", [N_MEM, HID])
        mem_v = sb("mem_v", [N_MEM, HID + 4])
        tmp = sb("tmp", [P, DIM])
        st = sb("st", [P, TILES, 6])
        mv = sb("mv", [P, TILES, 2])
        s1 = sb("s1", [P, TILES])
        s2 = sb("s2", [P, TILES])
        rstd = sb("rstd", [P, TILES])
        r_scale = sb("r_scale", [P, TILES])
        r_bias = sb("r_bias", [P, TILES])
        un_scale = sb("un_scale", [P, TILES])
        eps = sb("eps", [P, 2])
        xr = carve(2, DIM)
        xrT = carve(2, DIM)
        hrow = carve(2, DIM + 8)
        small = carve(8, TILES * G_HEADS)
        drow = sb("drow", [P, TILES * 8])
        kmb = sb("kmb", [P, HID])
        kcol = sb("kcol", [P, 2])
        cmat = sb("cmat", [P, HID])
        cT = sb("cT", [P, HID])
        mmat = sb("mmat", [P, DIM])
        qT = carve(2, P)
        qn = carve(2, P)
        ps_t = pb("ps_t", [P, 2, DIM])
        ps_h = [pb(f"ps_h{i}", [P, 512]) for i in range(2)]
        ps_q = [pb(f"ps_q{i}", [P, 512]) for i in range(2)]
        ps_c = pb("ps_c", [P, 512])
        ps_m = pb("ps_m", [P, 512])

        x_in = [sem(f"x_in{i}") for i in range(X_GROUPS)]
        loads = sem("loads")
        consts = sem("consts")
        own_v, own_p, own_a = sem("own_v"), sem("own_p"), sem("own_a")
        stats = sem("stats")
        sqrt1, sqrt2 = sem("sqrt1"), sem("sqrt2")
        r_ready = sem("r_ready")
        weights = sem("weights")
        xr_ready, xT_ps, xT_ready = sem("xr_ready"), sem("xT_ps"), sem("xT_ready")
        h_ps, q_ps, h_ready, q_ready = sem("h_ps"), sem("q_ps"), sem("h_ready"), sem("q_ready")
        table_out = [sem(f"table_out{i}") for i in range(2)]
        x_done = sem("x_done")
        smax_ready, smax_T, gdiag, gmax_ps = sem("smax_ready"), sem("smax_T"), sem("gdiag"), sem("gmax_ps")
        dlog, dexp, drow_ready, d_out = sem("dlog"), sem("dexp"), sem("drow_ready"), sem("d_out")
        kmax_ready, kmax_T, kdiag, kmax_ps = sem("kmax_ready"), sem("kmax_T"), sem("kdiag"), sem("kmax_ps")
        k_shift, k_exp = sem("k_shift"), sem("k_exp")
        q_shift, q_exp, q_norm = sem("q_shift"), sem("q_exp"), sem("q_norm")
        ctx_ps, c_ready, cT_ps, cT_ready, m_ps, m_ready = (sem(n) for n in ("ctx_ps", "c_ready", "cT_ps", "cT_ready", "m_ps", "m_ready"))
        qn_ready = sem("qn_ready")
        qT_ps, qT_ready, o_ps, o_ready = sem("qT_ps"), sem("qT_ready"), sem("o_ps"), sem("o_ready")
        ss_ready, ss_sqrt, b_ready, b_out = sem("ss_ready"), sem("ss_sqrt"), sem("b_ready"), sem("b_outs")
        block = ctx.enter_context(nc.Block())
        N_LOADS = 12

        @block.sync
        def _(sp):
            xv = g["x"].rearrange("(t p) d -> p t d", p=P)
            for i in range(X_GROUPS):
                sp.dma_start(x_all[:, i * XG:(i + 1) * XG, :], xv[:, i * XG:(i + 1) * XG, :]).then_inc(x_in[i], 16)
            def body(n, s):
                sp.wait_ge(h_ready, n + 3)
                sp.dma_start(table[at(n, P), :], hrow[:, s, 0:ROW]).then_inc(table_out[s], 16)
            for_sp(sp, TILES, body)
            sp.wait_ge(drow_ready, 1)
            sp.dma_start(dst_table[0:N_PAD, :].rearrange("(t p) c -> p t c", p=P),
                         drow[:, :].rearrange("p (t c) -> p t c", c=8)).then_inc(d_out, 16)
            sp.dma_start(dst_table[N_PAD:ACC_W, :], tmp[0:WIN, 0:8]).then_inc(d_out, 16)
            sp.wait_ge(b_ready, 1)
            sp.dma_start(base_rows[:, :].rearrange("(t p) d -> p t d", p=P), x_all).then_inc(b_out, 16)
            for i in range(2):
                sp.wait_ge(table_out[i], 16 * ((TILES + 1 - i) // 2))
            sp.wait_ge(d_out, 32)
            sp.wait_ge(b_out, 16)

        @block.gpsimd
        def _(pool):
            pool.memset(ident[:, :], 0.0).then_inc(own_p, 1)
            pool.memset(valid[:, :], 1.0).then_inc(own_p, 1)
            pool.memset(ones[:, :], 1.0).then_inc(consts, 1)
            pool.wait_ge(own_p, 2)
            pool.affine_select(out=ident[:, :], in_=ident[:, :], compare_op=ALU.not_equal, fill=1.0, base=0,
                               pattern=[[-1, P]], channel_multiplier=1).then_inc(consts, 1)
            pool.affine_select(out=valid[:, :], in_=valid[:, :], compare_op=ALU.is_gt, fill=0.0, base=N_NODES,
                               pattern=[[-P, TILES]], channel_multiplier=-1).then_inc(consts, 1)
            pool.wait_ge(q_norm, 1)

            def q_rows(n, s):
                pool.wait_ge(qT_ps, n + 1)
                pool.tensor_tensor(qn[:, s, :].rearrange("p (h d) -> p h d", d=D_HEAD),
                                   qkv[:, at(n), 0:HID].squeeze(1).rearrange("p (h d) -> p h d", d=D_HEAD),
                                   bcast(small[:, 2, at(n, G_HEADS)], 2, D_HEAD), ALU.mult).then_inc(qn_ready, 1)
            repeat(pool, Own(pool, own_p), 0, TILES, 2, 0, q_rows)

        @block.scalar
        def _(act):
            own = Own(act, own_a)
            for c in range(KC):
                act.dma_start(w_h[:, c, 0:DIM].rearrange("p (h f) -> p h f", f=F_HEAD),
                              g["g_W"][:, c * P:(c + 1) * P, :].rearrange("h p f -> p h f")).then_inc(loads, 16)
            act.dma_start(w_q[:, :, :], g["w_qkv"].rearrange("(c p) n -> p c n", p=P)).then_inc(loads, 16)
            act.dma_start(gpre[:, :], g["g_pre"].rearrange("(c p) -> p c", p=P), allow_slow_non_contiguous=True).then_inc(loads, 16)
            for i, a in enumerate((g["g_asrc"], g["g_adst"])):
                act.dma_start(att[:, i, :], a.rearrange("h f -> (h f)").partition_broadcast(P)).then_inc(loads, 16)
            for i, a in enumerate((g["g_bias"], g["b_out"], g["g_out"])):
                act.dma_start(rows[:, i, :], a.partition_broadcast(P)).then_inc(loads, 16)
            act.dma_start(w_o[:, :], g["w_out"]).then_inc(loads, 16)
            act.dma_start(mem_k[:, :], g["mem_kv"][0].rearrange("h d m -> m (h d)"), allow_slow_non_contiguous=True).then_inc(loads, 16)
            act.dma_start(mem_v[:, 0:HID], g["mem_kv"][1].rearrange("h d m -> m (h d)"), allow_slow_non_contiguous=True).then_inc(loads, 16)
            act.wait_ge(stats, 1)
            act.activation(s1[:, :], mv[:, :, 1], ACT.Sqrt, bias=eps[:, 0:1]).then_inc(sqrt1, 1)
            act.wait_ge(stats, 2)
            act.activation(s2[:, :], s1[:, :], ACT.Sqrt).then_inc(sqrt2, 1)
            act.wait_ge(r_ready, 1)

            def unit_rows(n, s):
                act.wait_ge(xT_ps, n + 1)
                act.wait_ge(q_ready, n + 1)
                act.activation(xr[:, s, :], x_all[:, at(n), :].squeeze(1), ACT.Identity,
                               bias=r_bias[:, at(n)], scale=r_scale[:, at(n)]).then_inc(xr_ready, 1)

            def table_rows(n, s):
                act.wait_ge(h_ps, n + 1)
                act.activation(hrow[:, s, :], ps_h[s][:, 0:DIM + 8], ACT.Copy, scale=un_scale[:, at(n)]).then_inc(h_ready, 1)

            for_act(act, TILES, unit_rows, table_rows, table_out)
            act.wait_ge(dlog, 1)
            act.activation(w_self[:, :], small[:, 0, :], ACT.Exp).then_inc(dexp, 1)
            act.wait_ge(k_shift, 1)
            act.activation(qkv[:, :, HID:2 * HID], qkv[:, :, HID:2 * HID], ACT.Exp).then_inc(k_exp, 1)
            act.activation(mem_k[:, :], mem_k[:, :], ACT.Exp).then_inc(k_exp, 1)
            act.wait_ge(q_shift, 1)
            act.activation(qkv[:, :, 0:HID], qkv[:, :, 0:HID], ACT.Exp).then_inc(q_exp, 1)

            def q_copy(n, s):
                act.wait_ge(qT_ps, n + 3)
                act.activation(qT[:, s, :], ps_q[s][:, 0:P], ACT.Copy).then_inc(qT_ready, 1)
            repeat(act, own, 0, TILES, 2, 0, q_copy)
            act.wait_ge(ss_ready, 1)
            act.activation(s2[:, :], s1[:, :], ACT.Sqrt).then_inc(ss_sqrt, 1)

        @block.tensor
        def _(pe):
            own = Own(pe, own_p)
            pe.sem_inc(xT_ps, 2)
            pe.sem_inc(qT_ps, 2)
            pe.wait_ge(consts, 3)
            pe.wait_ge(weights, 1)

            def body(n, s):
                pe.wait_ge(xr_ready, n + 1)
                for c in range(KC):
                    m = pe.transpose(ps_t[:, s, c * P:(c + 1) * P], xr[:, s, c * P:(c + 1) * P], ident[:, :])
                m.then_inc(xT_ps, 1)
                pe.wait_ge(xT_ready, n + 1)
                pe.wait_ge(h_ready, n + 1)
                for c in range(KC):
                    m = pe.matmul(ps_h[s][:, 0:DIM + 8], xrT[:, s, c * P:(c + 1) * P], w_h[:, c, :],
                                  start=c == 0, stop=c == KC - 1)
                m.then_inc(h_ps, 1)
                pe.wait_ge(q_ready, n + 1)
                for c in range(KC):
                    m = pe.matmul(ps_q[s][:, 0:3 * HID], xrT[:, s, c * P:(c + 1) * P], w_q[:, c, :],
                                  start=c == 0, stop=c == KC - 1)
                m.then_inc(q_ps, 1)
            repeat(pe, own, 0, TILES, 2, 0, body)
            pe.wait_ge(smax_ready, 1)
            pe.transpose(ps_c[0:G_HEADS, 0:P], small[:, 7, 0:G_HEADS], ident[:, :]).then_inc(smax_T, 1)
            pe.wait_ge(gdiag, 1)
            pe.matmul(ps_c[:, 256:256 + G_HEADS], ones[0:G_HEADS, :], tmp[0:G_HEADS, 128:128 + G_HEADS],
                      start=True, stop=True).then_inc(gmax_ps, 1)
            pe.wait_ge(kmax_ready, 1)
            pe.transpose(ps_t[:, 0, 0:P], kmb[:, :], ident[:, :]).then_inc(kmax_T, 1)
            pe.wait_ge(kdiag, 1)
            pe.matmul(ps_t[:, 1, 0:HID], ones[:, :], cmat[:, :], start=True, stop=True).then_inc(kmax_ps, 1)
            pe.wait_ge(k_exp, 2)
            for n in range(TILES):
                rows_n = P if n < TILES - 1 else LAST
                pe.matmul(ps_m[:, 0:HID + 4], qkv[0:rows_n, n, HID:2 * HID], qkv[0:rows_n, n, 2 * HID:QKV_W],
                          start=n == 0, stop=False)
            pe.matmul(ps_m[:, 0:HID + 4], mem_k[:, :], mem_v[:, :], start=False, stop=True).then_inc(ctx_ps, 1)
            pe.wait_ge(c_ready, 1)
            pe.transpose(ps_t[:, 0, 0:P], cmat[:, :], ident[:, :]).then_inc(cT_ps, 1)
            pe.wait_ge(cT_ready, 1)
            pe.matmul(ps_m[:, 0:DIM], cT[:, :], w_o[:, :], start=True, stop=True).then_inc(m_ps, 1)
            pe.wait_ge(m_ready, 1)

            def mix(n, s):
                pe.wait_ge(o_ready, n + 1)
                pe.wait_ge(qn_ready, n + 1)
                pe.transpose(ps_q[s][:, 0:P], qn[:, s, :], ident[:, :]).then_inc(qT_ps, 1)
                pe.wait_ge(qT_ready, n + 1)
                pe.matmul(ps_h[s][:, 0:DIM], qT[:, s, :], mmat[:, :], start=True, stop=True).then_inc(o_ps, 1)
            repeat(pe, own, 0, TILES, 2, 0, mix)

        @block.vector
        def _(dve):
            own = Own(dve, own_v)
            dve.sem_inc(h_ready, 2)
            dve.sem_inc(q_ready, 2)
            dve.sem_inc(o_ready, 2)
            dve.memset(eps[:, 0:1], LN_EPS)
            own.do(dve.memset(qkv[:, :, 3 * HID:QKV_W], 1.0))
            for i in range(X_GROUPS):
                dve.wait_ge(x_in[i], 16)

                def moments(n, s):
                    own.step(dve.bn_stats(st[:, at(n + i * XG), :].squeeze(1), x_all[:, at(n + i * XG), :].squeeze(1)))
                repeat(dve, own, 0, XG, 1, 1, moments)
            own.wait()
            join_moments(dve, own, st, mv, s1)
            dve.sem_inc(stats, 1)
            dve.wait_ge(sqrt1, 1)
            own.do(dve.reciprocal(rstd[:, :], s1[:, :]))
            own.do(dve.tensor_tensor(s2[:, :], rstd[:, :], rstd[:, :], ALU.mult))
            own.do(dve.tensor_tensor(s2[:, :], s2[:, :], mv[:, :, 1], ALU.mult))
            own.do(dve.tensor_scalar(s1[:, :], s2[:, :], float(DIM), 1e-24, ALU.mult, ALU.max))
            dve.sem_inc(stats, 1)
            dve.wait_ge(sqrt2, 1)
            own.do(dve.tensor_scalar(un_scale[:, :], s2[:, :], 1.0 / 16, None, ALU.mult))
            own.do(dve.reciprocal(s1[:, :], un_scale[:, :]))
            own.do(dve.tensor_tensor(r_scale[:, :], s1[:, :], rstd[:, :], ALU.mult))
            own.do(dve.scalar_tensor_tensor(out=r_bias[:, :], in0=mv[:, :, 0], scalar=-1.0, in1=r_scale[:, :],
                                            op0=ALU.mult, op1=ALU.mult))
            dve.sem_inc(r_ready, 1)
            dve.wait_ge(loads, 16 * N_LOADS)
            for i in range(2):
                for c in range(KC):
                    own.do(dve.tensor_tensor(tmp[:, :], w_h[:, c, 0:DIM], att[:, i, :], ALU.mult))
                    own.do(dve.tensor_reduce(w_h[:, c, DIM + 4 * i:DIM + 4 * i + 4],
                                             tmp[:, :].rearrange("p (h f) -> p h f", f=F_HEAD), AX.X, ALU.add))
            for c in range(KC):
                own.do(dve.tensor_scalar(w_q[:, c, :], w_q[:, c, :], gpre[:, c:c + 1], None, ALU.mult))
            dve.sem_inc(weights, 1)

            def body(n, s):
                dve.wait_ge(xT_ps, n + 3)
                dve.tensor_copy(xrT[:, s, :], ps_t[:, s, :]).then_inc(xT_ready, 1)
                xt = x_all[:, at(n), :].squeeze(1)
                own.do(dve.scalar_tensor_tensor(out=xt, in0=xr[:, s, :], scalar=un_scale[:, at(n)], in1=xt,
                                                op0=ALU.mult, op1=ALU.add))
                own.do(dve.tensor_tensor(xt, xt, rows[:, 0, :], ALU.add))
                dve.wait_ge(h_ready, n + 3)
                own.do(dve.tensor_copy(sd3[:, at(n), :].squeeze(1), hrow[:, s, DIM:DIM + 8]))
                dve.wait_ge(q_ps, n + 1)
                dve.tensor_copy(qkv[:, at(n), 0:3 * HID].squeeze(1), ps_q[s][:, 0:3 * HID]).then_inc(q_ready, 1)
            repeat(dve, own, 0, TILES, 2, 3, body)
            dve.wait_ge(q_ready, TILES + 2)
            s_, d_ = sd3[:, :, 0:4], sd3[:, :, 4:8]

            def sm(i):
                return small[:, i, :].rearrange("p (t h) -> p t h", h=G_HEADS)
            dve.wait_ge(consts, 3)
            own.do(dve.tensor_tensor(sm(1), s_, bcast(valid[:, :], 2, G_HEADS), ALU.mult))
            own.do(dve.tensor_scalar(s1[:, :], valid[:, :], 1e30, -1e30, ALU.mult, ALU.add))
            own.do(dve.tensor_tensor(sm(1), sm(1), bcast(s1[:, :], 2, G_HEADS), ALU.add))
            own.do(dve.tensor_reduce(small[:, 7, 0:G_HEADS], sm(1).rearrange("p t h -> p h t"), AX.X, ALU.max))
            dve.sem_inc(smax_ready, 1)
            dve.wait_ge(smax_T, 1)
            own.do(dve.tensor_reduce(kcol[0:G_HEADS, 0:1], ps_c[0:G_HEADS, 0:P], AX.X, ALU.max))
            own.do(dve.tensor_scalar(tmp[0:G_HEADS, 128:128 + G_HEADS], ident[0:G_HEADS, 0:G_HEADS],
                                     kcol[0:G_HEADS, 0:1], None, ALU.mult))
            dve.sem_inc(gdiag, 1)
            dve.wait_ge(gmax_ps, 1)
            own.do(dve.tensor_copy(small[:, 7, 0:G_HEADS], ps_c[:, 256:256 + G_HEADS]))
            own.do(dve.tensor_tensor(sm(1), d_, bcast(small[:, 7, 0:G_HEADS], 1, TILES), ALU.add))
            own.do(dve.scalar_tensor_tensor(out=sm(2), in0=sm(1), scalar=SLOPE, in1=sm(1), op0=ALU.mult, op1=ALU.max))
            own.do(dve.tensor_tensor(sm(3), s_, d_, ALU.add))
            own.do(dve.scalar_tensor_tensor(out=sm(4), in0=sm(3), scalar=SLOPE, in1=sm(3), op0=ALU.mult, op1=ALU.max))
            own.do(dve.scalar_tensor_tensor(out=sm(5), in0=sm(4), scalar=GUARD, in1=sm(2), op0=ALU.add, op1=ALU.min))
            own.do(dve.tensor_tensor(sm(0), sm(4), sm(5), ALU.subtract))
            dve.sem_inc(dlog, 1)
            dr = drow[:, :].rearrange("p (t c) -> p t c", c=8)
            own.do(dve.tensor_copy(dr[:, :, 0:4], d_))
            own.do(dve.tensor_copy(dr[:, :, 4:8], sm(5)))
            own.do(dve.memset(tmp[:, 0:8], 0.0))
            dve.sem_inc(drow_ready, 1)
            own.do(dve.memset(mem_v[:, HID:HID + 4], 1.0))
            kk = qkv[:, :, HID:2 * HID]
            own.do(dve.tensor_reduce(kmb[:, :], kk[:, 0:TILES - 1, :].rearrange("p t c -> p c t"), AX.X, ALU.max))
            own.do(dve.tensor_tensor(kmb[0:LAST, :], kmb[0:LAST, :], qkv[0:LAST, TILES - 1, HID:2 * HID], ALU.max))
            own.do(dve.tensor_tensor(kmb[0:N_MEM, :], kmb[0:N_MEM, :], mem_k[:, :], ALU.max))
            dve.sem_inc(kmax_ready, 1)
            dve.wait_ge(kmax_T, 1)
            own.do(dve.tensor_reduce(kcol[:, 0:1], ps_t[:, 0, 0:P], AX.X, ALU.max))
            own.do(dve.tensor_scalar(cmat[:, :], ident[:, :], kcol[:, 0:1], None, ALU.mult))
            dve.sem_inc(kdiag, 1)
            dve.wait_ge(kmax_ps, 1)
            own.do(dve.tensor_copy(kmb[:, :], ps_t[:, 1, 0:HID]))
            own.do(dve.tensor_tensor(mem_k[:, :], mem_k[:, :], kmb[0:N_MEM, :], ALU.subtract))
            own.do(dve.tensor_tensor(kk, kk, bcast(kmb[:, :], 1, TILES), ALU.subtract))
            dve.sem_inc(k_shift, 1)
            qv = qkv[:, :, 0:HID].rearrange("p t (h d) -> p t h d", d=D_HEAD)
            qm = small[:, 1, :].rearrange("p (t h) -> p t h", h=M_HEADS)
            own.do(dve.tensor_reduce(qm, qv, AX.X, ALU.max))
            for h in range(M_HEADS):
                own.step(dve.tensor_tensor(qv[:, :, h, :], qv[:, :, h, :], bcast(qm[:, :, h], 2, D_HEAD), ALU.subtract))
            own.wait()
            dve.sem_inc(q_shift, 1)
            own.do(dve.memset(cmat[:, :], 0.0))
            dve.wait_ge(ctx_ps, 1)
            own.do(dve.reciprocal(kcol[:, 1:2], ps_m[:, HID:HID + 1]))
            for h in range(M_HEADS):
                r = slice(h * D_HEAD, (h + 1) * D_HEAD)
                own.step(dve.tensor_scalar(cmat[r, r], ps_m[r, r], kcol[r, 1:2], None, ALU.mult))
            own.wait()
            dve.sem_inc(c_ready, 1)
            dve.wait_ge(cT_ps, 1)
            own.do(dve.tensor_copy(cT[:, :], ps_t[:, 0, 0:P]))
            dve.sem_inc(cT_ready, 1)
            dve.wait_ge(m_ps, 1)
            own.do(dve.tensor_copy(mmat[:, :], ps_m[:, 0:DIM]))
            dve.sem_inc(m_ready, 1)
            dve.wait_ge(q_exp, 1)
            own.do(dve.tensor_reduce(qm, qv, AX.X, ALU.add))
            q2 = small[:, 2, :].rearrange("p (t h) -> p t h", h=M_HEADS)
            own.do(dve.reciprocal(q2, qm))
            own.do(dve.tensor_scalar(q2, q2, D_HEAD ** -0.5, None, ALU.mult))
            dve.sem_inc(q_norm, 1)

            dve.wait_ge(d_out, 32)
            def mixed(n, s):
                dve.wait_ge(o_ps, n + 1)
                o = qkv[:, at(n), 0:DIM].squeeze(1)
                dve.tensor_tensor(o, ps_h[s][:, 0:DIM], rows[:, 1, :], ALU.add).then_inc(o_ready, 1)
                dve.wait_ge(o_ready, n + 3)
                own.step(dve.bn_stats(st[:, at(n), :].squeeze(1), o))
            repeat(dve, own, 0, TILES, 2, 1, mixed)
            own.wait()
            join_moments(dve, own, st, mv, s1)
            own.do(dve.tensor_tensor(s1[:, :], mv[:, :, 0], mv[:, :, 0], ALU.mult))
            own.do(dve.tensor_tensor(s1[:, :], s1[:, :], mv[:, :, 1], ALU.add))
            own.do(dve.tensor_scalar(s1[:, :], s1[:, :], float(DIM), 1e-24, ALU.mult, ALU.max))
            dve.sem_inc(ss_ready, 1)
            dve.wait_ge(ss_sqrt, 1)
            own.do(dve.reciprocal(s1[:, :], s2[:, :]))
            own.do(dve.tensor_scalar(s1[:, :], s1[:, :], 16.0, None, ALU.mult))

            def normed(n, s):
                o, xt = qkv[:, at(n), 0:DIM].squeeze(1), x_all[:, at(n), :].squeeze(1)
                own.do(dve.scalar_tensor_tensor(out=o, in0=o, scalar=s1[:, at(n)], in1=rows[:, 2, :],
                                                op0=ALU.mult, op1=ALU.mult))
                own.do(dve.tensor_tensor(xt, xt, o, ALU.add))
            repeat(dve, own, 0, TILES, 1, 2, normed)
            dve.sem_inc(b_ready, 1)


def join_moments(dve, own, st, mv, tmp):
    own.do(dve.tensor_tensor(mv[:, :, 0], st[:, :, 1], st[:, :, 4], ALU.add))
    own.do(dve.tensor_scalar(mv[:, :, 0], mv[:, :, 0], 0.5, None, ALU.mult))
    own.do(dve.tensor_tensor(tmp[:, :], st[:, :, 1], st[:, :, 4], ALU.subtract))
    own.do(dve.scalar_tensor_tensor(out=tmp[:, :], in0=tmp[:, :], scalar=0.25, in1=tmp[:, :], op0=ALU.mult, op1=ALU.mult))
    own.do(dve.tensor_tensor(mv[:, :, 1], st[:, :, 2], st[:, :, 5], ALU.add))
    own.do(dve.scalar_tensor_tensor(out=mv[:, :, 1], in0=mv[:, :, 1], scalar=1.0 / DIM, in1=tmp[:, :],
                                    op0=ALU.mult, op1=ALU.add))


def for_sp(sp, total, body):
    with sp.Fori(0, total // 2) as it:
        for u in range(2):
            body(it * 2 + u, u)
    for n in range(total // 2 * 2, total):
        body(n, n % 2)


def for_act(act, total, first, second, table_out):
    first(0, 0)
    first(1, 1)
    second(0, 0)
    second(1, 1)
    with act.Fori(1, total // 2) as it:
        for u in range(2):
            first(it * 2 + u, u)
        for u in range(2):
            act.wait_ge(table_out[u], it * 16)
            second(it * 2 + u, u)
    n = total - 1
    first(n, 0)
    act.wait_ge(table_out[0], n // 2 * 16)
    second(n, 0)


def edge_stage(nc, g):
    acc, region, ident, ones, spans = (g[k] for k in ("acc", "region", "ident", "ones", "spans"))
    table, dst_table = g["table"], g["dst_table"]
    acc4 = acc[:, :].rearrange("p (w c) -> p w c", c=4)
    SL = 3

    used = [0]

    def carve(*shape, dt=F32):
        size = 1
        for s in shape:
            size *= s
        v = region[:, used[0]:used[0] + size]
        used[0] += size
        if dt != F32:
            v = v.bitcast(dt)
        return v

    src_idx = carve((BLOCKS + 2) * SUB, dt=I32)
    idx = carve(SL * SUB, dt=I32)
    dst_raw = carve((BLOCKS + 1) * SUB, dt=I32)
    rel = carve((BLOCKS + 1) * SUB)
    rows = carve(SL * SUB * ROW).rearrange("p (s j c) -> p s j c", s=SL, j=SUB)
    mask = carve(SL * SUB * WIN).rearrange("p (s j w) -> p s j w", s=SL, j=SUB)
    maskT = carve(SL * P).rearrange("p (s e) -> p s e", s=SL)
    dwin = carve(SL * 8).rearrange("p (s c) -> p s c", s=SL)
    dblk = carve(SL * SUB * 8).rearrange("p (s j c) -> p s j c", s=SL, j=SUB)
    wts = carve(SL * SUB * P).rearrange("p (s j c) -> p s j c", s=SL, j=SUB)
    wsum = carve(SL * P).rearrange("p (s c) -> p s c", s=SL)
    lg = carve(SL * SUB * G_HEADS).rearrange("p (s j h) -> p s j h", s=SL, j=SUB)
    ex = carve(SL * SUB * G_HEADS).rearrange("p (s j h) -> p s j h", s=SL, j=SUB)
    z = carve(SUB * G_HEADS).rearrange("p (j h) -> p j h", j=SUB)
    lr = carve(SUB * G_HEADS).rearrange("p (j h) -> p j h", j=SUB)
    win_i = carve(WIN, dt=I32)
    win = carve(WIN)
    bm = carve(SUB * 8).rearrange("p (j c) -> p j c", j=SUB)
    bases = carve(BLOCKS + 1, dt=I32)
    bases_f = carve(BLOCKS)
    bad = carve((BLOCKS + 1) * SUB)
    badc = carve((BLOCKS + 1) * SUB)
    badn = carve(2)
    zeros = carve(DIM)
    g["edge_buffers"].update(locals())

    with ExitStack() as ctx:
        def sem(name):
            return ctx.enter_context(nc.semaphore(name))
        ps_p = [ctx.enter_context(nc.psum_tensor(f"ps_p{i}", [P, 512], F32)) for i in range(SL)]
        ps_s = [ctx.enter_context(nc.psum_tensor(f"ps_s{i}", [P, 512], F32)) for i in range(SL)]
        ps_b = ctx.enter_context(nc.psum_tensor("ps_b", [P, 512], F32))

        src_in, dst_in, own_v, own_p = sem("src_in"), sem("dst_in"), sem("own_v2"), sem("own_p2")
        pool_consts, bases_f_ready, bases_ps, span_ready, span_ps, spans_ready = (sem(n) for n in (
            "pool_consts", "bases_f_ready", "bases_ps", "span_ready", "span_ps", "spans_ready"))
        gathered = [sem(f"gathered{i}") for i in range(SL)]
        dwin_in = [sem(f"dwin_in{i}") for i in range(SL)]
        zeros_ready, cleared = sem("zeros_ready"), sem("cleared")
        idx_ready, slots_open = sem("idx_ready"), sem("slots_open")
        (zeroed_a, mask_ready, maskT_ps, maskT_ready, dlog_ps, logits_ready, ex_ready, w_ready, wsum_ready,
         block_ps, block_done) = (sem(n) for n in (
             "zeroed_a", "mask_ready", "maskT_ps", "maskT_ready", "dlog_ps", "logits_ready", "ex_ready",
             "w_ready", "wsum_ready", "block_ps", "block_done"))
        block = ctx.enter_context(nc.Block())

        @block.sync
        def _(sp):
            sp.dma_start(src_idx[:, 0:BLOCKS * SUB], g["src"]).then_inc(src_in, 16)
            sp.dma_start(dst_raw[:, 0:BLOCKS * SUB], g["dst"]).then_inc(dst_in, 16)
            sp.wait_ge(zeros_ready, 1)
            sp.dma_start(g["expert_in"][:, :].rearrange("(t p) d -> p t d", p=P), bcast(zeros, 1, MOE_TILES)).then_inc(cleared, 16)
            sp.dma_start(bases[0:1, 0:BLOCKS], g["dst"][0:1, :].rearrange("p (b j) -> p b j", j=SUB)[:, :, 0],
                         allow_slow_non_contiguous=True).then_inc(dst_in, 16)
            sp.wait_ge(dst_in, 32)
            sp.wait_ge(pool_consts, 2)

            def body(n, s):
                base = sp.value_load(bases[0:1, at(n)], min_val=0, max_val=N_PAD)
                sp.wait_ge(mask_ready, n + 1)
                sp.dma_start(dwin[:, s, :], bcast(dst_table[bass.ds(base, WIN), :], 0, SUB)).then_inc(dwin_in[s], 16)
            repeat(sp, Own(sp, own_v), 0, BLOCKS + 1, SL, 0, body)
            for s in range(SL):
                sp.wait_ge(dwin_in[s], 16 * len(range(s, BLOCKS + 1, SL)))
            sp.wait_ge(cleared, 16)

        @block.gpsimd
        def _(pool):
            pool.memset(zeros, 0.0).then_inc(zeros_ready, 1)
            pool.memset(bases[0:1, BLOCKS:BLOCKS + 1], 0).then_inc(pool_consts, 1)
            pool.memset(src_idx[:, BLOCKS * SUB:], 0).then_inc(pool_consts, 1)
            pool.iota(win_i, [[1, WIN]], base=0, channel_multiplier=0).then_inc(pool_consts, 1)
            pool.memset(bm, 1.0).then_inc(own_p, 1)
            pool.wait_ge(own_p, 1)
            pool.affine_select(out=bm, in_=bm, compare_op=ALU.is_ge, fill=0.0, base=0,
                               pattern=[[-WIN, SUB], [0, 8]], channel_multiplier=1).then_inc(own_p, 1)
            pool.wait_ge(own_p, 2)
            pool.affine_select(out=bm, in_=bm, compare_op=ALU.is_ge, fill=0.0, base=WIN - 1,
                               pattern=[[WIN, SUB], [0, 8]], channel_multiplier=-1).then_inc(pool_consts, 1)
            def body(n, s):
                pool.wait_ge(block_done, n + 1)
                pool.wait_ge(idx_ready, n + 1)
                pool.sem_inc(slots_open, 1)
                for j in range(SUB):
                    pool.indirect_dma_start(
                        out=rows[:, s, j, :], out_offset=None, in_=table[:, :],
                        in_offset=bass.IndirectOffsetOnAxis(ap=idx[:, s * SUB + j:s * SUB + j + 1], axis=0),
                    ).then_inc(gathered[s], 16)
            repeat(pool, Own(pool, own_p), 0, BLOCKS, SL, 0, body)
            for s in range(SL):
                pool.wait_ge(gathered[s], 64 * len(range(s, BLOCKS, SL)))

        @block.scalar
        def _(act):
            act.wait_ge(src_in, 16)
            act.wait_ge(pool_consts, 2)

            def indices(n, s):
                act.activation(idx[:, s * SUB:(s + 1) * SUB], src_idx[:, at(n, SUB)], ACT.Copy).then_inc(idx_ready, 1)
            indices(0, 0)
            indices(1, 1)
            half = ACC_W * 2
            act.memzero(acc[:, half:]).then_inc(zeroed_a, 1)

            def mask_copy(n, s):
                act.wait_ge(maskT_ps, n + 1)
                act.activation(maskT[:, s, :], ps_s[s][:, 0:P], ACT.Copy).then_inc(maskT_ready, 1)

            def body(n, s):
                indices(n + 2, (s + 2) % SL)
                act.wait_ge(logits_ready, n + 1)
                act.activation(ex[:, s], lg[:, s], ACT.Exp).then_inc(ex_ready, 1)
                mask_copy(n + 1, (s + 1) % SL)
            mask_copy(0, 0)
            body(0, 0)
            repeat(act, Own(act, own_v), 1, BLOCKS, SL, 0, body)

        @block.tensor
        def _(pe):
            pe.wait_ge(bases_f_ready, 1)
            pe.matmul(ps_b[:, 0:BLOCKS], ones[0:1, :], bases_f[0:1, :], start=True, stop=True).then_inc(bases_ps, 1)

            def prepare(n, s):
                pe.wait_ge(mask_ready, n + 4)
                pe.transpose(ps_s[s][:, 0:P], mask[:, s].rearrange("p j w -> p (j w)"), ident[:, :]).then_inc(maskT_ps, 1)
                pe.wait_ge(maskT_ready, n + 1)
                pe.matmul(ps_s[s][:, P:P + SUB * 8], maskT[:, s, :], dblk[:, s].rearrange("p j c -> p (j c)"),
                          start=True, stop=True).then_inc(dlog_ps, 1)

            def body(n, s):
                prepare(n + 1, (s + 1) % SL)
                pe.wait_ge(w_ready, n + 1)
                pe.wait_ge(block_done, n + 1)
                for y in range(2):
                    for j in range(SUB):
                        pe.matmul(ps_p[s][:, y * P:(y + 1) * P], rows[:, s, j, y * P:(y + 1) * P], wts[:, s, j, :],
                                  start=j == 0, stop=j == SUB - 1)
                pe.wait_ge(wsum_ready, n + 1)
                pe.matmul(strided(ps_p[s], 2 * P, 192), ones[:, :], wsum[:, s].rearrange("p (a b) -> p a b", a=2),
                          start=True, stop=True).then_inc(block_ps, 1)
            prepare(0, 0)
            body(0, 0)
            repeat(pe, Own(pe, own_v), 1, BLOCKS, SL, 0, body)
            pe.wait_ge(span_ready, 1)
            pe.matmul(ps_b[0:1, 0:1], badn[:, 0:1], ones[:, 0:1], start=True, stop=True).then_inc(span_ps, 1)

        @block.vector
        def _(dve):
            own = Own(dve, own_v)
            dve.sem_inc(block_done, SL)
            dve.sem_inc(mask_ready, SL)
            dve.wait_ge(dst_in, 32)
            own.do(dve.tensor_copy(bases_f[0:1, :], bases[0:1, 0:BLOCKS]))
            dve.sem_inc(bases_f_ready, 1)
            dve.wait_ge(pool_consts, 4)
            own.do(dve.tensor_copy(win, win_i))
            own.do(dve.memset(rel[:, BLOCKS * SUB:], -1.0))
            own.do(dve.tensor_copy(rel[:, 0:BLOCKS * SUB], dst_raw[:, 0:BLOCKS * SUB]))
            r0 = rel[:, 0:BLOCKS * SUB]
            own.do(dve.tensor_scalar(badc[:, 0:BLOCKS * SUB], r0, float(N_NODES), None, ALU.is_lt))
            dve.wait_ge(bases_ps, 1)
            r3 = r0.rearrange("p (b j) -> p b j", j=SUB)
            own.do(dve.tensor_tensor(r3, r3, bcast(ps_b[:, 0:BLOCKS], 2, SUB), ALU.subtract))
            b0, c0 = bad[:, 0:BLOCKS * SUB], badc[:, 0:BLOCKS * SUB]
            own.do(dve.scalar_tensor_tensor(out=b0, in0=r0, scalar=float(WIN), in1=c0, op0=ALU.is_ge, op1=ALU.mult))
            own.do(dve.scalar_tensor_tensor(out=c0, in0=r0, scalar=0.0, in1=c0, op0=ALU.is_lt, op1=ALU.mult))
            own.do(dve.tensor_tensor_reduce(b0, b0, c0, 1.0, 0.0, ALU.add, ALU.add, badn[:, 0:1]))
            own.do(dve.memset(acc[:, 0:ACC_W * 2], 0.0))
            dve.wait_ge(zeroed_a, 1)

            def prepare(n, s):
                own.do(dve.tensor_tensor(mask[:, s], bcast(rel[:, bass.ds(n * SUB, SUB)], 2, WIN), bcast(win, 1, SUB),
                                         ALU.is_equal))
                dve.wait_ge(dwin_in[s], slot_count(n, s, 16))
                dve.tensor_tensor(dblk[:, s], bm, bcast(dwin[:, s, :], 1, SUB), ALU.mult).then_inc(mask_ready, 1)

            def logits(n, s):
                dve.wait_ge(gathered[s], slot_count(n, s, 64))
                dve.wait_ge(dlog_ps, n + 1)
                d8 = ps_s[s][:, P:P + SUB * 8].rearrange("p (j c) -> p j c", c=8)
                own.do(dve.tensor_tensor(z, rows[:, s, :, DIM:ROW], d8[:, :, 0:4], ALU.add))
                own.do(dve.scalar_tensor_tensor(out=lr, in0=z, scalar=SLOPE, in1=z, op0=ALU.mult, op1=ALU.max))
                dve.tensor_tensor(lg[:, s], lr, d8[:, :, 4:8], ALU.subtract).then_inc(logits_ready, 1)

            def weigh(n, s):
                dve.wait_ge(ex_ready, n + 1)
                for j in range(SUB):
                    m = dve.tensor_tensor(wts[:, s, j, :].rearrange("p (h w) -> p h w", h=G_HEADS),
                                          bcast(mask[:, s, j, :], 1, G_HEADS), bcast(ex[:, s, j, :], 2, WIN), ALU.mult)
                    if j < SUB - 1:
                        own.step(m)
                m.then_inc(w_ready, 1)

            def sum_weights(n, s):
                dve.wait_ge(w_ready, n + 1)
                dve.tensor_reduce(wsum[:, s, :], wts[:, s].rearrange("p j c -> p c j"), AX.X, ALU.add).then_inc(wsum_ready, 1)

            def accumulate(n, s):
                dve.wait_ge(block_ps, n + 1)
                base = dve.value_load(bases[0:1, at(n)], min_val=0, max_val=N_PAD)
                for half in range(2):
                    r = slice(64 * half, 64 * half + 64)
                    a = acc4[r, bass.ds(base, WIN), :].rearrange("p w c -> p c w")
                    m = dve.tensor_tensor(a, a, quads(ps_p[s], half), ALU.add)
                    if half == 0:
                        own.step(m)
                m.then_inc(block_done, 1)

            def body(n, s):
                logits(n, s)
                prepare(n + 1, (s + 1) % SL)
                weigh(n, s)
                dve.wait_ge(block_done, n - 1 + SL)
                accumulate(n - 1, (s + 2) % SL)
                sum_weights(n, s)
            prepare(0, 0)
            logits(0, 0)
            prepare(1, 1)
            weigh(0, 0)
            sum_weights(0, 0)
            repeat(dve, own, 1, BLOCKS, SL, 2 + 1 + 3 + 1, body)
            dve.wait_ge(block_done, BLOCKS - 1 + SL)
            accumulate(BLOCKS - 1, (BLOCKS - 1) % SL)
            dve.sem_inc(span_ready, 1)
            dve.wait_ge(span_ps, 1)
            own.do(dve.tensor_copy(spans[0:1, 0:1], ps_b[0:1, 0:1]))


def any_order_stage(nc, g):
    e = g["edge_buffers"]
    acc, ident, ones, spans = (g[k] for k in ("acc", "ident", "ones", "spans"))
    table, dst_table = g["table"], g["dst_table"]
    src_idx, idx, dst_raw, rel, rows, mask, maskT, dwin, dblk, wts, wsum, lg, ex, z, lr, win, bm = (e[k] for k in (
        "src_idx", "idx", "dst_raw", "rel", "rows", "mask", "maskT", "dwin", "dblk", "wts", "wsum", "lg", "ex",
        "z", "lr", "win", "bm"))
    acc4 = acc[:, :].rearrange("p (w c) -> p w c", c=4)

    with ExitStack() as ctx:
        ps_p = ctx.enter_context(nc.psum_tensor("ps_ap", [P, 512], F32))
        ps_s = ctx.enter_context(nc.psum_tensor("ps_as", [P, 512], F32))
        (own_v, zeroed, indexed, slots_open, gathered, windowed, masked, mask_ps, mask_back, dlog_ps, lg_ready,
         ex_ready, w_ready, sum_ps, summed, shifted) = (ctx.enter_context(nc.semaphore("any_" + n)) for n in (
             "own_v", "zeroed", "indexed", "slots_open", "gathered", "windowed", "masked", "mask_ps", "mask_back",
             "dlog_ps", "lg_ready", "ex_ready", "w_ready", "sum_ps", "summed", "shifted"))
        block = ctx.enter_context(nc.Block())

        def steps(eng, body):
            outside = eng.value_load(spans[0:1, 0:1], min_val=0, max_val=N_EDGES)
            with eng.If(outside > 0):
                if eng is nc.vector or eng is nc.scalar:
                    body(None, None, None)
                with eng.Fori(0, WINDOWS) as v:
                    if eng is nc.vector:
                        body(None, v, None)
                    with eng.Fori(0, BLOCKS) as n:
                        body(v * BLOCKS + n, v, n)

        @block.sync
        def _(sp):
            def body(m, v, n):
                sp.wait_ge(summed, m + 1)
                sp.dma_start(dwin[:, 0, :], bcast(dst_table[at(v, WIN), :], 0, SUB)).then_inc(windowed, 16)
            steps(sp, body)

        @block.gpsimd
        def _(pool):
            def body(m, v, n):
                pool.wait_ge(indexed, m + 1)
                pool.sem_inc(slots_open, 1)
                for j in range(SUB):
                    pool.indirect_dma_start(
                        out=rows[:, 0, j, :], out_offset=None, in_=table[:, :],
                        in_offset=bass.IndirectOffsetOnAxis(ap=idx[:, j:j + 1], axis=0)).then_inc(gathered, 16)
            steps(pool, body)

        @block.scalar
        def _(act):
            def body(m, v, n):
                if m is None:
                    act.memzero(acc[:, ACC_W * 2:]).then_inc(zeroed, 1)
                    return
                act.wait_ge(summed, m + 1)
                act.activation(idx[:, 0:SUB], src_idx[:, at(n, SUB)], ACT.Copy).then_inc(indexed, 1)
                act.wait_ge(mask_ps, m + 1)
                act.activation(maskT[:, 0, :], ps_s[:, 0:P], ACT.Copy).then_inc(mask_back, 1)
                act.wait_ge(lg_ready, m + 1)
                act.activation(ex[:, 0], lg[:, 0], ACT.Exp).then_inc(ex_ready, 1)
            steps(act, body)

        @block.tensor
        def _(pe):
            def body(m, v, n):
                pe.wait_ge(masked, m + 1)
                pe.transpose(ps_s[:, 0:P], mask[:, 0].rearrange("p j w -> p (j w)"), ident[:, :]).then_inc(mask_ps, 1)
                pe.wait_ge(mask_back, m + 1)
                pe.matmul(ps_s[:, P:P + SUB * 8], maskT[:, 0, :], dblk[:, 0].rearrange("p j c -> p (j c)"),
                          start=True, stop=True).then_inc(dlog_ps, 1)
                pe.wait_ge(w_ready, m + 1)
                for y in range(2):
                    for j in range(SUB):
                        pe.matmul(ps_p[:, y * P:(y + 1) * P], rows[:, 0, j, y * P:(y + 1) * P], wts[:, 0, j, :],
                                  start=j == 0, stop=j == SUB - 1)
                pe.matmul(strided(ps_p, 2 * P, 192), ones[:, :], wsum[:, 0].rearrange("p (a b) -> p a b", a=2),
                          start=True, stop=True).then_inc(sum_ps, 1)
            steps(pe, body)

        @block.vector
        def _(dve):
            own = Own(dve, own_v)
            OWN = 1 + 2 + SUB + 1

            def body(m, v, n):
                if v is None:
                    dve.sem_inc(summed, 1)
                    own.do(dve.tensor_scalar(win, win, float(-WIN), None, ALU.add))
                    own.do(dve.tensor_copy(rel[:, 0:BLOCKS * SUB], dst_raw[:, 0:BLOCKS * SUB]))
                    own.do(dve.memset(acc[:, 0:ACC_W * 2], 0.0))
                    dve.wait_ge(zeroed, 1)
                    own.start = own.k
                    return
                if n is None:
                    own.base, own.k = own.start + v * (BLOCKS * OWN + 1), 0
                    own.do(dve.tensor_scalar(win, win, float(WIN), None, ALU.add))
                    own.inner = own.base + 1
                    dve.sem_inc(shifted, 1)
                    return
                own.base, own.k = own.inner + n * OWN, 0
                own.do(dve.tensor_tensor(mask[:, 0], bcast(rel[:, bass.ds(n * SUB, SUB)], 2, WIN), bcast(win, 1, SUB),
                                         ALU.is_equal))
                dve.wait_ge(windowed, m * 16 + 16)
                dve.tensor_tensor(dblk[:, 0], bm, bcast(dwin[:, 0, :], 1, SUB), ALU.mult).then_inc(masked, 1)
                dve.wait_ge(gathered, m * 64 + 64)
                dve.wait_ge(dlog_ps, m + 1)
                d8 = ps_s[:, P:P + SUB * 8].rearrange("p (j c) -> p j c", c=8)
                own.do(dve.tensor_tensor(z, rows[:, 0, :, DIM:ROW], d8[:, :, 0:4], ALU.add))
                own.do(dve.scalar_tensor_tensor(out=lr, in0=z, scalar=SLOPE, in1=z, op0=ALU.mult, op1=ALU.max))
                dve.tensor_tensor(lg[:, 0], lr, d8[:, :, 4:8], ALU.subtract).then_inc(lg_ready, 1)
                dve.wait_ge(ex_ready, m + 1)
                for j in range(SUB):
                    own.step(dve.tensor_tensor(wts[:, 0, j, :].rearrange("p (h w) -> p h w", h=G_HEADS),
                                               bcast(mask[:, 0, j, :], 1, G_HEADS), bcast(ex[:, 0, j, :], 2, WIN), ALU.mult))
                own.wait()
                dve.tensor_reduce(wsum[:, 0, :], wts[:, 0].rearrange("p j c -> p c j"), AX.X, ALU.add).then_inc(w_ready, 1)
                dve.wait_ge(sum_ps, m + 1)
                for half in range(2):
                    a = acc4[64 * half:64 * half + 64, at(v, WIN), :].rearrange("p w c -> p c w")
                    ins = dve.tensor_tensor(a, a, quads(ps_p, half), ALU.add)
                    if half == 0:
                        own.step(ins)
                ins.then_inc(summed, 1)
                assert own.k == OWN, own.k
            steps(dve, body)


def slot_count(n, s, inc, slots=3):
    return (n - s + slots) * inc // slots


def strided(ps, start, step):
    v = ps[:, start:start + 64]
    return bass.AP(v.tensor, v.offset, [list(v.ap[0]), [step, 2], [1, 64]])


def quads(ps, half):
    v = ps[64 * half:64 * half + 64, 32 * half:32 * half + 32]
    return bass.AP(v.tensor, v.offset, [list(v.ap[0]), [256, 2], [192, 2], [1, 32]])


def rows_stage(nc, g):
    acc, ident, valid, w_self, region = (g[k] for k in ("acc", "ident", "valid", "w_self", "region"))
    table, base_rows = g["table"], g["base_rows"]
    acc4 = acc[:, :].rearrange("p (w c) -> p w c", c=4)
    w1_sb, w2_sb, b2_sb, logits, wr = (g[k] for k in ("w1_sb", "w2_sb", "b2_sb", "logits", "wr"))

    with ExitStack() as ctx:
        def sb(name, shape, dt=F32):
            return ctx.enter_context(nc.sbuf_tensor(name, shape, dt))

        def sem(name):
            return ctx.enter_context(nc.semaphore(name))

        planes = sb("planes", [P, 2, 4, P])
        h_in = sb("h_in", [P, 2, DIM])
        b_in = sb("b_in", [P, 2, DIM])
        rl = sb("rl", [P, 2, G_HEADS])
        tmp = sb("tmpr", [P, DIM])
        tmpx = sb("tmpx", [P, 2, DIM])
        lnrows = sb("lnrows", [P, 2, DIM])
        brow = sb("brow", [P, EXPERTS])
        st = sb("st2", [P, TILES, 6])
        mv = sb("mv2", [P, TILES, 2])
        s1, s2, s3 = sb("r1", [P, TILES]), sb("r2", [P, TILES]), sb("r3", [P, TILES])
        eps = sb("eps2", [P, 1])
        xT = sb("xT", [P, 2, DIM])
        ps_t = [ctx.enter_context(nc.psum_tensor(f"ps_r{i}", [P, 512], F32)) for i in range(2)]
        ps_x = ctx.enter_context(nc.psum_tensor("ps_rx", [P, 2, DIM], F32))
        ps_l = [ctx.enter_context(nc.psum_tensor(f"ps_rl{i}", [P, 512], F32)) for i in range(2)]

        loads, own_v, own_a = sem("loads2"), sem("own_v4"), sem("own_a4")
        weights_in = g["weights_in"]
        row_in = [sem(f"row_in{i}") for i in range(2)]
        planes_ready, planes_ps, x1_ready, var_ready, dev_ready, scale_ready = (sem(n) for n in (
            "planes_ready", "planes_ps", "x1_ready", "var_ready", "dev_ready", "scale_ready"))
        n_ready, f_ready, f_ps, fT_ready, l_ps, l_ready = (sem(n) for n in (
            "n_ready", "f_ready", "f_ps", "fT_ready", "l_ps", "l_ready"))
        block = ctx.enter_context(nc.Block())

        def x1_of(n):
            return acc[:, bass.ds(n * 4 * P + DIM, DIM)]

        def xn_of(n):
            return acc[:, bass.ds(n * 4 * P, DIM)]

        @block.sync
        def _(sp):
            def body(n, s):
                sp.wait_ge(x1_ready, n + 1)
                sp.dma_start(h_in[:, s, :], table[at(n, P), 0:DIM]).then_inc(row_in[s], 16)
                sp.dma_start(b_in[:, s, :], base_rows[at(n, P), :]).then_inc(row_in[s], 16)
            for_sp(sp, TILES, body)

        @block.gpsimd
        def _(pool):
            def body(n, s):
                pool.wait_ge(planes_ps, n + 1)
                pool.tensor_copy(planes[:, s], acc4[:, at(n, P), :].rearrange("p w c -> p c w")).then_inc(planes_ready, 1)
            repeat(pool, Own(pool, own_v), 0, TILES, 2, 0, body)

        @block.scalar
        def _(act):
            act.dma_start(lnrows[:, 0, :], g["gamma"].partition_broadcast(P)).then_inc(loads, 16)
            act.dma_start(lnrows[:, 1, :], g["beta"].partition_broadcast(P)).then_inc(loads, 16)
            act.dma_start(brow[:, :], g["br"].partition_broadcast(P)).then_inc(loads, 16)
            act.dma_start(wr[:, :].rearrange("p (c e) -> p c e", e=EXPERTS),
                          g["Wr"].rearrange("(c p) e -> p c e", p=P)).then_inc(loads, 16)
            act.dma_start(b2_sb, g["b2"].rearrange("e f -> (e f)").partition_broadcast(P)).then_inc(weights_in, 16)
            for e in range(EXPERTS):
                act.dma_start(w1_sb[:, e], g["W1"][e].rearrange("(c p) f -> p c f", p=P)).then_inc(weights_in, 16)
                act.dma_start(w2_sb[:, e], g["W2"][e].rearrange("(c p) d -> p c d", p=P)).then_inc(weights_in, 16)
            for i in range(2):
                act.wait_ge(var_ready, i + 1)
                act.activation(s2[:, :], s1[:, :], ACT.Sqrt, bias=eps[:, 0:1]).then_inc(dev_ready, 1)
            act.wait_ge(scale_ready, 1)

            def body(n, s):
                act.activation(xn_of(n), x1_of(n), ACT.Identity, bias=s2[:, at(n)], scale=s1[:, at(n)]).then_inc(n_ready, 1)

            def copy(n, s):
                act.wait_ge(f_ps, n + 1)
                act.activation(xT[:, s, :], ps_x[:, s, :], ACT.Copy).then_inc(fT_ready, 1)
            body(0, 0)

            def both(n, s):
                body(n, s)
                copy(n - 1, 1 - s)
            repeat(act, Own(act, own_a), 1, TILES, 2, 0, both)
            copy(TILES - 1, 0)

        @block.tensor
        def _(pe):
            pe.sem_inc(planes_ps, 2)

            def body(n, s):
                pe.wait_ge(planes_ready, n + 1)
                pe.wait_ge(x1_ready, n + 1)
                for c in range(4):
                    m = pe.transpose(ps_t[s][:, c * P:(c + 1) * P], planes[:, s, c, :], ident[:, :])
                m.then_inc(planes_ps, 1)
            repeat(pe, Own(pe, own_v), 0, TILES, 2, 0, body)
            pe.wait_ge(loads, 64)

            def route(n, s):
                pe.wait_ge(f_ready, n + 1)
                for c in range(KC):
                    m = pe.transpose(ps_x[:, s, c * P:(c + 1) * P], tmpx[:, s, c * P:(c + 1) * P], ident[:, :])
                m.then_inc(f_ps, 1)
                pe.wait_ge(fT_ready, n + 1)
                pe.wait_ge(l_ready, n + 1)
                for c in range(KC):
                    m = pe.matmul(ps_l[s][:, 0:EXPERTS], xT[:, s, c * P:(c + 1) * P], wr[:, c * EXPERTS:(c + 1) * EXPERTS],
                                  start=c == 0, stop=c == KC - 1)
                m.then_inc(l_ps, 1)
            repeat(pe, Own(pe, own_v), 0, TILES, 2, 0, route)

        @block.vector
        def _(dve):
            own = Own(dve, own_v)
            dve.sem_inc(x1_ready, 2)
            dve.sem_inc(l_ready, 2)
            own.do(dve.memset(eps[:, :], LN_EPS))

            def heads(ap):
                return ap.rearrange("p (h f) -> p h f", f=F_HEAD)

            def body(n, s):
                dve.wait_ge(planes_ps, n + 3)
                ws = w_self[:, at(n, G_HEADS)]
                l4 = heads(ps_t[s][:, DIM:2 * DIM])[:, :, 0]
                own.do(dve.tensor_tensor(rl[:, s, :], l4, ws, ALU.add))
                own.do(dve.reciprocal(rl[:, s, :], rl[:, s, :]))
                dve.wait_ge(row_in[s], slot_count(n, s, 32, 2))
                own.do(dve.tensor_tensor(heads(h_in[:, s, :]), heads(h_in[:, s, :]), bcast(ws, 2, F_HEAD), ALU.mult))
                own.do(dve.tensor_tensor(tmp[:, :], h_in[:, s, :], ps_t[s][:, 0:DIM], ALU.add))
                own.do(dve.tensor_tensor(heads(tmp[:, :]), heads(tmp[:, :]), bcast(rl[:, s, :], 2, F_HEAD), ALU.mult))
                own.do(dve.tensor_tensor(x1_of(n), tmp[:, :], b_in[:, s, :], ALU.add))
                dve.bn_stats(st[:, at(n), :].squeeze(1), x1_of(n)).then_inc(x1_ready, 1)
            repeat(dve, own, 0, TILES, 2, 6, body)
            dve.wait_ge(x1_ready, TILES + 2)
            join_moments(dve, own, st, mv, s1)
            own.do(dve.tensor_copy(s1[:, :], mv[:, :, 1]))
            dve.sem_inc(var_ready, 1)
            dve.wait_ge(dev_ready, 1)
            own.do(dve.reciprocal(s3[:, :], s2[:, :]))
            own.do(dve.tensor_tensor(s1[:, :], s1[:, :], s3[:, :], ALU.mult))
            own.do(dve.tensor_tensor(s1[:, :], s1[:, :], s3[:, :], ALU.mult))
            dve.sem_inc(var_ready, 1)
            dve.wait_ge(dev_ready, 2)
            own.do(dve.reciprocal(s2[:, :], s2[:, :]))
            own.do(dve.tensor_tensor(s1[:, :], s2[:, :], s3[:, :], ALU.mult))
            own.do(dve.scalar_tensor_tensor(out=s2[:, :], in0=mv[:, :, 0], scalar=-1.0, in1=s1[:, :],
                                            op0=ALU.mult, op1=ALU.mult))
            dve.sem_inc(scale_ready, 1)
            dve.wait_ge(loads, 64)

            def route(n, s):
                dve.wait_ge(n_ready, n + 1)
                own.do(dve.tensor_tensor(tmp[:, :], xn_of(n), lnrows[:, 0, :], ALU.mult))
                own.do(dve.tensor_tensor(tmpx[:, s, :], tmp[:, :], lnrows[:, 1, :], ALU.add))
                dve.tensor_tensor(xn_of(n), tmp[:, :], lnrows[:, 1, :], ALU.add).then_inc(f_ready, 1)
                dve.wait_ge(f_ready, n + 1)

            def take(n, s):
                dve.wait_ge(l_ps, n + 1)
                dve.tensor_tensor(logits[:, at(n, EXPERTS)], ps_l[s][:, 0:EXPERTS], brow[:, :], ALU.add).then_inc(l_ready, 1)
            route(0, 0)

            def both(n, s):
                route(n, s)
                take(n - 1, 1 - s)
            repeat(dve, own, 1, TILES, 2, 2, both)
            take(TILES - 1, 0)


def route_stage(nc, g):
    acc, ident, ones, valid, logits = (g[k] for k in ("acc", "ident", "ones", "valid", "logits"))
    place, gate, tile_expert, expert_in = g["place"], g["gate"], g["tile_expert"], g["expert_in"]
    TE = TILES * EXPERTS

    with ExitStack() as ctx:
        def sb(name, shape, dt=F32):
            return ctx.enter_context(nc.sbuf_tensor(name, shape, dt))

        def sem(name):
            return ctx.enter_context(nc.semaphore(name))

        def te(name):
            return sb(name, [P, TE])[:, :].rearrange("p (t e) -> p t e", e=EXPERTS)

        before = sb("before", [P, P])
        rank_i, rank = sb("rank_i", [P, EXPERTS], I32), sb("rank", [P, EXPERTS])
        tau_i, tau = sb("tau_i", [1, MOE_TILES], I32), sb("tau", [1, MOE_TILES])
        le = sb("le", [1, MOE_TILES * EXPERTS])
        tmpf = sb("tmpf", [P, TE])
        work = tmpf[:, :].rearrange("p (t e) -> p t e", e=EXPERTS)
        first, second, both = te("first"), te("second"), te("both_")
        pos = te("pos")
        top = sb("top", [P, 2, TILES])
        t1 = sb("t1", [P, TILES])
        cnt = sb("cnt", [P, 4, EXPERTS])
        cnt_i = sb("cnt_i", [P, EXPERTS], I32)
        ps_pos = ctx.enter_context(nc.psum_tensor("ps_pos", [P, 512], F32))
        ps_tot = ctx.enter_context(nc.psum_tensor("ps_tot", [P, 512], F32))
        own_v, own_p, consts, picked, counted, exp_in, exp_out, placed = (sem(n) for n in (
            "own_v5", "own_p5", "consts5", "picked", "counted", "exp_in5", "exp_out5", "placed"))
        sent = sem("sent")
        block = ctx.enter_context(nc.Block())

        @block.gpsimd
        def _(pool):
            pool.memset(before[:, :], 1.0).then_inc(own_p, 1)
            pool.iota(rank_i[:, :], [[-1, EXPERTS]], base=EXPERTS, channel_multiplier=0).then_inc(consts, 1)
            pool.iota(tau_i[:, :], [[1, MOE_TILES]], base=0, channel_multiplier=0).then_inc(consts, 1)
            pool.wait_ge(own_p, 1)
            pool.affine_select(out=before[:, :], in_=before[:, :], compare_op=ALU.is_gt, fill=0.0, base=0,
                               pattern=[[1, P]], channel_multiplier=-1).then_inc(consts, 1)
            pool.wait_ge(placed, 1)
            for n in range(TILES):
                r = P if n < TILES - 1 else LAST
                for k in range(2):
                    pool.indirect_dma_start(
                        out=expert_in[:, :], out_offset=bass.IndirectOffsetOnAxis(ap=place[0:r, k * TILES + n:k * TILES + n + 1], axis=0),
                        in_=acc[0:r, n * 4 * P:n * 4 * P + DIM], in_offset=None).then_inc(sent, 16)
            pool.wait_ge(sent, 16 * 2 * TILES)

        @block.scalar
        def _(act):
            act.wait_ge(exp_in, 1)
            act.activation(t1[:, :], t1[:, :], ACT.Exp).then_inc(exp_out, 1)

        @block.tensor
        def _(pe):
            pe.wait_ge(picked, 1)
            pe.matmul(ps_pos[:, 0:TE], before[:, :], both.rearrange("p t e -> p (t e)"), start=True, stop=True)
            pe.matmul(ps_tot[:, 0:TE], ones[:, :], both.rearrange("p t e -> p (t e)"), start=True, stop=True).then_inc(counted, 1)

        @block.vector
        def _(dve):
            own = Own(dve, own_v)
            lg = logits[:, :].rearrange("p (t e) -> p t e", e=EXPERTS)
            dve.wait_ge(consts, 3)
            own.do(dve.tensor_copy(rank[:, :], rank_i[:, :]))
            own.do(dve.tensor_copy(tau[:, :], tau_i[:, :]))

            def pick(values, k, onehot):
                own.do(dve.tensor_reduce(top[:, k, :], values, AX.X, ALU.max))
                own.do(dve.tensor_tensor(work, values, bcast(top[:, k, :], 2, EXPERTS), ALU.is_equal))
                own.do(dve.tensor_tensor(work, work, bcast(rank[:, :], 1, TILES), ALU.mult))
                own.do(dve.tensor_reduce(t1[:, :], work, AX.X, ALU.max))
                own.do(dve.tensor_tensor(onehot, bcast(rank[:, :], 1, TILES), bcast(t1[:, :], 2, EXPERTS), ALU.is_equal))
            pick(lg, 0, first)
            own.do(dve.scalar_tensor_tensor(out=pos, in0=first, scalar=-3e38, in1=lg, op0=ALU.mult, op1=ALU.add))
            pick(pos, 1, second)
            own.do(dve.tensor_tensor(both, first, second, ALU.add))
            own.do(dve.tensor_tensor(both, both, bcast(valid[:, :], 2, EXPERTS), ALU.mult))
            dve.sem_inc(picked, 1)
            own.do(dve.tensor_tensor(t1[:, :], top[:, 1, :], top[:, 0, :], ALU.subtract))
            dve.sem_inc(exp_in, 1)
            dve.wait_ge(counted, 1)
            tot = ps_tot[:, 0:TE].rearrange("p (t e) -> p t e", e=EXPERTS)
            own.do(dve.memset(work, 1.0))
            for e in range(EXPERTS):
                own.step(dve.tensor_tensor_scan(pos[:, :, e], work[:, :, e], tot[:, :, e], 0.0, ALU.mult, ALU.add))
            own.wait()
            own.do(dve.tensor_scalar(cnt_i[:, :], pos[:, TILES - 1, :], float(P - 1), None, ALU.add))
            own.do(dve.tensor_scalar(cnt_i[:, :], cnt_i[:, :], P.bit_length() - 1, None, ALU.arith_shift_right))
            own.do(dve.tensor_copy(cnt[:, 0, :], cnt_i[:, :]))
            own.do(dve.tensor_tensor_scan(cnt[:, 1, :], work[:, 0, :], cnt[:, 0, :], 0.0, ALU.mult, ALU.add))
            own.do(dve.tensor_tensor(cnt[:, 2, :], cnt[:, 1, :], cnt[:, 0, :], ALU.subtract))
            own.do(dve.tensor_scalar(cnt[:, 2, :], cnt[:, 2, :], float(P), None, ALU.mult))
            own.do(dve.tensor_tensor(pos, pos, tot, ALU.subtract))
            own.do(dve.tensor_tensor(pos, pos, ps_pos[:, 0:TE].rearrange("p (t e) -> p t e", e=EXPERTS), ALU.add))
            own.do(dve.tensor_tensor(pos, pos, bcast(cnt[:, 2, :], 1, TILES), ALU.add))
            for k, oh in enumerate((first, second)):
                own.do(dve.tensor_tensor(work, oh, pos, ALU.mult))
                own.do(dve.tensor_reduce(top[:, k, :], work, AX.X, ALU.add))
                own.do(dve.tensor_copy(place[:, k * TILES:(k + 1) * TILES], top[:, k, :]))
            dve.sem_inc(placed, 1)
            dve.wait_ge(exp_out, 1)
            own.do(dve.tensor_scalar(top[:, 0, :], t1[:, :], 1.0, None, ALU.add))
            own.do(dve.reciprocal(gate[:, 0:TILES], top[:, 0, :]))
            own.do(dve.tensor_tensor(gate[:, TILES:2 * TILES], gate[:, 0:TILES], t1[:, :], ALU.mult))
            l3 = le[:, :].rearrange("p (t e) -> p t e", e=EXPERTS)
            own.do(dve.tensor_tensor(l3, bcast(cnt[0:1, 1, :], 1, MOE_TILES), bcast(tau[:, :], 2, EXPERTS), ALU.is_le))
            own.do(dve.tensor_reduce(tau[:, :], l3, AX.X, ALU.add))
            own.do(dve.tensor_scalar(tile_expert[0:1, :], tau[:, :], float(EXPERTS - 1), None, ALU.min))


def expert_stage(nc, g):
    acc, ident = g["acc"], g["ident"]
    w1_sb, w2_sb, b2_sb, weights_in = (g[k] for k in ("w1_sb", "w2_sb", "b2_sb", "weights_in"))
    place, gate, tile_expert = g["place"], g["gate"], g["tile_expert"]
    expert_in, expert_out, out = g["expert_in"], g["expert_out"], g["out"]
    T = MOE_TILES

    with ExitStack() as ctx:
        def sb(name, shape, dt=F32):
            return ctx.enter_context(nc.sbuf_tensor(name, shape, dt))

        def sem(name):
            return ctx.enter_context(nc.semaphore(name))

        xe = sb("xe", [P, 2, DIM])
        xeT = sb("xeT", [P, 2, DIM])
        hid = sb("hid", [P, 2, FF])
        hidT = sb("hidT", [P, 2, FF])
        b1_sb = sb("b1_sb", [P, EXPERTS * FF])
        ye = g["ye_sb"].rearrange("p (s d) -> p s d", s=2)
        ps_x = ctx.enter_context(nc.psum_tensor("ps_ex", [P, 2, DIM], F32))
        ps_y = ctx.enter_context(nc.psum_tensor("ps_ey", [P, 2, DIM], F32))
        ps_u = [ctx.enter_context(nc.psum_tensor(f"ps_eu{i}", [P, FF], F32)) for i in range(2)]
        ps_g = [ctx.enter_context(nc.psum_tensor(f"ps_eg{i}", [P, FF], F32)) for i in range(2)]
        own_v, b1_in = None, sem("b1_in")
        xe_in = [sem(f"xe_in{i}") for i in range(2)]
        ye_out = [sem(f"ye_out{i}") for i in range(2)]
        xe_ps, xeT_ready, up_ps, biased, hid_ready, hid_ps, hidT_ready, down_ps, ye_ready = (sem(n) for n in (
            "xe_ps", "xeT_ready", "up_ps", "biased", "hid_ready", "hid_ps", "hidT_ready", "down_ps", "ye_ready"))
        block = ctx.enter_context(nc.Block())

        @block.sync
        def _(sp):
            def load(n, s):
                sp.wait_ge(xe_ps, n + 1)
                sp.dma_start(xe[:, s, :], expert_in[at(n, P), :]).then_inc(xe_in[s], 16)

            def body(n, s):
                load(n, s)
                sp.wait_ge(ye_ready, n - 2 + 1)
                sp.dma_start(expert_out[at(n - 2, P), :], ye[:, s, :]).then_inc(ye_out[s], 16)
            load(0, 0)
            load(1, 1)
            repeat(sp, Own(sp, own_v), 2, T, 2, 0, body)
            for n in (T - 2, T - 1):
                sp.wait_ge(ye_ready, n + 1)
                sp.dma_start(expert_out[n * P:(n + 1) * P, :], ye[:, n % 2, :]).then_inc(ye_out[n % 2], 16)
            for s in range(2):
                sp.wait_ge(ye_out[s], 16 * len(range(s, T, 2)))

        @block.scalar
        def _(act):
            act.dma_start(b1_sb[:, :], g["b1"].rearrange("e f -> (e f)").partition_broadcast(P)).then_inc(b1_in, 16)

            def body(n, s):
                act.wait_ge(xe_ps, n + 3)
                act.activation(xeT[:, s, :], ps_x[:, s, :], ACT.Copy).then_inc(xeT_ready, 1)
                act.wait_ge(biased, n + 1)
                act.activation(hid[:, s, :], hid[:, s, :], ACT.Gelu).then_inc(hid_ready, 1)
            repeat(act, Own(act, own_v), 0, T, 2, 0, body)

        @block.tensor
        def _(pe):
            pe.sem_inc(xe_ps, 2)
            pe.wait_ge(weights_in, 16 * (1 + 2 * EXPERTS))

            def up(n, s):
                pe.wait_ge(xe_in[s], slot_count(n, s, 16, 2))
                for c in range(KC):
                    m = pe.transpose(ps_x[:, s, c * P:(c + 1) * P], xe[:, s, c * P:(c + 1) * P], ident[:, :])
                m.then_inc(xe_ps, 1)
                e = pe.value_load(tile_expert[0:1, at(n)], min_val=0, max_val=EXPERTS - 1)
                pe.wait_ge(xeT_ready, n + 1)
                for c in range(KC):
                    m = pe.matmul(ps_u[s][:, :], xeT[:, s, c * P:(c + 1) * P], w1_sb[:, at(e), c, :].squeeze(1),
                                  start=c == 0, stop=c == KC - 1)
                m.then_inc(up_ps, 1)

            def down(n, s):
                pe.wait_ge(hid_ready, n + 1)
                for c in range(FC):
                    m = pe.transpose(ps_g[s][:, c * P:(c + 1) * P], hid[:, s, c * P:(c + 1) * P], ident[:, :])
                m.then_inc(hid_ps, 1)
                e = pe.value_load(tile_expert[0:1, at(n)], min_val=0, max_val=EXPERTS - 1)
                pe.wait_ge(hidT_ready, n + 1)
                for c in range(FC):
                    m = pe.matmul(ps_y[:, s, :], hidT[:, s, c * P:(c + 1) * P], w2_sb[:, at(e), c, :].squeeze(1),
                                  start=c == 0, stop=c == FC - 1)
                m.then_inc(down_ps, 1)
            up(0, 0)

            def body(n, s):
                up(n, s)
                down(n - 1, 1 - s)
            repeat(pe, Own(pe, own_v), 1, T, 2, 0, body)
            down(T - 1, (T - 1) % 2)

        @block.vector
        def _(dve):
            dve.wait_ge(b1_in, 16)
            dve.wait_ge(weights_in, 16 * (1 + 2 * EXPERTS))

            def bias(n, s):
                dve.wait_ge(up_ps, n + 1)
                e = dve.value_load(tile_expert[0:1, at(n)], min_val=0, max_val=EXPERTS - 1)
                dve.tensor_tensor(hid[:, s, :], ps_u[s][:, :], b1_sb[:, at(e, FF)], ALU.add).then_inc(biased, 1)

            def hidden(n, s):
                dve.wait_ge(hid_ps, n + 1)
                dve.tensor_copy(hidT[:, s, :], ps_g[s][:, :]).then_inc(hidT_ready, 1)

            def result(n, s):
                dve.wait_ge(down_ps, n + 1)
                e = dve.value_load(tile_expert[0:1, at(n)], min_val=0, max_val=EXPERTS - 1)
                if not isinstance(n, int) or n >= 2:
                    dve.wait_ge(ye_out[s], slot_count(n - 2, s, 16, 2))
                dve.tensor_tensor(ye[:, s, :], ps_y[:, s, :], b2_sb[:, at(e, DIM)], ALU.add).then_inc(ye_ready, 1)
            bias(0, 0)
            bias(1, 1)
            hidden(0, 0)
            bias(2, 0)
            result(0, 0)
            hidden(1, 1)
            bias(3, 1)
            result(1, 1)
            hidden(2, 0)

            def body(n, s):
                bias(n, s)
                result(n - 2, s)
                hidden(n - 1, 1 - s)
            repeat(dve, Own(dve, own_v), 4, T, 2, 0, body)
            result(T - 2, (T - 2) % 2)
            hidden(T - 1, (T - 1) % 2)
            result(T - 1, (T - 1) % 2)

    CS = 4
    with ExitStack() as ctx:
        y = ctx.enter_context(nc.sbuf_tensor("y", [P, CS, 2, DIM], F32))
        got = [ctx.enter_context(nc.semaphore(f"got{i}")) for i in range(CS)]
        stored = [ctx.enter_context(nc.semaphore(f"stored{i}")) for i in range(CS)]
        summed, own_v = ctx.enter_context(nc.semaphore("summed")), ctx.enter_context(nc.semaphore("own_v7"))
        block = ctx.enter_context(nc.Block())

        @block.gpsimd
        def _(pool):
            for n in range(TILES):
                r, s = P if n < TILES - 1 else LAST, n % CS
                if n >= CS:
                    pool.wait_ge(stored[s], 16 * (n // CS))
                for k in range(2):
                    pool.indirect_dma_start(
                        out=y[0:r, s, k, :], out_offset=None, in_=expert_out[:, :],
                        in_offset=bass.IndirectOffsetOnAxis(ap=place[0:r, k * TILES + n:k * TILES + n + 1], axis=0),
                    ).then_inc(got[s], 16)

        @block.vector
        def _(dve):
            own = Own(dve, own_v)

            def combine(n, s, r):
                dve.wait_ge(got[s], slot_count(n, s, 32, CS))
                for k in range(2):
                    prev = acc[0:r, bass.ds(n * 4 * P + DIM, DIM)] if k == 0 else y[0:r, s, 0, :]
                    m = dve.scalar_tensor_tensor(out=y[0:r, s, 0, :], in0=y[0:r, s, k, :],
                                                 scalar=gate[0:r, bass.ds(n + k * TILES, 1)], in1=prev,
                                                 op0=ALU.mult, op1=ALU.add)
                    if k == 0:
                        own.do(m)
                m.then_inc(summed, 1)
            repeat(dve, own, 0, TILES - 1, CS, 1, lambda n, s: combine(n, s, P))
            combine(TILES - 1, (TILES - 1) % CS, LAST)

        @block.sync
        def _(sp):
            def body(n, s):
                sp.wait_ge(summed, n + 1)
                sp.dma_start(out[at(n, P), :], y[:, s, 0, :]).then_inc(stored[s], 16)
            repeat(sp, Own(sp, own_v), 0, TILES - 1, CS, 0, body)
            sp.wait_ge(summed, TILES)
            sp.dma_start(out[(TILES - 1) * P:N_NODES, :], y[0:LAST, (TILES - 1) % CS, 0, :]).then_inc(stored[(TILES - 1) % CS], 16)
            for s in range(CS):
                sp.wait_ge(stored[s], 16 * len(range(s, TILES, CS)))


_INS = ["x", "src", "dst", "g_W", "g_asrc", "g_adst", "g_bias", "w_qkv", "mem_kv", "w_out", "b_out", "g_out",
        "g_pre", "gamma", "beta", "Wr", "br", "W1", "b1", "W2", "b2"]


def kernel(x, src, dst, L0_gnn_W, L0_gnn_att_src, L0_gnn_att_dst, L0_gnn_bias, L0_mix_t, L0_mix_w_qkv, L0_mix_mem_kv,
           L0_mix_w_out, L0_mix_b_out, L0_mix_g_out, L0_mix_g_pre, L0_ffn_gamma, L0_ffn_beta, L0_ffn_Wr, L0_ffn_br,
           L0_ffn_W1, L0_ffn_b1, L0_ffn_W2, L0_ffn_b2):
    import numpy as _np
    import concourse.bacc as _bacc
    from concourse import mybir as _mybir
    from concourse.bass_utils import run_bass_kernel_spmd as _run

    def edges(a, fill):
        a = _np.pad(_np.asarray(a), (0, BLOCKS * BLOCK - N_EDGES), constant_values=fill)
        return _np.ascontiguousarray(a.reshape(BLOCKS, P, SUB).transpose(1, 0, 2).reshape(P, BLOCKS * SUB))

    values = dict(zip(_INS, [
        _np.pad(_np.asarray(x), ((0, N_PAD - N_NODES), (0, 0))), edges(src, 0), edges(dst, N_PAD + 2 * WIN),
        L0_gnn_W, L0_gnn_att_src, L0_gnn_att_dst, L0_gnn_bias, L0_mix_w_qkv, L0_mix_mem_kv, L0_mix_w_out, L0_mix_b_out,
        L0_mix_g_out, L0_mix_g_pre, L0_ffn_gamma, L0_ffn_beta, L0_ffn_Wr, L0_ffn_br, L0_ffn_W1, L0_ffn_b1, L0_ffn_W2,
        L0_ffn_b2]))
    nc = _bacc.Bacc("TRN2", target_bir_lowering=False, num_devices=1)
    arrays, args = {}, []
    for name in _INS:
        a = _np.ascontiguousarray(values[name])
        arrays[f"in_{name}_dram"] = a
        args.append(nc.dram_tensor(f"in_{name}_dram", a.shape, _mybir.dt.from_np(a.dtype), kind="ExternalInput").ap())
    args.append(nc.dram_tensor("out_0_dram", (N_NODES, DIM), _mybir.dt.float32, kind="ExternalOutput").ap())
    gps_layer(nc, *args)
    r = _run(nc, [arrays], core_ids=[0])
    return r.results[0]["out_0_dram"]
```

```python
from contextlib import ExitStack

import concourse.bass as bass
from concourse import mybir

ALU = mybir.AluOpType
ACT = mybir.ActivationFunctionType
AX = mybir.AxisListType
F32 = mybir.dt.float32
I32 = mybir.dt.int32

P = 128
N_NODES = 6250
DIM = 256
TILES = -(-N_NODES // P)
N_PAD = TILES * P
LAST = N_NODES - (TILES - 1) * P
KC = DIM // P

G_HEADS = 4
F_HEAD = DIM // G_HEADS
ROW = DIM + G_HEADS
SLOPE = 0.2
LN_EPS = 1e-5

N_EDGES = 206250
SUB = 4
BLOCK = SUB * P
BLOCKS = -(-N_EDGES // BLOCK)
WIN = 32
ACC_W = N_PAD + WIN
WINDOWS = -(-N_NODES // WIN)
GUARD = 40.0

M_HEADS = 4
D_HEAD = 32
HID = M_HEADS * D_HEAD
N_MEM = 4
KV_W = 2 * HID + 4

EXPERTS = 8
FF = 512
FC = FF // P
MOE_TILES = (2 * N_NODES + EXPERTS * (P - 1)) // P
SLOTS = MOE_TILES * P


class Own:

    def __init__(self, eng, sem):
        self.eng, self.sem, self.base, self.k = eng, sem, 0, 0

    def step(self, ins):
        ins.then_inc(self.sem, 1)
        self.k += 1
        return ins

    def wait(self):
        self.eng.wait_ge(self.sem, self.base + self.k)

    def do(self, ins):
        self.step(ins)
        self.wait()


def repeat(eng, own, first, total, unroll, per, body):
    full = (total - first) // unroll
    start = own.base + own.k
    if full:
        with eng.Fori(0, full) as it:
            for u in range(unroll):
                n = it * unroll + (first + u)
                own.base, own.k = start + (it * unroll + u) * per, 0
                body(n, (first + u) % unroll)
                assert own.k == per, (own.k, per)
    for n in range(first + full * unroll, total):
        own.base, own.k = start + (n - first) * per, 0
        body(n, n % unroll)
        assert own.k == per, (own.k, per)
    own.base, own.k = start + (total - first) * per, 0


def rounds(eng, own, first, count, slots, per, body, extra, extra_per):
    start, each = own.base + own.k, slots * per + sum(extra_per)
    with eng.Fori(0, count) as t:
        for u in range(slots):
            own.base, own.k = start + (t * each + (u * per + sum(extra_per[:u]))), 0
            body(t * slots + (first + u), (first + u) % slots)
            extra(t, u)
            assert own.k == per + extra_per[u], (own.k, per, extra_per[u])
    own.base, own.k = start + count * each, 0


def bcast(ap, axis, n):
    v = ap.unsqueeze(axis)
    shape = list(v.shape)
    shape[axis] = n
    return v.to_broadcast(shape)


def at(n, size=1):
    return bass.ds(n * size, size)


def gps_layer(nc, x, src, dst, g_W, g_asrc, g_adst, g_bias, w_qkv, mem_kv, w_out, b_out, g_out, g_pre,
              gamma, beta, Wr, br, W1, b1, W2, b2, out):
    table = nc.dram_tensor("node_table", [N_PAD, ROW], F32)
    dst_table = nc.dram_tensor("dst_table", [ACC_W, 2 * G_HEADS], F32)
    base_rows = nc.dram_tensor("base_rows", [N_PAD, DIM], F32)
    mixed_rows = nc.dram_tensor("mixed_rows", [N_PAD, DIM], F32)
    expert_in = nc.dram_tensor("expert_in", [SLOTS, DIM], F32)
    expert_out = nc.dram_tensor("expert_out", [SLOTS, DIM], F32)

    ctx = ExitStack()
    with ctx:
        def sb(name, shape, dt=F32, stack=ctx):
            return stack.enter_context(nc.sbuf_tensor(name, shape, dt))

        acc = sb("acc", [P, ACC_W * 4])
        region = sb("region", [P, TILES * (KV_W + HID)])
        ident = sb("ident", [P, P])
        ones = sb("ones", [P, P])
        valid = sb("valid", [P, TILES])
        sd = sb("sd", [P, TILES * 8])
        w_self = sb("w_self", [P, TILES * G_HEADS])
        spans = sb("spans", [1, 2], I32)

        dve_steps = Own(None, ctx.enter_context(nc.semaphore("dve_steps")))
        with ExitStack() as mix_ctx:
            q_all = region[:, TILES * KV_W:].rearrange("p (t c) -> p t c", c=HID)
            q_inv = sb("q_inv", [P, TILES * M_HEADS], stack=mix_ctx)
            mmat = sb("mmat", [P, DIM], stack=mix_ctx)
            mix_rows = sb("mix_rows", [P, 2, DIM], stack=mix_ctx)
            node_used = []
            node_stage(nc, ctx, locals())
            edge_buffers = {}
            edge_stage(nc, locals())
            any_order_stage(nc, locals())

        W = EXPERTS * KC * FF
        w1_sb = region[:, 0:W].rearrange("p (e c f) -> p e c f", e=EXPERTS, c=KC)
        w2_sb = region[:, W:2 * W].rearrange("p (e c f) -> p e c f", e=EXPERTS, c=FC)
        b2_sb = region[:, 2 * W:2 * W + EXPERTS * DIM]
        ye_sb = region[:, 2 * W + EXPERTS * DIM:2 * W + (EXPERTS + 2) * DIM]
        logits = sb("logits", [P, TILES * EXPERTS])
        wr = sb("wr", [P, KC * EXPERTS])
        place = sb("place", [P, 2 * TILES], I32)
        gate = sb("gate", [P, 2 * TILES])
        tile_expert = sb("tile_expert", [1, MOE_TILES], I32)
        weights_in = ctx.enter_context(nc.semaphore("weights_in"))
        rows_stage(nc, locals())
        route_stage(nc, locals())
        expert_stage(nc, locals())


def node_stage(nc, ctx0, g):
    acc, region, ident, ones, valid, sd, w_self = (g[k] for k in ("acc", "region", "ident", "ones", "valid", "sd", "w_self"))
    table, dst_table, base_rows = g["table"], g["dst_table"], g["base_rows"]
    x_all = acc[:, 0:TILES * DIM].rearrange("p (t d) -> p t d", d=DIM)
    kv = region[:, 0:TILES * KV_W].rearrange("p (t c) -> p t c", c=KV_W)
    q_all, q_inv, mmat, mix_rows = (g[k] for k in ("q_all", "q_inv", "mmat", "mix_rows"))
    sd3 = sd[:, :].rearrange("p (t c) -> p t c", c=8)
    X_GROUPS = 7
    XG = TILES // X_GROUPS

    used = [TILES * DIM]

    def carve(*shape):
        size = 1
        for d in shape:
            size *= d
        v = acc[:, used[0]:used[0] + size]
        used[0] += size
        return v if len(shape) == 1 else v.rearrange("p (a b) -> p a b", b=shape[1])

    with ExitStack() as ctx:
        def sb(name, shape, dt=F32):
            return ctx.enter_context(nc.sbuf_tensor(name, shape, dt))

        def pb(name, shape):
            return ctx.enter_context(nc.psum_tensor(name, shape, F32))

        def sem(name):
            return ctx.enter_context(nc.semaphore(name))

        w_h = carve(KC, DIM + 8)
        w_q = carve(KC, 3 * HID)
        gpre = sb("gpre", [P, KC])
        att = carve(2, DIM)
        bias_row = carve(DIM)
        w_o = sb("w_o", [P, DIM])
        mem_k = sb("mem_k", [N_MEM, HID])
        mem_v = sb("mem_v", [N_MEM, HID + 4])
        tmp = sb("tmp", [P, DIM])
        st = sb("st", [P, TILES, 6])
        mv = sb("mv", [P, TILES, 2])
        s1 = sb("s1", [P, TILES])
        s2 = sb("s2", [P, TILES])
        rstd = sb("rstd", [P, TILES])
        r_scale = sb("r_scale", [P, TILES])
        r_bias = sb("r_bias", [P, TILES])
        un_scale = sb("un_scale", [P, TILES])
        eps = sb("eps", [P, 2])
        xr = carve(2, DIM)
        xrT = carve(2, DIM)
        hrow = carve(2, DIM + 8)
        small = carve(8, TILES * G_HEADS)
        drow = sb("drow", [P, TILES * 8])
        kmb = sb("kmb", [P, HID])
        kcol = sb("kcol", [P, 2])
        cmat = sb("cmat", [P, HID])
        cT = sb("cT", [P, HID])
        ps_t = pb("ps_t", [P, 2, DIM])
        ps_h = [pb(f"ps_h{i}", [P, 512]) for i in range(2)]
        ps_q = [pb(f"ps_q{i}", [P, 512]) for i in range(2)]
        ps_c = pb("ps_c", [P, 512])
        ps_m = pb("ps_m", [P, 512])

        x_in = [sem(f"x_in{i}") for i in range(X_GROUPS)]
        loads = sem("loads")
        consts = sem("consts")
        own_p = sem("own_p")
        stats = sem("stats")
        sqrt1, sqrt2 = sem("sqrt1"), sem("sqrt2")
        r_ready = sem("r_ready")
        weights = sem("weights")
        xr_ready, xT_ps, xT_ready = sem("xr_ready"), sem("xT_ps"), sem("xT_ready")
        h_ps, q_ps, h_ready, q_ready = sem("h_ps"), sem("q_ps"), sem("h_ready"), sem("q_ready")
        table_out = [sem(f"table_out{i}") for i in range(2)]
        smax_ready, smax_T, gdiag, gmax_ps = sem("smax_ready"), sem("smax_T"), sem("gdiag"), sem("gmax_ps")
        dlog, dexp, drow_ready, d_out = sem("dlog"), sem("dexp"), sem("drow_ready"), sem("d_out")
        kmax_ready, kmax_T, kdiag, kmax_ps = sem("kmax_ready"), sem("kmax_T"), sem("kdiag"), sem("kmax_ps")
        k_shift, k_exp = sem("k_shift"), sem("k_exp")
        q_shift, q_exp = sem("q_shift"), sem("q_exp")
        ctx_ps, c_ready, cT_ps, cT_ready, m_ps = (sem(n) for n in ("ctx_ps", "c_ready", "cT_ps", "cT_ready", "m_ps"))
        base_ready, base_out = sem("base_ready"), sem("base_out")
        g["node_used"].append(used[0])
        block = ctx.enter_context(nc.Block())
        N_LOADS = 12

        @block.sync
        def _(sp):
            xv = g["x"].rearrange("(t p) d -> p t d", p=P)
            for i in range(X_GROUPS):
                sp.dma_start(x_all[:, i * XG:(i + 1) * XG, :], xv[:, i * XG:(i + 1) * XG, :]).then_inc(x_in[i], 16)
            def body(n, s):
                sp.wait_ge(h_ready, n + 3)
                sp.dma_start(table[at(n, P), :], hrow[:, s, 0:ROW]).then_inc(table_out[s], 16)
                sp.wait_ge(base_ready, n + 1)
                sp.dma_start(base_rows[at(n, P), :], x_all[:, at(n), :].squeeze(1)).then_inc(base_out, 16)
            for_sp(sp, TILES, body)
            sp.wait_ge(drow_ready, 1)
            sp.dma_start(dst_table[0:N_PAD, :].rearrange("(t p) c -> p t c", p=P),
                         drow[:, :].rearrange("p (t c) -> p t c", c=8)).then_inc(d_out, 16)
            sp.dma_start(dst_table[N_PAD:ACC_W, :], tmp[0:WIN, 0:8]).then_inc(d_out, 16)
            for i in range(2):
                sp.wait_ge(table_out[i], 16 * ((TILES + 1 - i) // 2))
            sp.wait_ge(d_out, 32)
            sp.wait_ge(base_out, 16 * TILES)

        @block.gpsimd
        def _(pool):
            pool.memset(ident[:, :], 0.0).then_inc(own_p, 1)
            pool.memset(valid[:, :], 1.0).then_inc(own_p, 1)
            pool.memset(ones[:, :], 1.0).then_inc(consts, 1)
            pool.wait_ge(own_p, 2)
            pool.affine_select(out=ident[:, :], in_=ident[:, :], compare_op=ALU.not_equal, fill=1.0, base=0,
                               pattern=[[-1, P]], channel_multiplier=1).then_inc(consts, 1)
            pool.affine_select(out=valid[:, :], in_=valid[:, :], compare_op=ALU.is_gt, fill=0.0, base=N_NODES,
                               pattern=[[-P, TILES]], channel_multiplier=-1).then_inc(consts, 1)
            pool.memzero(acc[:, used[0]:]).then_inc(consts, 1)

        @block.scalar
        def _(act):
            for c in range(KC):
                act.dma_start(w_h[:, c, 0:DIM].rearrange("p (h f) -> p h f", f=F_HEAD),
                              g["g_W"][:, c * P:(c + 1) * P, :].rearrange("h p f -> p h f")).then_inc(loads, 16)
            act.dma_start(w_q[:, :, :], g["w_qkv"].rearrange("(c p) n -> p c n", p=P)).then_inc(loads, 16)
            act.dma_start(gpre[:, :], g["g_pre"].rearrange("(c p) -> p c", p=P), allow_slow_non_contiguous=True).then_inc(loads, 16)
            for i, a in enumerate((g["g_asrc"], g["g_adst"])):
                act.dma_start(att[:, i, :], a.rearrange("h f -> (h f)").partition_broadcast(P)).then_inc(loads, 16)
            act.dma_start(bias_row, g["g_bias"].partition_broadcast(P)).then_inc(loads, 16)
            for i, a in enumerate((g["b_out"], g["g_out"])):
                act.dma_start(mix_rows[:, i, :], a.partition_broadcast(P)).then_inc(loads, 16)
            act.dma_start(w_o[:, :], g["w_out"]).then_inc(loads, 16)
            act.dma_start(mem_k[:, :], g["mem_kv"][0].rearrange("h d m -> m (h d)"), allow_slow_non_contiguous=True).then_inc(loads, 16)
            act.dma_start(mem_v[:, 0:HID], g["mem_kv"][1].rearrange("h d m -> m (h d)"), allow_slow_non_contiguous=True).then_inc(loads, 16)
            act.wait_ge(stats, 1)
            act.activation(s1[:, :], mv[:, :, 1], ACT.Sqrt, bias=eps[:, 0:1]).then_inc(sqrt1, 1)
            act.wait_ge(stats, 2)
            act.activation(s2[:, :], s1[:, :], ACT.Sqrt).then_inc(sqrt2, 1)
            act.wait_ge(r_ready, 1)

            def unit_rows(n, s):
                act.wait_ge(xT_ps, n + 1)
                act.wait_ge(q_ready, n + 1)
                act.activation(xr[:, s, :], x_all[:, at(n), :].squeeze(1), ACT.Identity,
                               bias=r_bias[:, at(n)], scale=r_scale[:, at(n)]).then_inc(xr_ready, 1)

            def table_rows(n, s):
                act.wait_ge(h_ps, n + 1)
                act.activation(hrow[:, s, :], ps_h[s][:, 0:DIM + 8], ACT.Copy, scale=un_scale[:, at(n)]).then_inc(h_ready, 1)

            for_act(act, TILES, unit_rows, table_rows, table_out)
            act.wait_ge(dlog, 1)
            act.activation(w_self[:, :], small[:, 0, :], ACT.Exp).then_inc(dexp, 1)
            act.wait_ge(k_shift, 1)
            act.activation(kv[:, :, 0:HID], kv[:, :, 0:HID], ACT.Exp).then_inc(k_exp, 1)
            act.activation(mem_k[:, :], mem_k[:, :], ACT.Exp).then_inc(k_exp, 1)
            act.wait_ge(q_shift, 1)
            act.activation(q_all, q_all, ACT.Exp).then_inc(q_exp, 1)

        @block.tensor
        def _(pe):
            own = Own(pe, None)
            pe.sem_inc(xT_ps, 2)
            pe.wait_ge(consts, 3)
            pe.wait_ge(weights, 1)

            def body(n, s):
                pe.wait_ge(xr_ready, n + 1)
                for c in range(KC):
                    m = pe.transpose(ps_t[:, s, c * P:(c + 1) * P], xr[:, s, c * P:(c + 1) * P], ident[:, :])
                m.then_inc(xT_ps, 1)
                pe.wait_ge(xT_ready, n + 1)
                pe.wait_ge(h_ready, n + 1)
                for c in range(KC):
                    m = pe.matmul(ps_h[s][:, 0:DIM + 8], xrT[:, s, c * P:(c + 1) * P], w_h[:, c, :],
                                  start=c == 0, stop=c == KC - 1)
                m.then_inc(h_ps, 1)
                pe.wait_ge(q_ready, n + 1)
                for c in range(KC):
                    m = pe.matmul(ps_q[s][:, 0:3 * HID], xrT[:, s, c * P:(c + 1) * P], w_q[:, c, :],
                                  start=c == 0, stop=c == KC - 1)
                m.then_inc(q_ps, 1)
            repeat(pe, own, 0, TILES, 2, 0, body)
            pe.wait_ge(smax_ready, 1)
            pe.transpose(ps_c[0:G_HEADS, 0:P], small[:, 7, 0:G_HEADS], ident[:, :]).then_inc(smax_T, 1)
            pe.wait_ge(gdiag, 1)
            pe.matmul(ps_c[:, 256:256 + G_HEADS], ones[0:G_HEADS, :], tmp[0:G_HEADS, 128:128 + G_HEADS],
                      start=True, stop=True).then_inc(gmax_ps, 1)
            pe.wait_ge(kmax_ready, 1)
            pe.transpose(ps_t[:, 0, 0:P], kmb[:, :], ident[:, :]).then_inc(kmax_T, 1)
            pe.wait_ge(kdiag, 1)
            pe.matmul(ps_t[:, 1, 0:HID], ones[:, :], cmat[:, :], start=True, stop=True).then_inc(kmax_ps, 1)
            pe.wait_ge(k_exp, 2)
            for n in range(TILES):
                rows_n = P if n < TILES - 1 else LAST
                pe.matmul(ps_m[:, 0:HID + 4], kv[0:rows_n, n, 0:HID], kv[0:rows_n, n, HID:KV_W],
                          start=n == 0, stop=False)
            pe.matmul(ps_m[:, 0:HID + 4], mem_k[:, :], mem_v[:, :], start=False, stop=True).then_inc(ctx_ps, 1)
            pe.wait_ge(c_ready, 1)
            pe.transpose(ps_t[:, 0, 0:P], cmat[:, :], ident[:, :]).then_inc(cT_ps, 1)
            pe.wait_ge(cT_ready, 1)
            pe.matmul(ps_m[:, 0:DIM], cT[:, :], w_o[:, :], start=True, stop=True).then_inc(m_ps, 1)

        @block.vector
        def _(dve):
            own = g["dve_steps"]
            own.eng = dve
            dve.sem_inc(h_ready, 2)
            dve.sem_inc(q_ready, 2)
            dve.memset(eps[:, 0:1], LN_EPS)
            own.do(dve.memset(kv[:, :, 2 * HID:KV_W], 1.0))
            for i in range(X_GROUPS):
                dve.wait_ge(x_in[i], 16)

                def moments(n, s):
                    own.step(dve.bn_stats(st[:, at(n + i * XG), :].squeeze(1), x_all[:, at(n + i * XG), :].squeeze(1)))
                repeat(dve, own, 0, XG, 1, 1, moments)
            own.wait()
            join_moments(dve, own, st, mv, s1)
            dve.sem_inc(stats, 1)
            dve.wait_ge(sqrt1, 1)
            own.do(dve.reciprocal(rstd[:, :], s1[:, :]))
            own.do(dve.tensor_tensor(s2[:, :], rstd[:, :], rstd[:, :], ALU.mult))
            own.do(dve.tensor_tensor(s2[:, :], s2[:, :], mv[:, :, 1], ALU.mult))
            own.do(dve.tensor_scalar(s1[:, :], s2[:, :], float(DIM), 1e-24, ALU.mult, ALU.max))
            dve.sem_inc(stats, 1)
            dve.wait_ge(sqrt2, 1)
            own.do(dve.tensor_scalar(un_scale[:, :], s2[:, :], 1.0 / 16, None, ALU.mult))
            own.do(dve.reciprocal(s1[:, :], un_scale[:, :]))
            own.do(dve.tensor_tensor(r_scale[:, :], s1[:, :], rstd[:, :], ALU.mult))
            own.do(dve.scalar_tensor_tensor(out=r_bias[:, :], in0=mv[:, :, 0], scalar=-1.0, in1=r_scale[:, :],
                                            op0=ALU.mult, op1=ALU.mult))
            dve.sem_inc(r_ready, 1)
            dve.wait_ge(loads, 16 * N_LOADS)
            for i in range(2):
                for c in range(KC):
                    own.do(dve.tensor_tensor(tmp[:, :], w_h[:, c, 0:DIM], att[:, i, :], ALU.mult))
                    own.do(dve.tensor_reduce(w_h[:, c, DIM + 4 * i:DIM + 4 * i + 4],
                                             tmp[:, :].rearrange("p (h f) -> p h f", f=F_HEAD), AX.X, ALU.add))
            for c in range(KC):
                own.do(dve.tensor_scalar(w_q[:, c, :], w_q[:, c, :], gpre[:, c:c + 1], None, ALU.mult))
            dve.sem_inc(weights, 1)

            def body(n, s):
                dve.wait_ge(xT_ps, n + 3)
                dve.tensor_copy(xrT[:, s, :], ps_t[:, s, :]).then_inc(xT_ready, 1)
                xt = x_all[:, at(n), :].squeeze(1)
                own.do(dve.scalar_tensor_tensor(out=xt, in0=xr[:, s, :], scalar=un_scale[:, at(n)], in1=xt,
                                                op0=ALU.mult, op1=ALU.add))
                own.do(dve.tensor_tensor(xt, xt, bias_row, ALU.add))
                dve.sem_inc(base_ready, 1)
                dve.wait_ge(h_ready, n + 3)
                own.do(dve.tensor_copy(sd3[:, at(n), :].squeeze(1), hrow[:, s, DIM:DIM + 8]))
                dve.wait_ge(q_ps, n + 1)
                own.step(dve.tensor_copy(q_all[:, at(n), :].squeeze(1), ps_q[s][:, 0:HID]))
                own.step(dve.tensor_copy(kv[:, at(n), 0:2 * HID].squeeze(1), ps_q[s][:, HID:3 * HID]))
                own.wait()
                dve.sem_inc(q_ready, 1)
            repeat(dve, own, 0, TILES, 2, 5, body)
            dve.wait_ge(q_ready, TILES + 2)
            s_, d_ = sd3[:, :, 0:4], sd3[:, :, 4:8]

            def sm(i):
                return small[:, i, :].rearrange("p (t h) -> p t h", h=G_HEADS)
            dve.wait_ge(consts, 3)
            own.do(dve.tensor_tensor(sm(1), s_, bcast(valid[:, :], 2, G_HEADS), ALU.mult))
            own.do(dve.tensor_scalar(s1[:, :], valid[:, :], 1e30, -1e30, ALU.mult, ALU.add))
            own.do(dve.tensor_tensor(sm(1), sm(1), bcast(s1[:, :], 2, G_HEADS), ALU.add))
            own.do(dve.tensor_reduce(small[:, 7, 0:G_HEADS], sm(1).rearrange("p t h -> p h t"), AX.X, ALU.max))
            dve.sem_inc(smax_ready, 1)
            dve.wait_ge(smax_T, 1)
            own.do(dve.tensor_reduce(kcol[0:G_HEADS, 0:1], ps_c[0:G_HEADS, 0:P], AX.X, ALU.max))
            own.do(dve.tensor_scalar(tmp[0:G_HEADS, 128:128 + G_HEADS], ident[0:G_HEADS, 0:G_HEADS],
                                     kcol[0:G_HEADS, 0:1], None, ALU.mult))
            dve.sem_inc(gdiag, 1)
            dve.wait_ge(gmax_ps, 1)
            own.do(dve.tensor_copy(small[:, 7, 0:G_HEADS], ps_c[:, 256:256 + G_HEADS]))
            own.do(dve.tensor_tensor(sm(1), d_, bcast(small[:, 7, 0:G_HEADS], 1, TILES), ALU.add))
            own.do(dve.scalar_tensor_tensor(out=sm(2), in0=sm(1), scalar=SLOPE, in1=sm(1), op0=ALU.mult, op1=ALU.max))
            own.do(dve.tensor_tensor(sm(3), s_, d_, ALU.add))
            own.do(dve.scalar_tensor_tensor(out=sm(4), in0=sm(3), scalar=SLOPE, in1=sm(3), op0=ALU.mult, op1=ALU.max))
            own.do(dve.scalar_tensor_tensor(out=sm(5), in0=sm(4), scalar=GUARD, in1=sm(2), op0=ALU.add, op1=ALU.min))
            own.do(dve.tensor_tensor(sm(0), sm(4), sm(5), ALU.subtract))
            dve.sem_inc(dlog, 1)
            dr = drow[:, :].rearrange("p (t c) -> p t c", c=8)
            own.do(dve.tensor_copy(dr[:, :, 0:4], d_))
            own.do(dve.tensor_copy(dr[:, :, 4:8], sm(5)))
            own.do(dve.memset(tmp[:, 0:8], 0.0))
            dve.sem_inc(drow_ready, 1)
            own.do(dve.memset(mem_v[:, HID:HID + 4], 1.0))
            kk = kv[:, :, 0:HID]
            own.do(dve.tensor_reduce(kmb[:, :], kk[:, 0:TILES - 1, :].rearrange("p t c -> p c t"), AX.X, ALU.max))
            own.do(dve.tensor_tensor(kmb[0:LAST, :], kmb[0:LAST, :], kv[0:LAST, TILES - 1, 0:HID], ALU.max))
            own.do(dve.tensor_tensor(kmb[0:N_MEM, :], kmb[0:N_MEM, :], mem_k[:, :], ALU.max))
            dve.sem_inc(kmax_ready, 1)
            dve.wait_ge(kmax_T, 1)
            own.do(dve.tensor_reduce(kcol[:, 0:1], ps_t[:, 0, 0:P], AX.X, ALU.max))
            own.do(dve.tensor_scalar(cmat[:, :], ident[:, :], kcol[:, 0:1], None, ALU.mult))
            dve.sem_inc(kdiag, 1)
            dve.wait_ge(kmax_ps, 1)
            own.do(dve.tensor_copy(kmb[:, :], ps_t[:, 1, 0:HID]))
            own.do(dve.tensor_tensor(mem_k[:, :], mem_k[:, :], kmb[0:N_MEM, :], ALU.subtract))
            own.do(dve.tensor_tensor(kk, kk, bcast(kmb[:, :], 1, TILES), ALU.subtract))
            dve.sem_inc(k_shift, 1)
            qv = q_all.rearrange("p t (h d) -> p t h d", d=D_HEAD)
            qm = small[:, 1, :].rearrange("p (t h) -> p t h", h=M_HEADS)
            own.do(dve.tensor_reduce(qm, qv, AX.X, ALU.max))
            for h in range(M_HEADS):
                own.step(dve.tensor_tensor(qv[:, :, h, :], qv[:, :, h, :], bcast(qm[:, :, h], 2, D_HEAD), ALU.subtract))
            own.wait()
            dve.sem_inc(q_shift, 1)
            own.do(dve.memset(cmat[:, :], 0.0))
            dve.wait_ge(ctx_ps, 1)
            own.do(dve.reciprocal(kcol[:, 1:2], ps_m[:, HID:HID + 1]))
            for h in range(M_HEADS):
                r = slice(h * D_HEAD, (h + 1) * D_HEAD)
                own.step(dve.tensor_scalar(cmat[r, r], ps_m[r, r], kcol[r, 1:2], None, ALU.mult))
            own.wait()
            dve.sem_inc(c_ready, 1)
            dve.wait_ge(cT_ps, 1)
            own.do(dve.tensor_copy(cT[:, :], ps_t[:, 0, 0:P]))
            dve.sem_inc(cT_ready, 1)
            dve.wait_ge(m_ps, 1)
            own.do(dve.tensor_copy(mmat[:, :], ps_m[:, 0:DIM]))
            dve.wait_ge(q_exp, 1)
            own.do(dve.tensor_reduce(qm, qv, AX.X, ALU.add))
            q2 = q_inv[:, :].rearrange("p (t h) -> p t h", h=M_HEADS)
            own.do(dve.reciprocal(q2, qm))
            own.do(dve.tensor_scalar(q2, q2, D_HEAD ** -0.5, None, ALU.mult))


def join_moments(dve, own, st, mv, tmp):
    own.do(dve.tensor_tensor(mv[:, :, 0], st[:, :, 1], st[:, :, 4], ALU.add))
    own.do(dve.tensor_scalar(mv[:, :, 0], mv[:, :, 0], 0.5, None, ALU.mult))
    own.do(dve.tensor_tensor(tmp[:, :], st[:, :, 1], st[:, :, 4], ALU.subtract))
    own.do(dve.scalar_tensor_tensor(out=tmp[:, :], in0=tmp[:, :], scalar=0.25, in1=tmp[:, :], op0=ALU.mult, op1=ALU.mult))
    own.do(dve.tensor_tensor(mv[:, :, 1], st[:, :, 2], st[:, :, 5], ALU.add))
    own.do(dve.scalar_tensor_tensor(out=mv[:, :, 1], in0=mv[:, :, 1], scalar=1.0 / DIM, in1=tmp[:, :],
                                    op0=ALU.mult, op1=ALU.add))


def for_sp(sp, total, body):
    with sp.Fori(0, total // 2) as it:
        for u in range(2):
            body(it * 2 + u, u)
    for n in range(total // 2 * 2, total):
        body(n, n % 2)


def for_act(act, total, first, second, table_out):
    first(0, 0)
    first(1, 1)
    second(0, 0)
    second(1, 1)
    with act.Fori(1, total // 2) as it:
        for u in range(2):
            first(it * 2 + u, u)
        for u in range(2):
            act.wait_ge(table_out[u], it * 16)
            second(it * 2 + u, u)
    n = total - 1
    first(n, 0)
    act.wait_ge(table_out[0], n // 2 * 16)
    second(n, 0)


def edge_stage(nc, g):
    acc, region, ident, ones, spans = (g[k] for k in ("acc", "region", "ident", "ones", "spans"))
    table, dst_table = g["table"], g["dst_table"]
    acc4 = acc[:, :].rearrange("p (w c) -> p w c", c=4)
    SL = 3
    PAUSE = 1 + SL * TILES
    SECOND = PAUSE + 2 * SL
    THIRD = SECOND + SL * TILES
    assert THIRD + SL <= BLOCKS

    def nothing(t, u):
        pass

    used = [0]

    def carve(*shape, dt=F32):
        size = 1
        for s in shape:
            size *= s
        v = region[:, used[0]:used[0] + size]
        used[0] += size
        if dt != F32:
            v = v.bitcast(dt)
        return v

    src_idx = carve((BLOCKS + 2) * SUB, dt=I32)
    idx = carve(SL * SUB, dt=I32)
    dst_raw = carve((BLOCKS + 1) * SUB, dt=I32)
    rel = carve((BLOCKS + 1) * SUB)
    rows = carve(SL * SUB * ROW).rearrange("p (s j c) -> p s j c", s=SL, j=SUB)
    mask = carve(SL * SUB * WIN).rearrange("p (s j w) -> p s j w", s=SL, j=SUB)
    maskT = carve(SL * P).rearrange("p (s e) -> p s e", s=SL)
    dwin = carve(SL * 8).rearrange("p (s c) -> p s c", s=SL)
    dblk = carve(SL * SUB * 8).rearrange("p (s j c) -> p s j c", s=SL, j=SUB)
    wts = carve(SL * SUB * P).rearrange("p (s j c) -> p s j c", s=SL, j=SUB)
    wsum = carve(SL * P).rearrange("p (s c) -> p s c", s=SL)
    lg = carve(SL * SUB * G_HEADS).rearrange("p (s j h) -> p s j h", s=SL, j=SUB)
    ex = carve(SL * SUB * G_HEADS).rearrange("p (s j h) -> p s j h", s=SL, j=SUB)
    z = carve(SUB * G_HEADS).rearrange("p (j h) -> p j h", j=SUB)
    lr = carve(SUB * G_HEADS).rearrange("p (j h) -> p j h", j=SUB)
    win_i = carve(WIN, dt=I32)
    win = carve(WIN)
    bm = carve(SUB * 8).rearrange("p (j c) -> p j c", j=SUB)
    bases = carve(BLOCKS + 1, dt=I32)
    bases_f = carve(BLOCKS)
    badn = carve(2)
    zeros = carve(DIM)
    assert used[0] <= TILES * KV_W
    DVE_ZERO = g["node_used"][0] * 9 // 16
    q_all, q_inv, mmat, mix_rows, base_rows, mixed_rows = (g[k] for k in (
        "q_all", "q_inv", "mmat", "mix_rows", "base_rows", "mixed_rows"))
    bad, badc = region[:, TILES * KV_W:TILES * KV_W + BLOCKS * SUB], region[:, TILES * KV_W + BLOCKS * SUB:
                                                                            TILES * KV_W + 2 * BLOCKS * SUB]
    g["edge_buffers"].update(locals())

    with ExitStack() as ctx:
        def sem(name):
            return ctx.enter_context(nc.semaphore(name))
        ps_p = [ctx.enter_context(nc.psum_tensor(f"ps_p{i}", [P, 512], F32)) for i in range(SL)]
        ps_s = [ctx.enter_context(nc.psum_tensor(f"ps_s{i}", [P, 512], F32)) for i in range(SL)]
        ps_b = ctx.enter_context(nc.psum_tensor("ps_b", [P, 512], F32))
        ps_o = ctx.enter_context(nc.psum_tensor("ps_o", [P, 512], F32))

        def sb(name, shape):
            return ctx.enter_context(nc.sbuf_tensor(name, shape, F32))
        qn, qT, o_row = sb("qn", [P, HID]), sb("qT", [P, HID]), sb("o_row", [P, DIM])
        ob_in = sb("ob_in", [P, 2, DIM])
        st, mv = sb("st_mix", [P, TILES, 6]), sb("mv_mix", [P, TILES, 2])
        s1, s2 = sb("s1_mix", [P, TILES]), sb("s2_mix", [P, TILES])
        qn_ready, qT_ps, qT_ready, o_ps, o_ready, o_out, ss_ready, ss_sqrt, tile_in, base_ready, base_out = (
            sem("mix_" + n) for n in ("qn_ready", "qT_ps", "qT_ready", "o_ps", "o_ready", "o_out", "ss_ready",
                                      "ss_sqrt", "tile_in", "base_ready", "base_out"))

        src_in, dst_in, own_p = sem("src_in"), sem("dst_in"), sem("own_p2")
        pool_consts, bases_f_ready, bases_ps, span_ready, span_ps = (sem(n) for n in (
            "pool_consts", "bases_f_ready", "bases_ps", "span_ready", "span_ps"))
        gathered = [sem(f"gathered{i}") for i in range(SL)]
        dwin_in = [sem(f"dwin_in{i}") for i in range(SL)]
        zeros_ready, cleared = sem("zeros_ready"), sem("cleared")
        idx_ready, slots_open = sem("idx_ready"), sem("slots_open")
        (zeroed_a, mask_ready, maskT_ps, maskT_ready, dlog_ps, logits_ready, ex_ready, w_ready, wsum_ready,
         block_ps, block_done) = (sem(n) for n in (
             "zeroed_a", "mask_ready", "maskT_ps", "maskT_ready", "dlog_ps", "logits_ready", "ex_ready",
             "w_ready", "wsum_ready", "block_ps", "block_done"))
        block = ctx.enter_context(nc.Block())

        @block.sync
        def _(sp):
            sp.dma_start(src_idx[:, 0:BLOCKS * SUB], g["src"]).then_inc(src_in, 16)
            sp.dma_start(dst_raw[:, 0:BLOCKS * SUB], g["dst"]).then_inc(dst_in, 16)
            sp.wait_ge(zeros_ready, 1)
            sp.dma_start(g["expert_in"][:, :].rearrange("(t p) d -> p t d", p=P), bcast(zeros, 1, MOE_TILES)).then_inc(cleared, 16)
            sp.dma_start(bases[0:1, 0:BLOCKS], g["dst"][0:1, :].rearrange("p (b j) -> p b j", j=SUB)[:, :, 0],
                         allow_slow_non_contiguous=True).then_inc(dst_in, 16)
            sp.wait_ge(dst_in, 32)
            sp.wait_ge(pool_consts, 2)

            def body(n, s):
                base = sp.value_load(bases[0:1, at(n)], min_val=0, max_val=N_PAD)
                sp.wait_ge(mask_ready, n + 1)
                sp.dma_start(dwin[:, s, :], bcast(dst_table[bass.ds(base, WIN), :], 0, SUB)).then_inc(dwin_in[s], 16)
            def run(first, count, extra):
                rounds(sp, Own(sp, None), first, count, SL, 0, body, extra, (0,) * SL)

            def mixed_out(n):
                sp.wait_ge(o_ready, n + 2)
                sp.dma_start(mixed_rows[at(n, P), :], o_row[:, :]).then_inc(o_out, 16)

            def tile_load(n):
                sp.dma_start(ob_in[:, 0, :], mixed_rows[at(n, P), :]).then_inc(tile_in, 16)
                sp.dma_start(ob_in[:, 1, :], base_rows[at(n, P), :]).then_inc(tile_in, 16)

            def base_store(n):
                sp.wait_ge(base_ready, n + 1)
                sp.dma_start(base_rows[at(n, P), :], ob_in[:, 1, :]).then_inc(base_out, 16)

            def stage_1(t, u):
                if u == SL - 1:
                    mixed_out(t)

            def stage_2(t, u):
                if u == SL - 2:
                    base_store(t)
                elif u == SL - 1:
                    sp.wait_ge(base_out, 16 * t + 16)
                    tile_load(t + 1)
            body(0, 0)
            run(1, 1, nothing)
            run(1 + SL, TILES - 1, stage_1)
            run(PAUSE, 1, nothing)
            mixed_out(TILES - 1)
            sp.wait_ge(o_out, 16 * TILES)
            tile_load(0)
            run(PAUSE + SL, 1, nothing)
            run(SECOND, 1, nothing)
            run(SECOND + SL, TILES - 1, stage_2)
            run(THIRD, 1, nothing)
            base_store(TILES - 1)
            repeat(sp, Own(sp, None), THIRD + SL, BLOCKS + 1, SL, 0, body)
            sp.wait_ge(base_out, 16 * TILES)
            for s in range(SL):
                sp.wait_ge(dwin_in[s], 16 * len(range(s, BLOCKS + 1, SL)))
            sp.wait_ge(cleared, 16)

        @block.gpsimd
        def _(pool):
            pool.memset(zeros, 0.0).then_inc(zeros_ready, 1)
            pool.memset(bases[0:1, BLOCKS:BLOCKS + 1], 0).then_inc(pool_consts, 1)
            pool.memset(src_idx[:, BLOCKS * SUB:], 0).then_inc(pool_consts, 1)
            pool.iota(win_i, [[1, WIN]], base=0, channel_multiplier=0).then_inc(pool_consts, 1)
            pool.memset(bm, 1.0).then_inc(own_p, 1)
            pool.wait_ge(own_p, 1)
            pool.affine_select(out=bm, in_=bm, compare_op=ALU.is_ge, fill=0.0, base=0,
                               pattern=[[-WIN, SUB], [0, 8]], channel_multiplier=1).then_inc(own_p, 1)
            pool.wait_ge(own_p, 2)
            pool.affine_select(out=bm, in_=bm, compare_op=ALU.is_ge, fill=0.0, base=WIN - 1,
                               pattern=[[WIN, SUB], [0, 8]], channel_multiplier=-1).then_inc(pool_consts, 1)
            def body(n, s):
                pool.wait_ge(block_ps, n + 1)
                pool.wait_ge(idx_ready, n + 1)
                pool.sem_inc(slots_open, 1)
                for j in range(SUB):
                    pool.indirect_dma_start(
                        out=rows[:, s, j, :], out_offset=None, in_=table[:, :],
                        in_offset=bass.IndirectOffsetOnAxis(ap=idx[:, s * SUB + j:s * SUB + j + 1], axis=0),
                    ).then_inc(gathered[s], 16)
            repeat(pool, Own(pool, None), 0, BLOCKS, SL, 0, body)
            for s in range(SL):
                pool.wait_ge(gathered[s], 64 * len(range(s, BLOCKS, SL)))

        @block.scalar
        def _(act):
            act.memzero(acc[:, DVE_ZERO:g["node_used"][0]]).then_inc(zeroed_a, 1)
            act.wait_ge(src_in, 16)
            act.wait_ge(pool_consts, 2)

            def indices(n, s):
                act.activation(idx[:, s * SUB:(s + 1) * SUB], src_idx[:, at(n, SUB)], ACT.Copy).then_inc(idx_ready, 1)
            indices(0, 0)
            indices(1, 1)

            def mask_copy(n, s):
                act.wait_ge(maskT_ps, n + 1)
                act.activation(maskT[:, s, :], ps_s[s][:, 0:P], ACT.Copy).then_inc(maskT_ready, 1)

            def body(n, s):
                indices(n + 2, (s + 2) % SL)
                act.wait_ge(logits_ready, n + 1)
                act.activation(ex[:, s], lg[:, s], ACT.Exp).then_inc(ex_ready, 1)
                mask_copy(n + 1, (s + 1) % SL)
            def stage_1(t, u):
                if u == 1:
                    act.wait_ge(qT_ps, t + 1)
                    act.activation(qT[:, :], ps_o[:, 0:P], ACT.Copy).then_inc(qT_ready, 1)
            mask_copy(0, 0)
            body(0, 0)
            rounds(act, Own(act, None), 1, TILES, SL, 0, body, stage_1, (0,) * SL)
            act.wait_ge(ss_ready, 1)
            act.activation(s2[:, :], s1[:, :], ACT.Sqrt).then_inc(ss_sqrt, 1)
            repeat(act, Own(act, None), PAUSE, BLOCKS, SL, 0, body)

        @block.tensor
        def _(pe):
            pe.sem_inc(block_ps, SL)
            pe.wait_ge(bases_f_ready, 1)
            pe.matmul(ps_b[:, 0:BLOCKS], ones[0:1, :], bases_f[0:1, :], start=True, stop=True).then_inc(bases_ps, 1)

            def prepare(n, s):
                pe.wait_ge(mask_ready, n + 4)
                pe.transpose(ps_s[s][:, 0:P], mask[:, s].rearrange("p j w -> p (j w)"), ident[:, :]).then_inc(maskT_ps, 1)
                pe.wait_ge(maskT_ready, n + 1)
                pe.matmul(ps_s[s][:, P:P + SUB * 8], maskT[:, s, :], dblk[:, s].rearrange("p j c -> p (j c)"),
                          start=True, stop=True).then_inc(dlog_ps, 1)

            def body(n, s):
                prepare(n + 1, (s + 1) % SL)
                pe.wait_ge(w_ready, n + 1)
                pe.wait_ge(block_done, n + 1)
                for y in range(2):
                    for j in range(SUB):
                        pe.matmul(ps_p[s][:, y * P:(y + 1) * P], rows[:, s, j, y * P:(y + 1) * P], wts[:, s, j, :],
                                  start=j == 0, stop=j == SUB - 1)
                pe.wait_ge(wsum_ready, n + 1)
                pe.matmul(strided(ps_p[s], 2 * P, 192), ones[:, :], wsum[:, s].rearrange("p (a b) -> p a b", a=2),
                          start=True, stop=True).then_inc(block_ps, 1)
            def stage_1(t, u):
                if u == 0:
                    pe.wait_ge(qn_ready, t + 1)
                    pe.wait_ge(o_ready, t + 1)
                    pe.transpose(ps_o[:, 0:P], qn[:, :], ident[:, :]).then_inc(qT_ps, 1)
                elif u == 1:
                    pe.wait_ge(qT_ready, t + 1)
                    pe.matmul(ps_o[:, DIM:2 * DIM], qT[:, :], mmat[:, :], start=True, stop=True).then_inc(o_ps, 1)
            prepare(0, 0)
            body(0, 0)
            rounds(pe, Own(pe, None), 1, TILES, SL, 0, body, stage_1, (0,) * SL)
            repeat(pe, Own(pe, None), PAUSE, BLOCKS, SL, 0, body)
            pe.wait_ge(span_ready, 1)
            pe.matmul(ps_b[0:1, 0:1], badn[:, 0:1], ones[:, 0:1], start=True, stop=True).then_inc(span_ps, 1)

        @block.vector
        def _(dve):
            own = g["dve_steps"]
            own.eng = dve
            dve.sem_inc(block_done, SL)
            dve.sem_inc(mask_ready, SL)
            dve.sem_inc(o_ready, 1)
            own.do(dve.memset(acc[:, 0:DVE_ZERO], 0.0))
            dve.wait_ge(dst_in, 32)
            own.do(dve.tensor_copy(bases_f[0:1, :], bases[0:1, 0:BLOCKS]))
            dve.sem_inc(bases_f_ready, 1)
            dve.wait_ge(pool_consts, 4)
            own.do(dve.tensor_copy(win, win_i))
            own.do(dve.memset(rel[:, BLOCKS * SUB:], -1.0))
            own.do(dve.tensor_copy(rel[:, 0:BLOCKS * SUB], dst_raw[:, 0:BLOCKS * SUB]))
            dve.wait_ge(bases_ps, 1)
            r0 = rel[:, 0:BLOCKS * SUB]
            r3 = r0.rearrange("p (b j) -> p b j", j=SUB)
            own.do(dve.tensor_tensor(r3, r3, bcast(ps_b[:, 0:BLOCKS], 2, SUB), ALU.subtract))

            def prepare(n, s):
                own.do(dve.tensor_tensor(mask[:, s], bcast(rel[:, bass.ds(n * SUB, SUB)], 2, WIN), bcast(win, 1, SUB),
                                         ALU.is_equal))
                dve.wait_ge(dwin_in[s], slot_count(n, s, 16))
                dve.tensor_tensor(dblk[:, s], bm, bcast(dwin[:, s, :], 1, SUB), ALU.mult).then_inc(mask_ready, 1)

            def logits(n, s):
                dve.wait_ge(gathered[s], slot_count(n, s, 64))
                dve.wait_ge(dlog_ps, n + 1)
                d8 = ps_s[s][:, P:P + SUB * 8].rearrange("p (j c) -> p j c", c=8)
                own.do(dve.tensor_tensor(z, rows[:, s, :, DIM:ROW], d8[:, :, 0:4], ALU.add))
                own.do(dve.scalar_tensor_tensor(out=lr, in0=z, scalar=SLOPE, in1=z, op0=ALU.mult, op1=ALU.max))
                dve.tensor_tensor(lg[:, s], lr, d8[:, :, 4:8], ALU.subtract).then_inc(logits_ready, 1)

            def weigh(n, s):
                dve.wait_ge(ex_ready, n + 1)
                for j in range(SUB):
                    m = dve.tensor_tensor(wts[:, s, j, :].rearrange("p (h w) -> p h w", h=G_HEADS),
                                          bcast(mask[:, s, j, :], 1, G_HEADS), bcast(ex[:, s, j, :], 2, WIN), ALU.mult)
                    if j < SUB - 1:
                        own.step(m)
                m.then_inc(w_ready, 1)

            def sum_weights(n, s):
                dve.wait_ge(w_ready, n + 1)
                dve.tensor_reduce(wsum[:, s, :], wts[:, s].rearrange("p j c -> p c j"), AX.X, ALU.add).then_inc(wsum_ready, 1)

            def accumulate(n, s):
                dve.wait_ge(block_ps, n + 1 + SL)
                base = dve.value_load(bases[0:1, at(n)], min_val=0, max_val=N_PAD)
                for half in range(2):
                    r = slice(64 * half, 64 * half + 64)
                    a = acc4[r, bass.ds(base, WIN), :].rearrange("p w c -> p c w")
                    m = dve.tensor_tensor(a, a, quads(ps_p[s], half), ALU.add)
                    if half == 0:
                        own.step(m)
                m.then_inc(block_done, 1)

            def body(n, s):
                logits(n, s)
                prepare(n + 1, (s + 1) % SL)
                weigh(n, s)
                dve.wait_ge(block_done, n - 1 + SL)
                accumulate(n - 1, (s + 2) % SL)
                sum_weights(n, s)
            prepare(0, 0)
            logits(0, 0)
            prepare(1, 1)
            weigh(0, 0)
            sum_weights(0, 0)

            def mix(n):
                dve.wait_ge(o_ps, n + 1)
                if not isinstance(n, int):
                    dve.wait_ge(o_out, n * 16)
                dve.tensor_tensor(o_row[:, :], ps_o[:, DIM:2 * DIM], mix_rows[:, 0, :], ALU.add).then_inc(o_ready, 1)
                dve.wait_ge(o_ready, n + 2)
                own.do(dve.bn_stats(st[:, at(n), :].squeeze(1), o_row[:, :]))

            def queries(n):
                dve.tensor_tensor(qn[:, :].rearrange("p (h d) -> p h d", d=D_HEAD),
                                  q_all[:, at(n), :].squeeze(1).rearrange("p (h d) -> p h d", d=D_HEAD),
                                  bcast(q_inv[:, at(n, M_HEADS)], 2, D_HEAD), ALU.mult).then_inc(qn_ready, 1)

            def first_tile(t, u):
                if u == 0:
                    queries(0)
                elif u == 2:
                    mix(0)

            def stage_1(t, u):
                if u == 0:
                    queries(t + 1)
                elif u == 2:
                    mix(t + 1)

            def stage_2(t, u):
                if u == 0:
                    dve.wait_ge(tile_in, 32 * t + 32)
                    own.do(dve.scalar_tensor_tensor(out=ob_in[:, 0, :], in0=ob_in[:, 0, :], scalar=s1[:, at(t)],
                                                    in1=mix_rows[:, 1, :], op0=ALU.mult, op1=ALU.mult))
                    dve.tensor_tensor(ob_in[:, 1, :], ob_in[:, 1, :], ob_in[:, 0, :], ALU.add).then_inc(base_ready, 1)
            OWN = 2 + 1 + 3 + 1
            dve.wait_ge(zeroed_a, 1)
            rounds(dve, own, 1, 1, SL, OWN, body, first_tile, (0, 0, 1))
            rounds(dve, own, 1 + SL, TILES - 1, SL, OWN, body, stage_1, (0, 0, 1))
            join_moments(dve, own, st, mv, s1)
            own.do(dve.tensor_tensor(s1[:, :], mv[:, :, 0], mv[:, :, 0], ALU.mult))
            own.do(dve.tensor_tensor(s1[:, :], s1[:, :], mv[:, :, 1], ALU.add))
            own.do(dve.tensor_scalar(s1[:, :], s1[:, :], float(DIM), 1e-24, ALU.mult, ALU.max))
            dve.sem_inc(ss_ready, 1)
            repeat(dve, own, PAUSE, SECOND, SL, OWN, body)
            dve.wait_ge(ss_sqrt, 1)
            own.do(dve.reciprocal(s1[:, :], s2[:, :]))
            own.do(dve.tensor_scalar(s1[:, :], s1[:, :], 16.0, None, ALU.mult))
            rounds(dve, own, SECOND, TILES, SL, OWN, body, stage_2, (1, 0, 0))
            repeat(dve, own, THIRD, BLOCKS, SL, OWN, body)
            dve.wait_ge(block_done, BLOCKS - 1 + SL)
            accumulate(BLOCKS - 1, (BLOCKS - 1) % SL)
            b0, c0 = bad[:, 0:BLOCKS * SUB], badc[:, 0:BLOCKS * SUB]
            own.do(dve.tensor_copy(c0, dst_raw[:, 0:BLOCKS * SUB]))
            own.do(dve.tensor_scalar(c0, c0, float(N_NODES), None, ALU.is_lt))
            own.do(dve.scalar_tensor_tensor(out=b0, in0=r0, scalar=float(WIN), in1=c0, op0=ALU.is_ge, op1=ALU.mult))
            own.do(dve.scalar_tensor_tensor(out=c0, in0=r0, scalar=0.0, in1=c0, op0=ALU.is_lt, op1=ALU.mult))
            own.do(dve.tensor_tensor_reduce(b0, b0, c0, 1.0, 0.0, ALU.add, ALU.add, badn[:, 0:1]))
            dve.sem_inc(span_ready, 1)
            dve.wait_ge(span_ps, 1)
            own.do(dve.tensor_copy(spans[0:1, 0:1], ps_b[0:1, 0:1]))


def any_order_stage(nc, g):
    e = g["edge_buffers"]
    acc, ident, ones, spans = (g[k] for k in ("acc", "ident", "ones", "spans"))
    table, dst_table = g["table"], g["dst_table"]
    src_idx, idx, dst_raw, rel, rows, mask, maskT, dwin, dblk, wts, wsum, lg, ex, z, lr, win, bm = (e[k] for k in (
        "src_idx", "idx", "dst_raw", "rel", "rows", "mask", "maskT", "dwin", "dblk", "wts", "wsum", "lg", "ex",
        "z", "lr", "win", "bm"))
    acc4 = acc[:, :].rearrange("p (w c) -> p w c", c=4)

    with ExitStack() as ctx:
        ps_p = ctx.enter_context(nc.psum_tensor("ps_ap", [P, 512], F32))
        ps_s = ctx.enter_context(nc.psum_tensor("ps_as", [P, 512], F32))
        (own_v, zeroed, indexed, slots_open, gathered, windowed, masked, mask_ps, mask_back, dlog_ps, lg_ready,
         ex_ready, w_ready, sum_ps, summed, shifted) = (ctx.enter_context(nc.semaphore("any_" + n)) for n in (
             "own_v", "zeroed", "indexed", "slots_open", "gathered", "windowed", "masked", "mask_ps", "mask_back",
             "dlog_ps", "lg_ready", "ex_ready", "w_ready", "sum_ps", "summed", "shifted"))
        block = ctx.enter_context(nc.Block())

        def steps(eng, body):
            outside = eng.value_load(spans[0:1, 0:1], min_val=0, max_val=N_EDGES)
            with eng.If(outside > 0):
                if eng is nc.vector or eng is nc.scalar:
                    body(None, None, None)
                with eng.Fori(0, WINDOWS) as v:
                    if eng is nc.vector:
                        body(None, v, None)
                    with eng.Fori(0, BLOCKS) as n:
                        body(v * BLOCKS + n, v, n)

        @block.sync
        def _(sp):
            def body(m, v, n):
                sp.wait_ge(summed, m + 1)
                sp.dma_start(dwin[:, 0, :], bcast(dst_table[at(v, WIN), :], 0, SUB)).then_inc(windowed, 16)
            steps(sp, body)

        @block.gpsimd
        def _(pool):
            def body(m, v, n):
                pool.wait_ge(indexed, m + 1)
                pool.sem_inc(slots_open, 1)
                for j in range(SUB):
                    pool.indirect_dma_start(
                        out=rows[:, 0, j, :], out_offset=None, in_=table[:, :],
                        in_offset=bass.IndirectOffsetOnAxis(ap=idx[:, j:j + 1], axis=0)).then_inc(gathered, 16)
            steps(pool, body)

        @block.scalar
        def _(act):
            def body(m, v, n):
                if m is None:
                    act.memzero(acc[:, ACC_W * 2:]).then_inc(zeroed, 1)
                    return
                act.wait_ge(summed, m + 1)
                act.activation(idx[:, 0:SUB], src_idx[:, at(n, SUB)], ACT.Copy).then_inc(indexed, 1)
                act.wait_ge(mask_ps, m + 1)
                act.activation(maskT[:, 0, :], ps_s[:, 0:P], ACT.Copy).then_inc(mask_back, 1)
                act.wait_ge(lg_ready, m + 1)
                act.activation(ex[:, 0], lg[:, 0], ACT.Exp).then_inc(ex_ready, 1)
            steps(act, body)

        @block.tensor
        def _(pe):
            def body(m, v, n):
                pe.wait_ge(masked, m + 1)
                pe.transpose(ps_s[:, 0:P], mask[:, 0].rearrange("p j w -> p (j w)"), ident[:, :]).then_inc(mask_ps, 1)
                pe.wait_ge(mask_back, m + 1)
                pe.matmul(ps_s[:, P:P + SUB * 8], maskT[:, 0, :], dblk[:, 0].rearrange("p j c -> p (j c)"),
                          start=True, stop=True).then_inc(dlog_ps, 1)
                pe.wait_ge(w_ready, m + 1)
                for y in range(2):
                    for j in range(SUB):
                        pe.matmul(ps_p[:, y * P:(y + 1) * P], rows[:, 0, j, y * P:(y + 1) * P], wts[:, 0, j, :],
                                  start=j == 0, stop=j == SUB - 1)
                pe.matmul(strided(ps_p, 2 * P, 192), ones[:, :], wsum[:, 0].rearrange("p (a b) -> p a b", a=2),
                          start=True, stop=True).then_inc(sum_ps, 1)
            steps(pe, body)

        @block.vector
        def _(dve):
            own = Own(dve, own_v)
            OWN = 1 + 2 + SUB + 1

            def body(m, v, n):
                if v is None:
                    dve.sem_inc(summed, 1)
                    own.do(dve.tensor_scalar(win, win, float(-WIN), None, ALU.add))
                    own.do(dve.tensor_copy(rel[:, 0:BLOCKS * SUB], dst_raw[:, 0:BLOCKS * SUB]))
                    own.do(dve.memset(acc[:, 0:ACC_W * 2], 0.0))
                    dve.wait_ge(zeroed, 1)
                    own.start = own.k
                    return
                if n is None:
                    own.base, own.k = own.start + v * (BLOCKS * OWN + 1), 0
                    own.do(dve.tensor_scalar(win, win, float(WIN), None, ALU.add))
                    own.inner = own.base + 1
                    dve.sem_inc(shifted, 1)
                    return
                own.base, own.k = own.inner + n * OWN, 0
                own.do(dve.tensor_tensor(mask[:, 0], bcast(rel[:, bass.ds(n * SUB, SUB)], 2, WIN), bcast(win, 1, SUB),
                                         ALU.is_equal))
                dve.wait_ge(windowed, m * 16 + 16)
                dve.tensor_tensor(dblk[:, 0], bm, bcast(dwin[:, 0, :], 1, SUB), ALU.mult).then_inc(masked, 1)
                dve.wait_ge(gathered, m * 64 + 64)
                dve.wait_ge(dlog_ps, m + 1)
                d8 = ps_s[:, P:P + SUB * 8].rearrange("p (j c) -> p j c", c=8)
                own.do(dve.tensor_tensor(z, rows[:, 0, :, DIM:ROW], d8[:, :, 0:4], ALU.add))
                own.do(dve.scalar_tensor_tensor(out=lr, in0=z, scalar=SLOPE, in1=z, op0=ALU.mult, op1=ALU.max))
                dve.tensor_tensor(lg[:, 0], lr, d8[:, :, 4:8], ALU.subtract).then_inc(lg_ready, 1)
                dve.wait_ge(ex_ready, m + 1)
                for j in range(SUB):
                    own.step(dve.tensor_tensor(wts[:, 0, j, :].rearrange("p (h w) -> p h w", h=G_HEADS),
                                               bcast(mask[:, 0, j, :], 1, G_HEADS), bcast(ex[:, 0, j, :], 2, WIN), ALU.mult))
                own.wait()
                dve.tensor_reduce(wsum[:, 0, :], wts[:, 0].rearrange("p j c -> p c j"), AX.X, ALU.add).then_inc(w_ready, 1)
                dve.wait_ge(sum_ps, m + 1)
                for half in range(2):
                    a = acc4[64 * half:64 * half + 64, at(v, WIN), :].rearrange("p w c -> p c w")
                    ins = dve.tensor_tensor(a, a, quads(ps_p, half), ALU.add)
                    if half == 0:
                        own.step(ins)
                ins.then_inc(summed, 1)
                assert own.k == OWN, own.k
            steps(dve, body)


def slot_count(n, s, inc, slots=3):
    return (n - s + slots) * inc // slots


def strided(ps, start, step):
    v = ps[:, start:start + 64]
    return bass.AP(v.tensor, v.offset, [list(v.ap[0]), [step, 2], [1, 64]])


def quads(ps, half):
    v = ps[64 * half:64 * half + 64, 32 * half:32 * half + 32]
    return bass.AP(v.tensor, v.offset, [list(v.ap[0]), [256, 2], [192, 2], [1, 32]])


def rows_stage(nc, g):
    acc, ident, valid, w_self, region = (g[k] for k in ("acc", "ident", "valid", "w_self", "region"))
    table, base_rows = g["table"], g["base_rows"]
    acc4 = acc[:, :].rearrange("p (w c) -> p w c", c=4)
    w1_sb, w2_sb, b2_sb, logits, wr = (g[k] for k in ("w1_sb", "w2_sb", "b2_sb", "logits", "wr"))

    with ExitStack() as ctx:
        def sb(name, shape, dt=F32):
            return ctx.enter_context(nc.sbuf_tensor(name, shape, dt))

        def sem(name):
            return ctx.enter_context(nc.semaphore(name))

        planes = sb("planes", [P, 2, 4, P])
        h_in = sb("h_in", [P, 2, DIM])
        b_in = sb("b_in", [P, 2, DIM])
        rl = sb("rl", [P, 2, G_HEADS])
        tmp = sb("tmpr", [P, DIM])
        tmpx = sb("tmpx", [P, 2, DIM])
        lnrows = sb("lnrows", [P, 2, DIM])
        brow = sb("brow", [P, EXPERTS])
        st = sb("st2", [P, TILES, 6])
        mv = sb("mv2", [P, TILES, 2])
        s1, s2, s3 = sb("r1", [P, TILES]), sb("r2", [P, TILES]), sb("r3", [P, TILES])
        eps = sb("eps2", [P, 1])
        xT = sb("xT", [P, 2, DIM])
        ps_t = [ctx.enter_context(nc.psum_tensor(f"ps_r{i}", [P, 512], F32)) for i in range(2)]
        ps_x = ctx.enter_context(nc.psum_tensor("ps_rx", [P, 2, DIM], F32))
        ps_l = [ctx.enter_context(nc.psum_tensor(f"ps_rl{i}", [P, 512], F32)) for i in range(2)]

        loads = sem("loads2")
        weights_in = g["weights_in"]
        row_in = [sem(f"row_in{i}") for i in range(2)]
        planes_ready, planes_ps, x1_ready, var_ready, dev_ready, scale_ready = (sem(n) for n in (
            "planes_ready", "planes_ps", "x1_ready", "var_ready", "dev_ready", "scale_ready"))
        n_ready, f_ready, f_ps, fT_ready, l_ps, l_ready = (sem(n) for n in (
            "n_ready", "f_ready", "f_ps", "fT_ready", "l_ps", "l_ready"))
        block = ctx.enter_context(nc.Block())

        def x1_of(n):
            return acc[:, bass.ds(n * 4 * P + DIM, DIM)]

        def xn_of(n):
            return acc[:, bass.ds(n * 4 * P, DIM)]

        @block.sync
        def _(sp):
            def body(n, s):
                sp.wait_ge(x1_ready, n + 1)
                sp.dma_start(h_in[:, s, :], table[at(n, P), 0:DIM]).then_inc(row_in[s], 16)
                sp.dma_start(b_in[:, s, :], base_rows[at(n, P), :]).then_inc(row_in[s], 16)
            for_sp(sp, TILES, body)

        @block.gpsimd
        def _(pool):
            def body(n, s):
                pool.wait_ge(planes_ps, n + 1)
                pool.tensor_copy(planes[:, s], acc4[:, at(n, P), :].rearrange("p w c -> p c w")).then_inc(planes_ready, 1)
            repeat(pool, Own(pool, None), 0, TILES, 2, 0, body)

        @block.scalar
        def _(act):
            act.dma_start(lnrows[:, 0, :], g["gamma"].partition_broadcast(P)).then_inc(loads, 16)
            act.dma_start(lnrows[:, 1, :], g["beta"].partition_broadcast(P)).then_inc(loads, 16)
            act.dma_start(brow[:, :], g["br"].partition_broadcast(P)).then_inc(loads, 16)
            act.dma_start(wr[:, :].rearrange("p (c e) -> p c e", e=EXPERTS),
                          g["Wr"].rearrange("(c p) e -> p c e", p=P)).then_inc(loads, 16)
            act.dma_start(b2_sb, g["b2"].rearrange("e f -> (e f)").partition_broadcast(P)).then_inc(weights_in, 16)
            for e in range(EXPERTS):
                act.dma_start(w1_sb[:, e], g["W1"][e].rearrange("(c p) f -> p c f", p=P)).then_inc(weights_in, 16)
                act.dma_start(w2_sb[:, e], g["W2"][e].rearrange("(c p) d -> p c d", p=P)).then_inc(weights_in, 16)
            for i in range(2):
                act.wait_ge(var_ready, i + 1)
                act.activation(s2[:, :], s1[:, :], ACT.Sqrt, bias=eps[:, 0:1]).then_inc(dev_ready, 1)
            act.wait_ge(scale_ready, 1)

            def body(n, s):
                act.activation(xn_of(n), x1_of(n), ACT.Identity, bias=s2[:, at(n)], scale=s1[:, at(n)]).then_inc(n_ready, 1)

            def copy(n, s):
                act.wait_ge(f_ps, n + 1)
                act.activation(xT[:, s, :], ps_x[:, s, :], ACT.Copy).then_inc(fT_ready, 1)
            body(0, 0)

            def both(n, s):
                body(n, s)
                copy(n - 1, 1 - s)
            repeat(act, Own(act, None), 1, TILES, 2, 0, both)
            copy(TILES - 1, 0)

        @block.tensor
        def _(pe):
            pe.sem_inc(planes_ps, 2)

            def body(n, s):
                pe.wait_ge(planes_ready, n + 1)
                pe.wait_ge(x1_ready, n + 1)
                for c in range(4):
                    m = pe.transpose(ps_t[s][:, c * P:(c + 1) * P], planes[:, s, c, :], ident[:, :])
                m.then_inc(planes_ps, 1)
            repeat(pe, Own(pe, None), 0, TILES, 2, 0, body)
            pe.wait_ge(loads, 64)

            def route(n, s):
                pe.wait_ge(f_ready, n + 1)
                for c in range(KC):
                    m = pe.transpose(ps_x[:, s, c * P:(c + 1) * P], tmpx[:, s, c * P:(c + 1) * P], ident[:, :])
                m.then_inc(f_ps, 1)
                pe.wait_ge(fT_ready, n + 1)
                pe.wait_ge(l_ready, n + 1)
                for c in range(KC):
                    m = pe.matmul(ps_l[s][:, 0:EXPERTS], xT[:, s, c * P:(c + 1) * P], wr[:, c * EXPERTS:(c + 1) * EXPERTS],
                                  start=c == 0, stop=c == KC - 1)
                m.then_inc(l_ps, 1)
            repeat(pe, Own(pe, None), 0, TILES, 2, 0, route)

        @block.vector
        def _(dve):
            own = g["dve_steps"]
            own.eng = dve
            dve.sem_inc(x1_ready, 2)
            dve.sem_inc(l_ready, 2)
            own.do(dve.memset(eps[:, :], LN_EPS))

            def heads(ap):
                return ap.rearrange("p (h f) -> p h f", f=F_HEAD)

            def body(n, s):
                dve.wait_ge(planes_ps, n + 3)
                ws = w_self[:, at(n, G_HEADS)]
                l4 = heads(ps_t[s][:, DIM:2 * DIM])[:, :, 0]
                own.do(dve.tensor_tensor(rl[:, s, :], l4, ws, ALU.add))
                own.do(dve.reciprocal(rl[:, s, :], rl[:, s, :]))
                dve.wait_ge(row_in[s], slot_count(n, s, 32, 2))
                own.do(dve.tensor_tensor(heads(h_in[:, s, :]), heads(h_in[:, s, :]), bcast(ws, 2, F_HEAD), ALU.mult))
                own.do(dve.tensor_tensor(tmp[:, :], h_in[:, s, :], ps_t[s][:, 0:DIM], ALU.add))
                own.do(dve.tensor_tensor(heads(tmp[:, :]), heads(tmp[:, :]), bcast(rl[:, s, :], 2, F_HEAD), ALU.mult))
                own.do(dve.tensor_tensor(x1_of(n), tmp[:, :], b_in[:, s, :], ALU.add))
                dve.bn_stats(st[:, at(n), :].squeeze(1), x1_of(n)).then_inc(x1_ready, 1)
            repeat(dve, own, 0, TILES, 2, 6, body)
            dve.wait_ge(x1_ready, TILES + 2)
            join_moments(dve, own, st, mv, s1)
            own.do(dve.tensor_copy(s1[:, :], mv[:, :, 1]))
            dve.sem_inc(var_ready, 1)
            dve.wait_ge(dev_ready, 1)
            own.do(dve.reciprocal(s3[:, :], s2[:, :]))
            own.do(dve.tensor_tensor(s1[:, :], s1[:, :], s3[:, :], ALU.mult))
            own.do(dve.tensor_tensor(s1[:, :], s1[:, :], s3[:, :], ALU.mult))
            dve.sem_inc(var_ready, 1)
            dve.wait_ge(dev_ready, 2)
            own.do(dve.reciprocal(s2[:, :], s2[:, :]))
            own.do(dve.tensor_tensor(s1[:, :], s2[:, :], s3[:, :], ALU.mult))
            own.do(dve.scalar_tensor_tensor(out=s2[:, :], in0=mv[:, :, 0], scalar=-1.0, in1=s1[:, :],
                                            op0=ALU.mult, op1=ALU.mult))
            dve.sem_inc(scale_ready, 1)
            dve.wait_ge(loads, 64)

            def route(n, s):
                dve.wait_ge(n_ready, n + 1)
                own.do(dve.tensor_tensor(tmp[:, :], xn_of(n), lnrows[:, 0, :], ALU.mult))
                own.do(dve.tensor_tensor(tmpx[:, s, :], tmp[:, :], lnrows[:, 1, :], ALU.add))
                dve.tensor_tensor(xn_of(n), tmp[:, :], lnrows[:, 1, :], ALU.add).then_inc(f_ready, 1)
                dve.wait_ge(f_ready, n + 1)

            def take(n, s):
                dve.wait_ge(l_ps, n + 1)
                dve.tensor_tensor(logits[:, at(n, EXPERTS)], ps_l[s][:, 0:EXPERTS], brow[:, :], ALU.add).then_inc(l_ready, 1)
            route(0, 0)

            def both(n, s):
                route(n, s)
                take(n - 1, 1 - s)
            repeat(dve, own, 1, TILES, 2, 2, both)
            take(TILES - 1, 0)


def route_stage(nc, g):
    acc, ident, ones, valid, logits = (g[k] for k in ("acc", "ident", "ones", "valid", "logits"))
    place, gate, tile_expert, expert_in = g["place"], g["gate"], g["tile_expert"], g["expert_in"]
    TE = TILES * EXPERTS

    with ExitStack() as ctx:
        def sb(name, shape, dt=F32):
            return ctx.enter_context(nc.sbuf_tensor(name, shape, dt))

        def sem(name):
            return ctx.enter_context(nc.semaphore(name))

        def te(name):
            return sb(name, [P, TE])[:, :].rearrange("p (t e) -> p t e", e=EXPERTS)

        before = sb("before", [P, P])
        rank_i, rank = sb("rank_i", [P, EXPERTS], I32), sb("rank", [P, EXPERTS])
        tau_i, tau = sb("tau_i", [1, MOE_TILES], I32), sb("tau", [1, MOE_TILES])
        le = sb("le", [1, MOE_TILES * EXPERTS])
        tmpf = sb("tmpf", [P, TE])
        work = tmpf[:, :].rearrange("p (t e) -> p t e", e=EXPERTS)
        first, second, both = te("first"), te("second"), te("both_")
        pos = te("pos")
        top = sb("top", [P, 2, TILES])
        t1 = sb("t1", [P, TILES])
        cnt = sb("cnt", [P, 4, EXPERTS])
        cnt_i = sb("cnt_i", [P, EXPERTS], I32)
        ps_pos = ctx.enter_context(nc.psum_tensor("ps_pos", [P, 512], F32))
        ps_tot = ctx.enter_context(nc.psum_tensor("ps_tot", [P, 512], F32))
        own_p, consts, picked, counted, exp_in, exp_out, placed = (sem(n) for n in (
            "own_p5", "consts5", "picked", "counted", "exp_in5", "exp_out5", "placed"))
        sent = sem("sent")
        block = ctx.enter_context(nc.Block())

        @block.gpsimd
        def _(pool):
            pool.memset(before[:, :], 1.0).then_inc(own_p, 1)
            pool.iota(rank_i[:, :], [[-1, EXPERTS]], base=EXPERTS, channel_multiplier=0).then_inc(consts, 1)
            pool.iota(tau_i[:, :], [[1, MOE_TILES]], base=0, channel_multiplier=0).then_inc(consts, 1)
            pool.wait_ge(own_p, 1)
            pool.affine_select(out=before[:, :], in_=before[:, :], compare_op=ALU.is_gt, fill=0.0, base=0,
                               pattern=[[1, P]], channel_multiplier=-1).then_inc(consts, 1)
            pool.wait_ge(placed, 1)
            for n in range(TILES):
                r = P if n < TILES - 1 else LAST
                for k in range(2):
                    pool.indirect_dma_start(
                        out=expert_in[:, :], out_offset=bass.IndirectOffsetOnAxis(ap=place[0:r, k * TILES + n:k * TILES + n + 1], axis=0),
                        in_=acc[0:r, n * 4 * P:n * 4 * P + DIM], in_offset=None).then_inc(sent, 16)
            pool.wait_ge(sent, 16 * 2 * TILES)

        @block.scalar
        def _(act):
            act.wait_ge(exp_in, 1)
            act.activation(t1[:, :], t1[:, :], ACT.Exp).then_inc(exp_out, 1)

        @block.tensor
        def _(pe):
            pe.wait_ge(picked, 1)
            pe.matmul(ps_pos[:, 0:TE], before[:, :], both.rearrange("p t e -> p (t e)"), start=True, stop=True)
            pe.matmul(ps_tot[:, 0:TE], ones[:, :], both.rearrange("p t e -> p (t e)"), start=True, stop=True).then_inc(counted, 1)

        @block.vector
        def _(dve):
            own = g["dve_steps"]
            own.eng = dve
            lg = logits[:, :].rearrange("p (t e) -> p t e", e=EXPERTS)
            dve.wait_ge(consts, 3)
            own.do(dve.tensor_copy(rank[:, :], rank_i[:, :]))
            own.do(dve.tensor_copy(tau[:, :], tau_i[:, :]))

            def pick(values, k, onehot):
                own.do(dve.tensor_reduce(top[:, k, :], values, AX.X, ALU.max))
                own.do(dve.tensor_tensor(work, values, bcast(top[:, k, :], 2, EXPERTS), ALU.is_equal))
                own.do(dve.tensor_tensor(work, work, bcast(rank[:, :], 1, TILES), ALU.mult))
                own.do(dve.tensor_reduce(t1[:, :], work, AX.X, ALU.max))
                own.do(dve.tensor_tensor(onehot, bcast(rank[:, :], 1, TILES), bcast(t1[:, :], 2, EXPERTS), ALU.is_equal))
            pick(lg, 0, first)
            own.do(dve.scalar_tensor_tensor(out=pos, in0=first, scalar=-3e38, in1=lg, op0=ALU.mult, op1=ALU.add))
            pick(pos, 1, second)
            own.do(dve.tensor_tensor(both, first, second, ALU.add))
            own.do(dve.tensor_tensor(both, both, bcast(valid[:, :], 2, EXPERTS), ALU.mult))
            dve.sem_inc(picked, 1)
            own.do(dve.tensor_tensor(t1[:, :], top[:, 1, :], top[:, 0, :], ALU.subtract))
            dve.sem_inc(exp_in, 1)
            dve.wait_ge(counted, 1)
            tot = ps_tot[:, 0:TE].rearrange("p (t e) -> p t e", e=EXPERTS)
            own.do(dve.memset(work, 1.0))
            for e in range(EXPERTS):
                own.step(dve.tensor_tensor_scan(pos[:, :, e], work[:, :, e], tot[:, :, e], 0.0, ALU.mult, ALU.add))
            own.wait()
            own.do(dve.tensor_scalar(cnt_i[:, :], pos[:, TILES - 1, :], float(P - 1), None, ALU.add))
            own.do(dve.tensor_scalar(cnt_i[:, :], cnt_i[:, :], P.bit_length() - 1, None, ALU.arith_shift_right))
            own.do(dve.tensor_copy(cnt[:, 0, :], cnt_i[:, :]))
            own.do(dve.tensor_tensor_scan(cnt[:, 1, :], work[:, 0, :], cnt[:, 0, :], 0.0, ALU.mult, ALU.add))
            own.do(dve.tensor_tensor(cnt[:, 2, :], cnt[:, 1, :], cnt[:, 0, :], ALU.subtract))
            own.do(dve.tensor_scalar(cnt[:, 2, :], cnt[:, 2, :], float(P), None, ALU.mult))
            own.do(dve.tensor_tensor(pos, pos, tot, ALU.subtract))
            own.do(dve.tensor_tensor(pos, pos, ps_pos[:, 0:TE].rearrange("p (t e) -> p t e", e=EXPERTS), ALU.add))
            own.do(dve.tensor_tensor(pos, pos, bcast(cnt[:, 2, :], 1, TILES), ALU.add))
            for k, oh in enumerate((first, second)):
                own.do(dve.tensor_tensor(work, oh, pos, ALU.mult))
                own.do(dve.tensor_reduce(top[:, k, :], work, AX.X, ALU.add))
                own.do(dve.tensor_copy(place[:, k * TILES:(k + 1) * TILES], top[:, k, :]))
            dve.sem_inc(placed, 1)
            dve.wait_ge(exp_out, 1)
            own.do(dve.tensor_scalar(top[:, 0, :], t1[:, :], 1.0, None, ALU.add))
            own.do(dve.reciprocal(gate[:, 0:TILES], top[:, 0, :]))
            own.do(dve.tensor_tensor(gate[:, TILES:2 * TILES], gate[:, 0:TILES], t1[:, :], ALU.mult))
            l3 = le[:, :].rearrange("p (t e) -> p t e", e=EXPERTS)
            own.do(dve.tensor_tensor(l3, bcast(cnt[0:1, 1, :], 1, MOE_TILES), bcast(tau[:, :], 2, EXPERTS), ALU.is_le))
            own.do(dve.tensor_reduce(tau[:, :], l3, AX.X, ALU.add))
            own.do(dve.tensor_scalar(tile_expert[0:1, :], tau[:, :], float(EXPERTS - 1), None, ALU.min))


def expert_stage(nc, g):
    acc, ident = g["acc"], g["ident"]
    w1_sb, w2_sb, b2_sb, weights_in = (g[k] for k in ("w1_sb", "w2_sb", "b2_sb", "weights_in"))
    b1_sb = acc[:, 0:EXPERTS * 8 * P].rearrange("p (e c f) -> p e c f", e=EXPERTS, f=2 * DIM)[:, :, :, 0:DIM]
    place, gate, tile_expert = g["place"], g["gate"], g["tile_expert"]
    expert_in, expert_out, out = g["expert_in"], g["expert_out"], g["out"]
    T = MOE_TILES
    XS = 4

    with ExitStack() as ctx:
        def sb(name, shape, dt=F32):
            return ctx.enter_context(nc.sbuf_tensor(name, shape, dt))

        def sem(name):
            return ctx.enter_context(nc.semaphore(name))

        xe = sb("xe", [P, XS, DIM])
        xeT = sb("xeT", [P, 2, DIM])
        hid = sb("hid", [P, 2, FF])
        hidT = sb("hidT", [P, 2, FF])
        ye = g["ye_sb"].rearrange("p (s d) -> p s d", s=2)
        ps_x = [ctx.enter_context(nc.psum_tensor(f"ps_ex{i}", [P, 512], F32)) for i in range(2)]
        ps_y = [ctx.enter_context(nc.psum_tensor(f"ps_ey{i}", [P, 512], F32)) for i in range(2)]
        ps_u = [ctx.enter_context(nc.psum_tensor(f"ps_eu{i}", [P, FF], F32)) for i in range(2)]
        ps_g = [ctx.enter_context(nc.psum_tensor(f"ps_eg{i}", [P, FF], F32)) for i in range(2)]
        b1_in = sem("b1_in")
        xe_in = [sem(f"xe_in{i}") for i in range(XS)]
        ye_out = [sem(f"ye_out{i}") for i in range(2)]
        xe_ps, xeT_ready, up_ps, biased, hid_ready, hid_ps, hidT_ready, down_ps, ye_ready = (sem(n) for n in (
            "xe_ps", "xeT_ready", "up_ps", "biased", "hid_ready", "hid_ps", "hidT_ready", "down_ps", "ye_ready"))
        block = ctx.enter_context(nc.Block())

        @block.sync
        def _(sp):
            def body(n, s):
                sp.wait_ge(xe_ps, n + 1)
                sp.dma_start(xe[:, s, :], expert_in[at(n, P), :]).then_inc(xe_in[s], 16)
            repeat(sp, Own(sp, None), 0, T, XS, 0, body)

        @block.scalar
        def _(act):
            for e in range(EXPERTS):
                act.dma_start(b1_sb[:, e], g["b1"][e].rearrange("(c f) -> c f", c=2).partition_broadcast(P)).then_inc(
                    b1_in, 16)

            def rows_back(n, s):
                act.wait_ge(xe_ps, n + 1 + XS)
                act.activation(xeT[:, s, :], ps_x[s][:, 0:DIM], ACT.Copy).then_inc(xeT_ready, 1)

            def gelu(n, s):
                act.wait_ge(biased, n + 1)
                act.activation(hid[:, s, :], hid[:, s, :], ACT.Gelu).then_inc(hid_ready, 1)
            def store(n, s):
                act.wait_ge(ye_ready, n + 1)
                act.dma_start(expert_out[at(n, P), :], ye[:, s, :]).then_inc(ye_out[s], 16)
            rows_back(0, 0)
            for n in range(1, 4):
                rows_back(n, n % 2)
                gelu(n - 1, (n - 1) % 2)

            def body(n, s):
                rows_back(n, s)
                gelu(n - 1, 1 - s)
                store(n - 4, s)
            repeat(act, Own(act, None), 4, T, 2, 0, body)
            gelu(T - 1, (T - 1) % 2)
            for n in range(T - 4, T):
                store(n, n % 2)
            for s in range(2):
                act.wait_ge(ye_out[s], 16 * len(range(s, T, 2)))

        @block.tensor
        def _(pe):
            pe.sem_inc(xe_ps, XS)

            def rows_across(n, s):
                pe.wait_ge(xe_in[s], slot_count(n, s, 16, XS))
                if not isinstance(n, int) or n >= 2:
                    pe.wait_ge(xeT_ready, n - 1)
                for c in range(KC):
                    m = pe.transpose(ps_x[s % 2][:, c * P:(c + 1) * P], xe[:, s, c * P:(c + 1) * P], ident[:, :])
                m.then_inc(xe_ps, 1)

            def up(n, s):
                e = pe.value_load(tile_expert[0:1, at(n)], min_val=0, max_val=EXPERTS - 1)
                pe.wait_ge(xeT_ready, n + 1)
                for c in range(KC):
                    m = pe.matmul(ps_u[s][:, :], xeT[:, s, c * P:(c + 1) * P], w1_sb[:, at(e), c, :].squeeze(1),
                                  start=c == 0, stop=c == KC - 1)
                m.then_inc(up_ps, 1)

            def hidden_across(n, s):
                pe.wait_ge(hid_ready, n + 1)
                for c in range(FC):
                    m = pe.transpose(ps_g[s][:, c * P:(c + 1) * P], hid[:, s, c * P:(c + 1) * P], ident[:, :])
                m.then_inc(hid_ps, 1)

            def down(n, s):
                e = pe.value_load(tile_expert[0:1, at(n)], min_val=0, max_val=EXPERTS - 1)
                pe.wait_ge(hidT_ready, n + 1)
                if not isinstance(n, int) or n >= 2:
                    pe.wait_ge(ye_ready, n - 1)
                for c in range(FC):
                    m = pe.matmul(ps_y[s][:, 0:DIM], hidT[:, s, c * P:(c + 1) * P], w2_sb[:, at(e), c, :].squeeze(1),
                                  start=c == 0, stop=c == FC - 1)
                m.then_inc(down_ps, 1)

            rows_across(0, 0)
            pe.wait_ge(weights_in, 16 * (1 + 2 * EXPERTS))
            rows_across(1, 1)
            up(0, 0)
            rows_across(2, 2)
            up(1, 1)
            hidden_across(0, 0)

            def body(n, s):
                rows_across(n, s)
                up(n - 1, (s + 1) % 2)
                hidden_across(n - 2, s % 2)
                down(n - 3, (s + 1) % 2)
            body(3, 3)
            body(4, 0)
            repeat(pe, Own(pe, None), 5, T, XS, 0, body)
            up(T - 1, (T - 1) % 2)
            hidden_across(T - 2, (T - 2) % 2)
            down(T - 3, (T - 3) % 2)
            hidden_across(T - 1, (T - 1) % 2)
            down(T - 2, (T - 2) % 2)
            down(T - 1, (T - 1) % 2)

        @block.vector
        def _(dve):
            dve.wait_ge(weights_in, 16 * (1 + 2 * EXPERTS))
            dve.wait_ge(b1_in, 16 * EXPERTS)

            def bias(n, s):
                dve.wait_ge(up_ps, n + 1)
                if not isinstance(n, int) or n >= 2:
                    dve.wait_ge(hid_ps, n - 1)
                e = dve.value_load(tile_expert[0:1, at(n)], min_val=0, max_val=EXPERTS - 1)
                dve.tensor_tensor(hid[:, s, :].rearrange("p (c f) -> p c f", c=2),
                                  ps_u[s][:, :].rearrange("p (c f) -> p c f", c=2), b1_sb[:, at(e)].squeeze(1),
                                  ALU.add).then_inc(biased, 1)

            def hidden(n, s):
                dve.wait_ge(hid_ps, n + 1)
                dve.tensor_copy(hidT[:, s, :], ps_g[s][:, :]).then_inc(hidT_ready, 1)

            def result(n, s):
                dve.wait_ge(down_ps, n + 1)
                e = dve.value_load(tile_expert[0:1, at(n)], min_val=0, max_val=EXPERTS - 1)
                if not isinstance(n, int) or n >= 2:
                    dve.wait_ge(ye_out[s], slot_count(n - 2, s, 16, 2))
                dve.tensor_tensor(ye[:, s, :], ps_y[s][:, 0:DIM], b2_sb[:, at(e, DIM)], ALU.add).then_inc(ye_ready, 1)
            bias(0, 0)
            bias(1, 1)
            hidden(0, 0)
            bias(2, 0)
            hidden(1, 1)
            result(0, 0)

            def body(n, s):
                bias(n, s)
                hidden(n - 1, 1 - s)
                result(n - 2, s)
            repeat(dve, Own(dve, None), 3, T, 2, 0, body)
            hidden(T - 1, (T - 1) % 2)
            result(T - 2, (T - 2) % 2)
            result(T - 1, (T - 1) % 2)

    CS = 4
    with ExitStack() as ctx:
        y = ctx.enter_context(nc.sbuf_tensor("y", [P, CS, 2, DIM], F32))
        got = [ctx.enter_context(nc.semaphore(f"got{i}")) for i in range(CS)]
        stored = [ctx.enter_context(nc.semaphore(f"stored{i}")) for i in range(CS)]
        summed = ctx.enter_context(nc.semaphore("summed"))
        block = ctx.enter_context(nc.Block())

        @block.gpsimd
        def _(pool):
            for n in range(TILES):
                r, s = P if n < TILES - 1 else LAST, n % CS
                if n >= CS:
                    pool.wait_ge(stored[s], 16 * (n // CS))
                for k in range(2):
                    pool.indirect_dma_start(
                        out=y[0:r, s, k, :], out_offset=None, in_=expert_out[:, :],
                        in_offset=bass.IndirectOffsetOnAxis(ap=place[0:r, k * TILES + n:k * TILES + n + 1], axis=0),
                    ).then_inc(got[s], 16)

        @block.vector
        def _(dve):
            own = g["dve_steps"]
            own.eng = dve

            def combine(n, s, r):
                dve.wait_ge(got[s], slot_count(n, s, 32, CS))
                for k in range(2):
                    prev = acc[0:r, bass.ds(n * 4 * P + DIM, DIM)] if k == 0 else y[0:r, s, 0, :]
                    m = dve.scalar_tensor_tensor(out=y[0:r, s, 0, :], in0=y[0:r, s, k, :],
                                                 scalar=gate[0:r, bass.ds(n + k * TILES, 1)], in1=prev,
                                                 op0=ALU.mult, op1=ALU.add)
                    if k == 0:
                        own.do(m)
                m.then_inc(summed, 1)
            repeat(dve, own, 0, TILES - 1, CS, 1, lambda n, s: combine(n, s, P))
            combine(TILES - 1, (TILES - 1) % CS, LAST)

        @block.sync
        def _(sp):
            def body(n, s):
                sp.wait_ge(summed, n + 1)
                sp.dma_start(out[at(n, P), :], y[:, s, 0, :]).then_inc(stored[s], 16)
            repeat(sp, Own(sp, None), 0, TILES - 1, CS, 0, body)
            sp.wait_ge(summed, TILES)
            sp.dma_start(out[(TILES - 1) * P:N_NODES, :], y[0:LAST, (TILES - 1) % CS, 0, :]).then_inc(stored[(TILES - 1) % CS], 16)
            for s in range(CS):
                sp.wait_ge(stored[s], 16 * len(range(s, TILES, CS)))


_INS = ["x", "src", "dst", "g_W", "g_asrc", "g_adst", "g_bias", "w_qkv", "mem_kv", "w_out", "b_out", "g_out",
        "g_pre", "gamma", "beta", "Wr", "br", "W1", "b1", "W2", "b2"]


def kernel(x, src, dst, L0_gnn_W, L0_gnn_att_src, L0_gnn_att_dst, L0_gnn_bias, L0_mix_t, L0_mix_w_qkv, L0_mix_mem_kv,
           L0_mix_w_out, L0_mix_b_out, L0_mix_g_out, L0_mix_g_pre, L0_ffn_gamma, L0_ffn_beta, L0_ffn_Wr, L0_ffn_br,
           L0_ffn_W1, L0_ffn_b1, L0_ffn_W2, L0_ffn_b2):
    import numpy as _np
    import concourse.bacc as _bacc
    from concourse import mybir as _mybir
    from concourse.bass_utils import run_bass_kernel_spmd as _run

    def edges(a, fill):
        a = _np.pad(_np.asarray(a), (0, BLOCKS * BLOCK - N_EDGES), constant_values=fill)
        return _np.ascontiguousarray(a.reshape(BLOCKS, P, SUB).transpose(1, 0, 2).reshape(P, BLOCKS * SUB))

    values = dict(zip(_INS, [
        _np.pad(_np.asarray(x), ((0, N_PAD - N_NODES), (0, 0))), edges(src, 0), edges(dst, N_PAD + 2 * WIN),
        L0_gnn_W, L0_gnn_att_src, L0_gnn_att_dst, L0_gnn_bias, L0_mix_w_qkv, L0_mix_mem_kv, L0_mix_w_out, L0_mix_b_out,
        L0_mix_g_out, L0_mix_g_pre, L0_ffn_gamma, L0_ffn_beta, L0_ffn_Wr, L0_ffn_br, L0_ffn_W1, L0_ffn_b1, L0_ffn_W2,
        L0_ffn_b2]))
    nc = _bacc.Bacc("TRN2", target_bir_lowering=False, num_devices=1)
    arrays, args = {}, []
    for name in _INS:
        a = _np.ascontiguousarray(values[name])
        arrays[f"in_{name}_dram"] = a
        args.append(nc.dram_tensor(f"in_{name}_dram", a.shape, _mybir.dt.from_np(a.dtype), kind="ExternalInput").ap())
    args.append(nc.dram_tensor("out_0_dram", (N_NODES, DIM), _mybir.dt.float32, kind="ExternalOutput").ap())
    gps_layer(nc, *args)
    r = _run(nc, [arrays], core_ids=[0])
    return r.results[0]["out_0_dram"]
```

```python
from contextlib import ExitStack

import concourse.bass as bass
from concourse import mybir

ALU = mybir.AluOpType
ACT = mybir.ActivationFunctionType
AX = mybir.AxisListType
F32 = mybir.dt.float32
I32 = mybir.dt.int32

P = 128
N_NODES = 6250
DIM = 256
TILES = -(-N_NODES // P)
N_PAD = TILES * P
LAST = N_NODES - (TILES - 1) * P
KC = DIM // P

G_HEADS = 4
F_HEAD = DIM // G_HEADS
ROW = DIM + G_HEADS
SLOPE = 0.2
LN_EPS = 1e-5

N_EDGES = 206250
SUB = 4
BLOCK = SUB * P
BLOCKS = -(-N_EDGES // BLOCK)
WIN = 32
ACC_W = N_PAD + WIN
WINDOWS = -(-N_NODES // WIN)
GUARD = 40.0

M_HEADS = 4
D_HEAD = 32
HID = M_HEADS * D_HEAD
N_MEM = 4
KV_W = 2 * HID + 4

EXPERTS = 8
FF = 512
FC = FF // P
MOE_TILES = (2 * N_NODES + EXPERTS * (P - 1)) // P
GT = 7
GROUPS = TILES // GT
assert GROUPS * GT == TILES
CAP = N_PAD + P
MROW = DIM + 2


class Own:

    def __init__(self, eng, sem):
        self.eng, self.sem, self.base, self.k = eng, sem, 0, 0

    def step(self, ins):
        ins.then_inc(self.sem, 1)
        self.k += 1
        return ins

    def wait(self):
        self.eng.wait_ge(self.sem, self.base + self.k)

    def do(self, ins):
        self.step(ins)
        self.wait()


def repeat(eng, own, first, total, unroll, per, body):
    full = (total - first) // unroll
    start = own.base + own.k
    if full:
        with eng.Fori(0, full) as it:
            for u in range(unroll):
                n = it * unroll + (first + u)
                own.base, own.k = start + (it * unroll + u) * per, 0
                body(n, (first + u) % unroll)
                assert own.k == per, (own.k, per)
    for n in range(first + full * unroll, total):
        own.base, own.k = start + (n - first) * per, 0
        body(n, n % unroll)
        assert own.k == per, (own.k, per)
    own.base, own.k = start + (total - first) * per, 0


def rounds(eng, own, first, count, slots, per, body, extra, extra_per):
    start, each = own.base + own.k, slots * per + sum(extra_per)
    with eng.Fori(0, count) as t:
        for u in range(slots):
            own.base, own.k = start + (t * each + (u * per + sum(extra_per[:u]))), 0
            body(t * slots + (first + u), (first + u) % slots)
            extra(t, u)
            assert own.k == per + extra_per[u], (own.k, per, extra_per[u])
    own.base, own.k = start + count * each, 0


def bcast(ap, axis, n):
    v = ap.unsqueeze(axis)
    shape = list(v.shape)
    shape[axis] = n
    return v.to_broadcast(shape)


def at(n, size=1):
    return bass.ds(n * size, size)


def gps_layer(nc, x, src, dst, g_W, g_asrc, g_adst, g_bias, w_qkv, mem_kv, w_out, b_out, g_out, g_pre,
              gamma, beta, Wr, br, W1, b1, W2, b2, out):
    table = nc.dram_tensor("node_table", [N_PAD, ROW], F32)
    dst_table = nc.dram_tensor("dst_table", [ACC_W, 2 * G_HEADS], F32)
    base_rows = nc.dram_tensor("base_rows", [N_PAD, DIM], F32)
    mixed_rows = nc.dram_tensor("mixed_rows", [N_PAD, DIM], F32)
    expert_in = nc.dram_tensor("expert_in", [EXPERTS * (CAP + P), MROW], F32)
    sum_rows = nc.dram_tensor("sum_rows", [N_PAD + P, DIM], F32)

    ctx = ExitStack()
    with ctx:
        def sb(name, shape, dt=F32, stack=ctx):
            return stack.enter_context(nc.sbuf_tensor(name, shape, dt))

        acc = sb("acc", [P, ACC_W * 4])
        region = sb("region", [P, TILES * (KV_W + HID)])
        ident = sb("ident", [P, P])
        ones = sb("ones", [P, P])
        valid = sb("valid", [P, TILES])
        sd = sb("sd", [P, TILES * 8])
        w_self = sb("w_self", [P, TILES * G_HEADS])
        spans = sb("spans", [1, 2], I32)

        dve_steps = Own(None, ctx.enter_context(nc.semaphore("dve_steps")))
        with ExitStack() as mix_ctx:
            q_all = region[:, TILES * KV_W:].rearrange("p (t c) -> p t c", c=HID)
            mmat = sb("mmat", [P, DIM], stack=mix_ctx)
            mix_rows = sb("mix_rows", [P, 2, DIM], stack=mix_ctx)
            src_idx = sb("src_idx", [P, (BLOCKS + 2) * SUB], I32, mix_ctx)[:, :]
            dst_raw = sb("dst_raw", [P, BLOCKS * SUB], I32, mix_ctx)[:, :]
            src_in, dst_in = (mix_ctx.enter_context(nc.semaphore(n)) for n in ("src_in", "dst_in"))
            node_used = []
            node_stage(nc, ctx, locals())
            edge_buffers = {}
            edge_stage(nc, locals())
            any_order_stage(nc, locals())

        W = EXPERTS * KC * FF
        SENT_AT = W
        w1_sb = region[:, 0:W].rearrange("p (e c f) -> p e c f", e=EXPERTS, c=KC)
        b2_sb = region[:, 2 * W:2 * W + EXPERTS * DIM]
        ye_sb = region[:, 2 * W + EXPERTS * DIM:2 * W + (EXPERTS + 2) * DIM]
        b1_sb = acc[:, W - EXPERTS * FF:W]
        w2_sb = acc[:, W:2 * W].rearrange("p (e c f) -> p e c f", e=EXPERTS, c=FC)
        assert 2 * W <= (GROUPS - 1) * GT * 4 * P
        affine = sb("affine", [P, 2, KC])
        tile_expert = sb("tile_expert", [1, MOE_TILES], I32)
        tile_start = sb("tile_start", [1, MOE_TILES], I32)
        weights_in = ctx.enter_context(nc.semaphore("weights_in"))
        rows_stage(nc, locals())
        expert_stage(nc, locals())


def node_stage(nc, ctx0, g):
    acc, region, ident, ones, valid, sd, w_self = (g[k] for k in ("acc", "region", "ident", "ones", "valid", "sd", "w_self"))
    table, dst_table, base_rows = g["table"], g["dst_table"], g["base_rows"]
    x_all = acc[:, 0:TILES * DIM].rearrange("p (t d) -> p t d", d=DIM)
    kv = region[:, 0:TILES * KV_W].rearrange("p (t c) -> p t c", c=KV_W)
    q_all, mmat, mix_rows = (g[k] for k in ("q_all", "mmat", "mix_rows"))
    sd3 = sd[:, :].rearrange("p (t c) -> p t c", c=8)
    X_GROUPS = 7
    XG = TILES // X_GROUPS
    KEY_PARTS = ((0, TILES // 2), (TILES // 2, TILES))
    XR = 4

    used = [TILES * DIM]

    def carve(*shape):
        size = 1
        for d in shape:
            size *= d
        v = acc[:, used[0]:used[0] + size]
        used[0] += size
        return v if len(shape) == 1 else v.rearrange("p (a b) -> p a b", b=shape[1])

    with ExitStack() as ctx:
        def sb(name, shape, dt=F32):
            return ctx.enter_context(nc.sbuf_tensor(name, shape, dt))

        def pb(name, shape):
            return ctx.enter_context(nc.psum_tensor(name, shape, F32))

        def sem(name):
            return ctx.enter_context(nc.semaphore(name))

        w_h = carve(KC, DIM + 8)
        w_q = carve(KC, 3 * HID)
        gpre = sb("gpre", [P, KC])
        att = carve(2, DIM)
        bias_row = carve(DIM)
        w_o = sb("w_o", [P, DIM])
        mem_k = sb("mem_k", [N_MEM, HID])
        mem_v = sb("mem_v", [N_MEM, HID + 4])
        tmp = sb("tmp", [P, DIM])
        st = sb("st", [P, TILES, 6])
        mv = sb("mv", [P, TILES, 2])
        s1 = sb("s1", [P, TILES])
        s2 = sb("s2", [P, TILES])
        rstd = sb("rstd", [P, TILES])
        r_scale = sb("r_scale", [P, TILES])
        r_bias = sb("r_bias", [P, TILES])
        un_scale = sb("un_scale", [P, TILES])
        eps = sb("eps", [P, 2])
        xr = carve(XR, DIM)
        xrT = carve(2, DIM)
        hrow = carve(2, DIM + 8)
        small = carve(8, TILES * G_HEADS)
        drow = sb("drow", [P, TILES * 8])
        kmb = sb("kmb", [P, HID])
        kcol = sb("kcol", [P, 2])
        cmat = sb("cmat", [P, HID])
        cT = sb("cT", [P, HID])
        ps_t = [pb(f"ps_t{i}", [P, 512]) for i in range(2)]
        ps_h = [pb(f"ps_h{i}", [P, 512]) for i in range(2)]
        ps_q = [pb(f"ps_q{i}", [P, 512]) for i in range(2)]
        ps_c = pb("ps_c", [P, 512])
        ps_m = pb("ps_m", [P, 512])

        x_in = [sem(f"x_in{i}") for i in range(X_GROUPS)]
        loads = sem("loads")
        consts = sem("consts")
        own_p = sem("own_p")
        stats = sem("stats")
        sqrt1, sqrt2 = sem("sqrt1"), sem("sqrt2")
        r_ready = sem("r_ready")
        weights = sem("weights")
        xr_ready, xT_ps, xT_ready = sem("xr_ready"), sem("xT_ps"), sem("xT_ready")
        h_ps, q_ps, h_ready, q_ready = sem("h_ps"), sem("q_ps"), sem("h_ready"), sem("q_ready")
        table_out = [sem(f"table_out{i}") for i in range(2)]
        smax_ready, smax_T, gdiag, gmax_ps = sem("smax_ready"), sem("smax_T"), sem("gdiag"), sem("gmax_ps")
        dlog, dexp, drow_ready, d_out = sem("dlog"), sem("dexp"), sem("drow_ready"), sem("d_out")
        kmax_ready, kmax_T, kdiag, kmax_ps = sem("kmax_ready"), sem("kmax_T"), sem("kdiag"), sem("kmax_ps")
        k_shift, k_exp = sem("k_shift"), sem("k_exp")
        ctx_ps, c_ready, cT_ps, cT_ready, m_ps = (sem(n) for n in ("ctx_ps", "c_ready", "cT_ps", "cT_ready", "m_ps"))
        base_ready, base_out, xr_used, sd_ready = sem("base_ready"), sem("base_out"), sem("xr_used"), sem("sd_ready")
        g["node_used"].append(used[0])
        block = ctx.enter_context(nc.Block())
        N_LOADS = 12

        @block.sync
        def _(sp):
            xv = g["x"].rearrange("(t p) d -> p t d", p=P)
            for i in range(X_GROUPS):
                sp.dma_start(x_all[:, i * XG:(i + 1) * XG, :], xv[:, i * XG:(i + 1) * XG, :]).then_inc(x_in[i], 16)
            sp.dma_start(g["src_idx"][:, 0:BLOCKS * SUB], g["src"]).then_inc(g["src_in"], 16)
            sp.dma_start(g["dst_raw"], g["dst"]).then_inc(g["dst_in"], 16)
            def body(n, s):
                sp.wait_ge(h_ready, n + 3)
                sp.dma_start(table[at(n, P), :], hrow[:, s, 0:ROW]).then_inc(table_out[s], 16)
                sp.wait_ge(base_ready, n + 1)
                sp.dma_start(base_rows[at(n, P), :], x_all[:, at(n), :].squeeze(1)).then_inc(base_out, 16)
            for_sp(sp, TILES, body)
            sp.wait_ge(drow_ready, 1)
            sp.dma_start(dst_table[0:N_PAD, :].rearrange("(t p) c -> p t c", p=P),
                         drow[:, :].rearrange("p (t c) -> p t c", c=8)).then_inc(d_out, 16)
            sp.dma_start(dst_table[N_PAD:ACC_W, :], tmp[0:WIN, 0:8]).then_inc(d_out, 16)
            for i in range(2):
                sp.wait_ge(table_out[i], 16 * ((TILES + 1 - i) // 2))
            sp.wait_ge(d_out, 32)
            sp.wait_ge(base_out, 16 * TILES)

        @block.gpsimd
        def _(pool):
            pool.memset(ident[:, :], 0.0).then_inc(own_p, 1)
            pool.memset(valid[:, :], 1.0).then_inc(own_p, 1)
            pool.memset(ones[:, :], 1.0).then_inc(consts, 1)
            pool.wait_ge(own_p, 2)
            pool.affine_select(out=ident[:, :], in_=ident[:, :], compare_op=ALU.not_equal, fill=1.0, base=0,
                               pattern=[[-1, P]], channel_multiplier=1).then_inc(consts, 1)
            pool.affine_select(out=valid[:, :], in_=valid[:, :], compare_op=ALU.is_gt, fill=0.0, base=N_NODES,
                               pattern=[[-P, TILES]], channel_multiplier=-1).then_inc(consts, 1)
            pool.memzero(acc[:, used[0]:]).then_inc(consts, 1)
            pool.wait_ge(base_out, 16 * TILES)
            pool.memzero(acc[:, 0:TILES * DIM]).then_inc(consts, 1)

        @block.scalar
        def _(act):
            for c in range(KC):
                act.dma_start(w_h[:, c, 0:DIM].rearrange("p (h f) -> p h f", f=F_HEAD),
                              g["g_W"][:, c * P:(c + 1) * P, :].rearrange("h p f -> p h f")).then_inc(loads, 16)
            act.dma_start(w_q[:, :, :], g["w_qkv"].rearrange("(c p) n -> p c n", p=P)).then_inc(loads, 16)
            act.dma_start(gpre[:, :], g["g_pre"].rearrange("(c p) -> p c", p=P), allow_slow_non_contiguous=True).then_inc(loads, 16)
            for i, a in enumerate((g["g_asrc"], g["g_adst"])):
                act.dma_start(att[:, i, :], a.rearrange("h f -> (h f)").partition_broadcast(P)).then_inc(loads, 16)
            act.dma_start(bias_row, g["g_bias"].partition_broadcast(P)).then_inc(loads, 16)
            for i, a in enumerate((g["b_out"], g["g_out"])):
                act.dma_start(mix_rows[:, i, :], a.partition_broadcast(P)).then_inc(loads, 16)
            act.dma_start(w_o[:, :], g["w_out"]).then_inc(loads, 16)
            act.dma_start(mem_k[:, :], g["mem_kv"][0].rearrange("h d m -> m (h d)"), allow_slow_non_contiguous=True).then_inc(loads, 16)
            act.dma_start(mem_v[:, 0:HID], g["mem_kv"][1].rearrange("h d m -> m (h d)"), allow_slow_non_contiguous=True).then_inc(loads, 16)
            act.wait_ge(stats, 1)
            act.activation(s1[:, :], mv[:, :, 1], ACT.Sqrt, bias=eps[:, 0:1]).then_inc(sqrt1, 1)
            act.wait_ge(stats, 2)
            act.activation(s2[:, :], s1[:, :], ACT.Sqrt).then_inc(sqrt2, 1)
            act.wait_ge(r_ready, 1)

            def unit_rows(n, s):
                act.wait_ge(xT_ps, n + 1)
                act.wait_ge(xr_used, n + 1)
                act.activation(xr[:, s, :], x_all[:, at(n), :].squeeze(1), ACT.Identity,
                               bias=r_bias[:, at(n)], scale=r_scale[:, at(n)]).then_inc(xr_ready, 1)

            def table_rows(n, s):
                act.wait_ge(h_ps, n + 1)
                if not isinstance(n, int) or n >= 2:
                    act.wait_ge(table_out[s], slot_count(n - 2, s, 16, 2))
                    act.wait_ge(sd_ready, n - 1)
                act.activation(hrow[:, s, :], ps_h[s][:, 0:DIM + 8], ACT.Copy, scale=un_scale[:, at(n)]).then_inc(h_ready, 1)

            def body(n, s):
                unit_rows(n + 2, (s + 2) % XR)
                table_rows(n, s % 2)
            unit_rows(0, 0)
            unit_rows(1, 1)
            body(0, 0)
            body(1, 1)
            repeat(act, Own(act, None), 2, TILES - 2, XR, 0, body)
            for n in (TILES - 2, TILES - 1):
                table_rows(n, n % 2)
            act.wait_ge(dlog, 1)
            act.activation(w_self[:, :], small[:, 0, :], ACT.Exp).then_inc(dexp, 1)
            for i, (a, b) in enumerate(KEY_PARTS):
                act.wait_ge(k_shift, i + 1)
                act.activation(kv[:, a:b, 0:HID], kv[:, a:b, 0:HID], ACT.Exp).then_inc(k_exp, 1)
            act.activation(mem_k[:, :], mem_k[:, :], ACT.Exp).then_inc(k_exp, 1)

        @block.tensor
        def _(pe):
            own = Own(pe, None)
            pe.sem_inc(xT_ps, XR)
            pe.wait_ge(consts, 3)
            pe.wait_ge(weights, 1)

            def across(n, s):
                pe.wait_ge(xr_ready, n + 1)
                pe.wait_ge(xT_ready, n + 1)
                for c in range(KC):
                    m = pe.transpose(ps_t[s % 2][:, c * P:(c + 1) * P], xr[:, s, c * P:(c + 1) * P], ident[:, :])
                m.then_inc(xT_ps, 1)

            def products(n, s):
                pe.wait_ge(xT_ready, n + 3)
                pe.wait_ge(h_ready, n + 1)
                for c in range(KC):
                    m = pe.matmul(ps_h[s][:, 0:DIM + 8], xrT[:, s, c * P:(c + 1) * P], w_h[:, c, :],
                                  start=c == 0, stop=c == KC - 1)
                m.then_inc(h_ps, 1)
                pe.wait_ge(q_ready, n + 1)
                for c in range(KC):
                    m = pe.matmul(ps_q[s][:, 0:3 * HID], xrT[:, s, c * P:(c + 1) * P], w_q[:, c, :],
                                  start=c == 0, stop=c == KC - 1)
                m.then_inc(q_ps, 1)

            def body(n, s):
                across(n + 1, (s + 1) % XR)
                products(n, s % 2)
            across(0, 0)
            repeat(pe, own, 0, TILES - 1, XR, 0, body)
            products(TILES - 1, (TILES - 1) % 2)
            pe.wait_ge(smax_ready, 1)
            pe.transpose(ps_c[0:G_HEADS, 0:P], small[:, 7, 0:G_HEADS], ident[:, :]).then_inc(smax_T, 1)
            pe.wait_ge(gdiag, 1)
            pe.matmul(ps_c[:, 256:256 + G_HEADS], ones[0:G_HEADS, :], tmp[0:G_HEADS, 128:128 + G_HEADS],
                      start=True, stop=True).then_inc(gmax_ps, 1)
            pe.wait_ge(kmax_ready, 1)
            pe.transpose(ps_t[0][:, 0:P], kmb[:, :], ident[:, :]).then_inc(kmax_T, 1)
            pe.wait_ge(kdiag, 1)
            pe.matmul(ps_t[1][:, 0:HID], ones[:, :], cmat[:, :], start=True, stop=True).then_inc(kmax_ps, 1)
            for n in range(TILES):
                if n in (KEY_PARTS[0][0], KEY_PARTS[1][0]):
                    pe.wait_ge(k_exp, 1 + (n > 0))
                rows_n = P if n < TILES - 1 else LAST
                pe.matmul(ps_m[:, 0:HID + 4], kv[0:rows_n, n, 0:HID], kv[0:rows_n, n, HID:KV_W],
                          start=n == 0, stop=False)
            pe.wait_ge(k_exp, 3)
            pe.matmul(ps_m[:, 0:HID + 4], mem_k[:, :], mem_v[:, :], start=False, stop=True).then_inc(ctx_ps, 1)
            pe.wait_ge(c_ready, 1)
            pe.transpose(ps_t[0][:, 0:P], cmat[:, :], ident[:, :]).then_inc(cT_ps, 1)
            pe.wait_ge(cT_ready, 1)
            pe.matmul(ps_m[:, 0:DIM], cT[:, :], w_o[:, :], start=True, stop=True).then_inc(m_ps, 1)

        @block.vector
        def _(dve):
            own = g["dve_steps"]
            own.eng = dve
            dve.sem_inc(h_ready, 2)
            dve.sem_inc(q_ready, 2)
            dve.sem_inc(xT_ready, 2)
            dve.sem_inc(xr_used, XR)
            dve.memset(eps[:, 0:1], LN_EPS)
            own.do(dve.memset(kv[:, :, 2 * HID:KV_W], 1.0))
            for i in range(X_GROUPS):
                dve.wait_ge(x_in[i], 16)

                def moments(n, s):
                    own.step(dve.bn_stats(st[:, at(n + i * XG), :].squeeze(1), x_all[:, at(n + i * XG), :].squeeze(1)))
                repeat(dve, own, 0, XG, XG, 1, moments)
            own.wait()
            join_moments(dve, own, st, mv, s1)
            dve.sem_inc(stats, 1)
            dve.wait_ge(sqrt1, 1)
            own.do(dve.reciprocal(rstd[:, :], s1[:, :]))
            own.do(dve.tensor_tensor(s2[:, :], rstd[:, :], rstd[:, :], ALU.mult))
            own.do(dve.tensor_tensor(s2[:, :], s2[:, :], mv[:, :, 1], ALU.mult))
            own.do(dve.tensor_scalar(s1[:, :], s2[:, :], float(DIM), 1e-24, ALU.mult, ALU.max))
            dve.sem_inc(stats, 1)
            dve.wait_ge(sqrt2, 1)
            own.do(dve.tensor_scalar(un_scale[:, :], s2[:, :], 1.0 / 16, None, ALU.mult))
            own.do(dve.reciprocal(s1[:, :], un_scale[:, :]))
            own.do(dve.tensor_tensor(r_scale[:, :], s1[:, :], rstd[:, :], ALU.mult))
            own.do(dve.scalar_tensor_tensor(out=r_bias[:, :], in0=mv[:, :, 0], scalar=-1.0, in1=r_scale[:, :],
                                            op0=ALU.mult, op1=ALU.mult))
            dve.sem_inc(r_ready, 1)
            dve.wait_ge(loads, 16 * N_LOADS)
            for i in range(2):
                for c in range(KC):
                    own.do(dve.tensor_tensor(tmp[:, :], w_h[:, c, 0:DIM], att[:, i, :], ALU.mult))
                    own.do(dve.tensor_reduce(w_h[:, c, DIM + 4 * i:DIM + 4 * i + 4],
                                             tmp[:, :].rearrange("p (h f) -> p h f", f=F_HEAD), AX.X, ALU.add))
            for c in range(KC):
                own.do(dve.tensor_scalar(w_q[:, c, :], w_q[:, c, :], gpre[:, c:c + 1], None, ALU.mult))
            dve.sem_inc(weights, 1)

            def rows_back(n, s):
                dve.wait_ge(xT_ps, n + 1 + XR)
                dve.tensor_copy(xrT[:, s, :], ps_t[s][:, 0:DIM]).then_inc(xT_ready, 1)

            def rest(n, x):
                s = x % 2
                xt = x_all[:, at(n), :].squeeze(1)
                dve.wait_ge(xr_ready, n + 1)
                own.do(dve.scalar_tensor_tensor(out=xt, in0=xr[:, x, :], scalar=un_scale[:, at(n)], in1=xt,
                                                op0=ALU.mult, op1=ALU.add))
                dve.sem_inc(xr_used, 1)
                dve.tensor_tensor(xt, xt, bias_row, ALU.add).then_inc(base_ready, 1)
                dve.wait_ge(h_ready, n + 3)
                dve.tensor_copy(sd3[:, at(n), :].squeeze(1), hrow[:, s, DIM:DIM + 8]).then_inc(sd_ready, 1)
                dve.wait_ge(q_ps, n + 1)
                own.step(dve.tensor_copy(q_all[:, at(n), :].squeeze(1), ps_q[s][:, 0:HID]))
                own.step(dve.tensor_copy(kv[:, at(n), 0:2 * HID].squeeze(1), ps_q[s][:, HID:3 * HID]))
                own.wait()
                dve.sem_inc(q_ready, 1)

            def body(n, s):
                rows_back(n + 1, (s + 1) % 2)
                rest(n, s)
            rows_back(0, 0)
            repeat(dve, own, 0, TILES - 1, XR, 3, body)
            rest(TILES - 1, (TILES - 1) % XR)
            dve.wait_ge(q_ready, TILES + 2)
            dve.wait_ge(sd_ready, TILES)
            s_, d_ = sd3[:, :, 0:4], sd3[:, :, 4:8]

            def sm(i):
                return small[:, i, :].rearrange("p (t h) -> p t h", h=G_HEADS)
            dve.wait_ge(consts, 3)
            own.do(dve.tensor_tensor(sm(1), s_, bcast(valid[:, :], 2, G_HEADS), ALU.mult))
            own.do(dve.tensor_scalar(s1[:, :], valid[:, :], 1e30, -1e30, ALU.mult, ALU.add))
            own.do(dve.tensor_tensor(sm(1), sm(1), bcast(s1[:, :], 2, G_HEADS), ALU.add))
            own.do(dve.tensor_reduce(small[:, 7, 0:G_HEADS], sm(1).rearrange("p t h -> p h t"), AX.X, ALU.max))
            dve.sem_inc(smax_ready, 1)
            dve.wait_ge(smax_T, 1)
            own.do(dve.tensor_reduce(kcol[0:G_HEADS, 0:1], ps_c[0:G_HEADS, 0:P], AX.X, ALU.max))
            own.do(dve.tensor_scalar(tmp[0:G_HEADS, 128:128 + G_HEADS], ident[0:G_HEADS, 0:G_HEADS],
                                     kcol[0:G_HEADS, 0:1], None, ALU.mult))
            dve.sem_inc(gdiag, 1)
            dve.wait_ge(gmax_ps, 1)
            own.do(dve.tensor_copy(small[:, 7, 0:G_HEADS], ps_c[:, 256:256 + G_HEADS]))
            own.do(dve.tensor_tensor(sm(1), d_, bcast(small[:, 7, 0:G_HEADS], 1, TILES), ALU.add))
            own.do(dve.scalar_tensor_tensor(out=sm(2), in0=sm(1), scalar=SLOPE, in1=sm(1), op0=ALU.mult, op1=ALU.max))
            own.do(dve.tensor_tensor(sm(3), s_, d_, ALU.add))
            own.do(dve.scalar_tensor_tensor(out=sm(4), in0=sm(3), scalar=SLOPE, in1=sm(3), op0=ALU.mult, op1=ALU.max))
            own.do(dve.scalar_tensor_tensor(out=sm(5), in0=sm(4), scalar=GUARD, in1=sm(2), op0=ALU.add, op1=ALU.min))
            own.do(dve.tensor_tensor(sm(0), sm(4), sm(5), ALU.subtract))
            dve.sem_inc(dlog, 1)
            dr = drow[:, :].rearrange("p (t c) -> p t c", c=8)
            own.do(dve.tensor_copy(dr[:, :, 0:4], d_))
            own.do(dve.tensor_copy(dr[:, :, 4:8], sm(5)))
            own.do(dve.memset(tmp[:, 0:8], 0.0))
            dve.sem_inc(drow_ready, 1)
            own.do(dve.memset(mem_v[:, HID:HID + 4], 1.0))
            kk = kv[:, :, 0:HID]
            own.do(dve.tensor_reduce(kmb[:, :], kk[:, 0:TILES - 1, :].rearrange("p t c -> p c t"), AX.X, ALU.max))
            own.do(dve.tensor_tensor(kmb[0:LAST, :], kmb[0:LAST, :], kv[0:LAST, TILES - 1, 0:HID], ALU.max))
            own.do(dve.tensor_tensor(kmb[0:N_MEM, :], kmb[0:N_MEM, :], mem_k[:, :], ALU.max))
            dve.sem_inc(kmax_ready, 1)
            dve.wait_ge(kmax_T, 1)
            own.do(dve.tensor_reduce(kcol[:, 0:1], ps_t[0][:, 0:P], AX.X, ALU.max))
            own.do(dve.tensor_scalar(cmat[:, :], ident[:, :], kcol[:, 0:1], None, ALU.mult))
            dve.sem_inc(kdiag, 1)
            dve.wait_ge(kmax_ps, 1)
            own.do(dve.tensor_copy(kmb[:, :], ps_t[1][:, 0:HID]))
            own.do(dve.tensor_tensor(mem_k[:, :], mem_k[:, :], kmb[0:N_MEM, :], ALU.subtract))
            for a, b in KEY_PARTS:
                own.do(dve.tensor_tensor(kk[:, a:b, :], kk[:, a:b, :], bcast(kmb[:, :], 1, b - a), ALU.subtract))
                dve.sem_inc(k_shift, 1)
            own.do(dve.memset(cmat[:, :], 0.0))
            dve.wait_ge(ctx_ps, 1)
            own.do(dve.reciprocal(kcol[:, 1:2], ps_m[:, HID:HID + 1]))
            for h in range(M_HEADS):
                r = slice(h * D_HEAD, (h + 1) * D_HEAD)
                own.step(dve.tensor_scalar(cmat[r, r], ps_m[r, r], kcol[r, 1:2], None, ALU.mult))
            own.wait()
            dve.sem_inc(c_ready, 1)
            dve.wait_ge(cT_ps, 1)
            own.do(dve.tensor_copy(cT[:, :], ps_t[0][:, 0:P]))
            dve.sem_inc(cT_ready, 1)
            dve.wait_ge(m_ps, 1)
            own.do(dve.tensor_copy(mmat[:, :], ps_m[:, 0:DIM]))


def join_moments(dve, own, st, mv, tmp):
    own.do(dve.tensor_tensor(mv[:, :, 0], st[:, :, 1], st[:, :, 4], ALU.add))
    own.do(dve.tensor_scalar(mv[:, :, 0], mv[:, :, 0], 0.5, None, ALU.mult))
    own.do(dve.tensor_tensor(tmp[:, :], st[:, :, 1], st[:, :, 4], ALU.subtract))
    own.do(dve.scalar_tensor_tensor(out=tmp[:, :], in0=tmp[:, :], scalar=0.25, in1=tmp[:, :], op0=ALU.mult, op1=ALU.mult))
    own.do(dve.tensor_tensor(mv[:, :, 1], st[:, :, 2], st[:, :, 5], ALU.add))
    own.do(dve.scalar_tensor_tensor(out=mv[:, :, 1], in0=mv[:, :, 1], scalar=1.0 / DIM, in1=tmp[:, :],
                                    op0=ALU.mult, op1=ALU.add))


def for_sp(sp, total, body):
    with sp.Fori(0, total // 2) as it:
        for u in range(2):
            body(it * 2 + u, u)
    for n in range(total // 2 * 2, total):
        body(n, n % 2)


def edge_stage(nc, g):
    acc, region, ident, ones, spans = (g[k] for k in ("acc", "region", "ident", "ones", "spans"))
    table, dst_table = g["table"], g["dst_table"]
    acc4 = acc[:, :].rearrange("p (w c) -> p w c", c=4)
    SL = 3
    PAUSE = 1 + SL * (TILES + 2)
    SECOND = PAUSE + 2 * SL
    THIRD = SECOND + SL * TILES
    assert THIRD + SL <= BLOCKS

    def nothing(t, u):
        pass

    used = [0]

    def carve(*shape, dt=F32):
        size = 1
        for s in shape:
            size *= s
        v = region[:, used[0]:used[0] + size]
        used[0] += size
        if dt != F32:
            v = v.bitcast(dt)
        return v

    src_idx, dst_raw, src_in, dst_in = (g[k] for k in ("src_idx", "dst_raw", "src_in", "dst_in"))
    idx = carve(SL * SUB, dt=I32)
    rel = carve((BLOCKS + 1) * SUB)
    rows = carve(SL * SUB * ROW).rearrange("p (s j c) -> p s j c", s=SL, j=SUB)
    mask = carve(SL * SUB * WIN).rearrange("p (s j w) -> p s j w", s=SL, j=SUB)
    maskT = carve(SL * P).rearrange("p (s e) -> p s e", s=SL)
    dwin = carve(SL * 8).rearrange("p (s c) -> p s c", s=SL)
    dblk = carve(SL * SUB * 8).rearrange("p (s j c) -> p s j c", s=SL, j=SUB)
    wts = carve(SL * SUB * P).rearrange("p (s j c) -> p s j c", s=SL, j=SUB)
    wsum = carve(SL * P).rearrange("p (s c) -> p s c", s=SL)
    lg = carve(SL * SUB * G_HEADS).rearrange("p (s j h) -> p s j h", s=SL, j=SUB)
    ex = carve(SL * SUB * G_HEADS).rearrange("p (s j h) -> p s j h", s=SL, j=SUB)
    z = carve(SUB * G_HEADS).rearrange("p (j h) -> p j h", j=SUB)
    lr = carve(SUB * G_HEADS).rearrange("p (j h) -> p j h", j=SUB)
    win_i = carve(WIN, dt=I32)
    win = carve(WIN)
    bm = carve(SUB * 8).rearrange("p (j c) -> p j c", j=SUB)
    bases = carve(BLOCKS + 1, dt=I32)
    bases_f = carve(BLOCKS)
    badn = carve(2)
    assert used[0] <= TILES * KV_W
    q_all, mmat, mix_rows, base_rows, mixed_rows = (g[k] for k in (
        "q_all", "mmat", "mix_rows", "base_rows", "mixed_rows"))
    bad, badc = region[:, TILES * KV_W:TILES * KV_W + BLOCKS * SUB], region[:, TILES * KV_W + BLOCKS * SUB:
                                                                            TILES * KV_W + 2 * BLOCKS * SUB]
    g["edge_buffers"].update(locals())

    with ExitStack() as ctx:
        def sem(name):
            return ctx.enter_context(nc.semaphore(name))
        ps_p = [ctx.enter_context(nc.psum_tensor(f"ps_p{i}", [P, 512], F32)) for i in range(SL)]
        ps_s = [ctx.enter_context(nc.psum_tensor(f"ps_s{i}", [P, 512], F32)) for i in range(SL)]
        ps_b = ctx.enter_context(nc.psum_tensor("ps_b", [P, 512], F32))
        ps_o = ctx.enter_context(nc.psum_tensor("ps_o", [P, 512], F32))

        def sb(name, shape):
            return ctx.enter_context(nc.sbuf_tensor(name, shape, F32))
        qn, qT, o_row = sb("qn", [P, HID]), sb("qT", [P, HID]), sb("o_row", [P, DIM])
        ob_in = sb("ob_in", [P, 2, DIM])
        st, mv = sb("st_mix", [P, TILES, 6]), sb("mv_mix", [P, TILES, 2])
        s1, s2 = sb("s1_mix", [P, TILES]), sb("s2_mix", [P, TILES])
        q_sum = sb("q_sum", [P, 2, M_HEADS])
        (q_shifted, q_exp, q_taken, qn_ready, qT_ps, qT_ready, o_ps, o_ready, o_out, ss_ready, ss_sqrt, tile_in, base_ready,
         base_out) = (
            sem("mix_" + n) for n in ("q_shifted", "q_exp", "q_taken", "qn_ready", "qT_ps", "qT_ready", "o_ps", "o_ready", "o_out", "ss_ready",
                                      "ss_sqrt", "tile_in", "base_ready", "base_out"))

        own_p = sem("own_p2")
        pool_consts, bases_f_ready, bases_ps, span_ready, span_ps = (sem(n) for n in (
            "pool_consts", "bases_f_ready", "bases_ps", "span_ready", "span_ps"))
        gathered = [sem(f"gathered{i}") for i in range(SL)]
        dwin_in = [sem(f"dwin_in{i}") for i in range(SL)]
        idx_ready, slots_open = sem("idx_ready"), sem("slots_open")
        (zeroed_a, mask_ready, maskT_ps, maskT_ready, dlog_ps, logits_ready, ex_ready, w_ready, wsum_ready,
         block_ps, block_done) = (sem(n) for n in (
             "zeroed_a", "mask_ready", "maskT_ps", "maskT_ready", "dlog_ps", "logits_ready", "ex_ready",
             "w_ready", "wsum_ready", "block_ps", "block_done"))
        block = ctx.enter_context(nc.Block())

        @block.sync
        def _(sp):
            sp.dma_start(bases[0:1, 0:BLOCKS], g["dst"][0:1, :].rearrange("p (b j) -> p b j", j=SUB)[:, :, 0],
                         allow_slow_non_contiguous=True).then_inc(dst_in, 16)
            sp.wait_ge(dst_in, 32)
            sp.wait_ge(pool_consts, 2)

            def body(n, s):
                base = sp.value_load(bases[0:1, at(n)], min_val=0, max_val=N_PAD)
                sp.wait_ge(mask_ready, n + 1)
                sp.dma_start(dwin[:, s, :], bcast(dst_table[bass.ds(base, WIN), :], 0, SUB)).then_inc(dwin_in[s], 16)
            def run(first, count, extra):
                rounds(sp, Own(sp, None), first, count, SL, 0, body, extra, (0,) * SL)

            def mixed_out(n):
                sp.wait_ge(o_ready, n + 2)
                sp.dma_start(mixed_rows[at(n, P), :], o_row[:, :]).then_inc(o_out, 16)

            def tile_load(n):
                sp.dma_start(ob_in[:, 0, :], mixed_rows[at(n, P), :]).then_inc(tile_in, 16)
                sp.dma_start(ob_in[:, 1, :], base_rows[at(n, P), :]).then_inc(tile_in, 16)

            def base_store(n):
                sp.wait_ge(base_ready, n + 1)
                sp.dma_start(base_rows[at(n, P), :], ob_in[:, 1, :]).then_inc(base_out, 16)

            def stage_1(t, u):
                if u == 2:
                    mixed_out(t)

            def stage_2(t, u):
                if u == SL - 2:
                    base_store(t)
                elif u == SL - 1:
                    sp.wait_ge(base_out, 16 * t + 16)
                    tile_load(t + 1)
            body(0, 0)
            run(1, 3, nothing)
            run(1 + 3 * SL, TILES - 1, stage_1)
            run(PAUSE, 1, nothing)
            mixed_out(TILES - 1)
            sp.wait_ge(o_out, 16 * TILES)
            tile_load(0)
            run(PAUSE + SL, 1, nothing)
            run(SECOND, 1, nothing)
            run(SECOND + SL, TILES - 1, stage_2)
            run(THIRD, 1, nothing)
            base_store(TILES - 1)
            repeat(sp, Own(sp, None), THIRD + SL, BLOCKS + 1, SL, 0, body)
            sp.wait_ge(base_out, 16 * TILES)
            for s in range(SL):
                sp.wait_ge(dwin_in[s], 16 * len(range(s, BLOCKS + 1, SL)))

        @block.gpsimd
        def _(pool):
            pool.memset(bases[0:1, BLOCKS:BLOCKS + 1], 0).then_inc(pool_consts, 1)
            pool.memset(src_idx[:, BLOCKS * SUB:], 0).then_inc(pool_consts, 1)
            pool.iota(win_i, [[1, WIN]], base=0, channel_multiplier=0).then_inc(pool_consts, 1)
            pool.memset(bm, 1.0).then_inc(own_p, 1)
            pool.wait_ge(own_p, 1)
            pool.affine_select(out=bm, in_=bm, compare_op=ALU.is_ge, fill=0.0, base=0,
                               pattern=[[-WIN, SUB], [0, 8]], channel_multiplier=1).then_inc(own_p, 1)
            pool.wait_ge(own_p, 2)
            pool.affine_select(out=bm, in_=bm, compare_op=ALU.is_ge, fill=0.0, base=WIN - 1,
                               pattern=[[WIN, SUB], [0, 8]], channel_multiplier=-1).then_inc(pool_consts, 1)
            def body(n, s):
                pool.wait_ge(block_ps, n + 1)
                pool.wait_ge(idx_ready, n + 1)
                pool.sem_inc(slots_open, 1)
                for j in range(SUB):
                    pool.indirect_dma_start(
                        out=rows[:, s, j, :], out_offset=None, in_=table[:, :],
                        in_offset=bass.IndirectOffsetOnAxis(ap=idx[:, s * SUB + j:s * SUB + j + 1], axis=0),
                    ).then_inc(gathered[s], 16)
            repeat(pool, Own(pool, None), 0, BLOCKS, SL, 0, body)
            for s in range(SL):
                pool.wait_ge(gathered[s], 64 * len(range(s, BLOCKS, SL)))

        @block.scalar
        def _(act):
            act.wait_ge(src_in, 16)
            act.wait_ge(pool_consts, 2)

            def indices(n, s):
                act.activation(idx[:, s * SUB:(s + 1) * SUB], src_idx[:, at(n, SUB)], ACT.Copy).then_inc(idx_ready, 1)
            indices(0, 0)
            indices(1, 1)
            indices(2, 2)
            act.memzero(acc[:, TILES * DIM:g["node_used"][0]]).then_inc(zeroed_a, 1)

            def mask_copy(n, s):
                act.wait_ge(maskT_ps, n + 1)
                act.activation(maskT[:, s, :], ps_s[s][:, 0:P], ACT.Copy).then_inc(maskT_ready, 1)

            def body(n, s):
                if not isinstance(n, int) or n:
                    indices(n + 2, (s + 2) % SL)
                act.wait_ge(logits_ready, n + 1)
                act.activation(ex[:, s], lg[:, s], ACT.Exp).then_inc(ex_ready, 1)
                mask_copy(n + 1, (s + 1) % SL)
            def query_exp(t):
                act.wait_ge(q_shifted, t + 1)
                q = q_all[:, at(t), :].squeeze(1)
                act.activation(q, q, ACT.Exp).then_inc(q_exp, 1)

            def query_back(t):
                act.wait_ge(qT_ps, t + 2)
                act.activation(qT[:, :], ps_b[:, 0:P], ACT.Copy).then_inc(qT_ready, 1)

            def stage_1(t, u):
                if u == 1:
                    query_back(t)
                    query_exp(t + 1)

            def run(first, count, extra):
                rounds(act, Own(act, None), first, count, SL, 0, body, extra, (0,) * SL)
            mask_copy(0, 0)
            body(0, 0)
            run(1, 1, lambda t, u: query_exp(0) if u == 1 else None)
            run(1 + SL, TILES - 1, stage_1)
            run(PAUSE - 2 * SL, 1, lambda t, u: query_back(TILES - 1) if u == 1 else None)
            run(PAUSE - SL, 1, nothing)
            act.wait_ge(ss_ready, 1)
            act.activation(s2[:, :], s1[:, :], ACT.Sqrt).then_inc(ss_sqrt, 1)
            repeat(act, Own(act, None), PAUSE, BLOCKS, SL, 0, body)

        @block.tensor
        def _(pe):
            pe.sem_inc(block_ps, SL)
            pe.sem_inc(qT_ps, 1)
            pe.wait_ge(bases_f_ready, 1)
            pe.matmul(ps_b[:, 0:BLOCKS], ones[0:1, :], bases_f[0:1, :], start=True, stop=True).then_inc(bases_ps, 1)

            def prepare(n, s):
                pe.wait_ge(mask_ready, n + 4)
                pe.transpose(ps_s[s][:, 0:P], mask[:, s].rearrange("p j w -> p (j w)"), ident[:, :]).then_inc(maskT_ps, 1)
                pe.wait_ge(maskT_ready, n + 1)
                pe.matmul(ps_s[s][:, P:P + SUB * 8], maskT[:, s, :], dblk[:, s].rearrange("p j c -> p (j c)"),
                          start=True, stop=True).then_inc(dlog_ps, 1)

            def body(n, s):
                prepare(n + 1, (s + 1) % SL)
                pe.wait_ge(w_ready, n + 1)
                pe.wait_ge(block_done, n + 1)
                for y in range(2):
                    for j in range(SUB):
                        pe.matmul(ps_p[s][:, y * P:(y + 1) * P], rows[:, s, j, y * P:(y + 1) * P], wts[:, s, j, :],
                                  start=j == 0, stop=j == SUB - 1)
                pe.wait_ge(wsum_ready, n + 1)
                pe.matmul(strided(ps_p[s], 2 * P, 192), ones[:, :], wsum[:, s].rearrange("p (a b) -> p a b", a=2),
                          start=True, stop=True).then_inc(block_ps, 1)
            def stage_1(t, u):
                if u == 0:
                    pe.wait_ge(qn_ready, t + 1)
                    pe.transpose(ps_b[:, 0:P], qn[:, :], ident[:, :]).then_inc(qT_ps, 1)
                elif u == 2:
                    pe.wait_ge(qT_ready, t + 1)
                    pe.wait_ge(o_ready, t + 1)
                    pe.matmul(ps_o[:, 0:DIM], qT[:, :], mmat[:, :], start=True, stop=True).then_inc(o_ps, 1)
            prepare(0, 0)
            body(0, 0)
            rounds(pe, Own(pe, None), 1, 1, SL, 0, body, nothing, (0,) * SL)
            rounds(pe, Own(pe, None), 1 + SL, TILES, SL, 0, body, stage_1, (0,) * SL)
            repeat(pe, Own(pe, None), PAUSE - SL, BLOCKS, SL, 0, body)
            pe.wait_ge(span_ready, 1)
            pe.matmul(ps_b[0:1, 0:1], badn[:, 0:1], ones[:, 0:1], start=True, stop=True).then_inc(span_ps, 1)

        @block.vector
        def _(dve):
            own = g["dve_steps"]
            own.eng = dve
            dve.sem_inc(block_done, SL)
            dve.sem_inc(mask_ready, SL)
            dve.sem_inc(o_ready, 1)
            dve.wait_ge(dst_in, 32)
            own.do(dve.tensor_copy(bases_f[0:1, :], bases[0:1, 0:BLOCKS]))
            dve.sem_inc(bases_f_ready, 1)
            dve.wait_ge(pool_consts, 4)
            own.do(dve.tensor_copy(win, win_i))
            own.do(dve.memset(rel[:, BLOCKS * SUB:], -1.0))
            own.do(dve.tensor_copy(rel[:, 0:BLOCKS * SUB], dst_raw[:, 0:BLOCKS * SUB]))
            dve.wait_ge(bases_ps, 1)
            r0 = rel[:, 0:BLOCKS * SUB]
            r3 = r0.rearrange("p (b j) -> p b j", j=SUB)
            own.do(dve.tensor_tensor(r3, r3, bcast(ps_b[:, 0:BLOCKS], 2, SUB), ALU.subtract))

            def prepare(n, s):
                own.do(dve.tensor_tensor(mask[:, s], bcast(rel[:, bass.ds(n * SUB, SUB)], 2, WIN), bcast(win, 1, SUB),
                                         ALU.is_equal))
                dve.wait_ge(dwin_in[s], slot_count(n, s, 16))
                dve.tensor_tensor(dblk[:, s], bm, bcast(dwin[:, s, :], 1, SUB), ALU.mult).then_inc(mask_ready, 1)

            def logits(n, s):
                dve.wait_ge(gathered[s], slot_count(n, s, 64))
                dve.wait_ge(dlog_ps, n + 1)
                d8 = ps_s[s][:, P:P + SUB * 8].rearrange("p (j c) -> p j c", c=8)
                own.do(dve.tensor_tensor(z, rows[:, s, :, DIM:ROW], d8[:, :, 0:4], ALU.add))
                own.do(dve.scalar_tensor_tensor(out=lr, in0=z, scalar=SLOPE, in1=z, op0=ALU.mult, op1=ALU.max))
                dve.tensor_tensor(lg[:, s], lr, d8[:, :, 4:8], ALU.subtract).then_inc(logits_ready, 1)

            def weigh(n, s):
                dve.wait_ge(ex_ready, n + 1)
                for j in range(SUB):
                    m = dve.tensor_tensor(wts[:, s, j, :].rearrange("p (h w) -> p h w", h=G_HEADS),
                                          bcast(mask[:, s, j, :], 1, G_HEADS), bcast(ex[:, s, j, :], 2, WIN), ALU.mult)
                    if j < SUB - 1:
                        own.step(m)
                m.then_inc(w_ready, 1)

            def sum_weights(n, s):
                dve.wait_ge(w_ready, n + 1)
                dve.tensor_reduce(wsum[:, s, :], wts[:, s].rearrange("p j c -> p c j"), AX.X, ALU.add).then_inc(wsum_ready, 1)

            def accumulate(n, s):
                dve.wait_ge(block_ps, n + 1 + SL)
                dve.wait_ge(block_done, n + SL)
                base = dve.value_load(bases[0:1, at(n)], min_val=0, max_val=N_PAD)
                for half in range(2):
                    r = slice(64 * half, 64 * half + 64)
                    a = acc4[r, bass.ds(base, WIN), :].rearrange("p w c -> p c w")
                    m = dve.tensor_tensor(a, a, quads(ps_p[s], half), ALU.add)
                    if half == 0:
                        own.step(m)
                m.then_inc(block_done, 1)

            def body(n, s):
                logits(n, s)
                prepare(n + 1, (s + 1) % SL)
                weigh(n, s)
                if not isinstance(n, int) or n >= 2:
                    accumulate(n - 2, (s + 1) % SL)
                sum_weights(n, s)
            prepare(0, 0)
            logits(0, 0)
            prepare(1, 1)
            weigh(0, 0)
            sum_weights(0, 0)

            def mix(n):
                dve.wait_ge(o_ps, n + 1)
                if not isinstance(n, int) or n:
                    dve.wait_ge(o_out, n * 16)
                dve.tensor_tensor(o_row[:, :], ps_o[:, 0:DIM], mix_rows[:, 0, :], ALU.add).then_inc(o_ready, 1)
                dve.wait_ge(o_ready, n + 2)
                own.do(dve.bn_stats(st[:, at(n), :].squeeze(1), o_row[:, :]))

            def heads(q):
                return q.rearrange("p (h d) -> p h d", d=D_HEAD)

            def query_shift(n):
                q = heads(q_all[:, at(n), :].squeeze(1))
                own.do(dve.tensor_reduce(q_sum[:, 0, :], q, AX.X, ALU.max))
                dve.tensor_tensor(q, q, bcast(q_sum[:, 0, :], 2, D_HEAD), ALU.subtract).then_inc(q_shifted, 1)

            def query_norm(n):
                q = heads(q_all[:, at(n), :].squeeze(1))
                dve.wait_ge(q_exp, n + 1)
                dve.sem_inc(q_taken, 1)
                own.do(dve.tensor_reduce(q_sum[:, 1, :], q, AX.X, ALU.add))
                own.do(dve.reciprocal(q_sum[:, 1, :], q_sum[:, 1, :]))
                dve.wait_ge(qT_ps, n + 1)
                dve.scalar_tensor_tensor(out=heads(qn[:, :]), in0=q, scalar=D_HEAD ** -0.5,
                                         in1=bcast(q_sum[:, 1, :], 2, D_HEAD), op0=ALU.mult,
                                         op1=ALU.mult).then_inc(qn_ready, 1)

            def queries(tile):
                def extra(t, u):
                    if u == 0:
                        query_shift(tile)
                    elif u == 2:
                        query_norm(tile)
                return extra

            def row(tile):
                def extra(t, u):
                    if u == 1:
                        mix(tile)
                return extra

            def stage_1(t, u):
                row(t + 1)(t, u)
                queries(t + 3)(t, u)

            def stage_2(t, u):
                if u == 0:
                    dve.wait_ge(tile_in, 32 * t + 32)
                    own.do(dve.scalar_tensor_tensor(out=ob_in[:, 0, :], in0=ob_in[:, 0, :], scalar=s1[:, at(t)],
                                                    in1=mix_rows[:, 1, :], op0=ALU.mult, op1=ALU.mult))
                    dve.tensor_tensor(ob_in[:, 1, :], ob_in[:, 1, :], ob_in[:, 0, :], ALU.add).then_inc(base_ready, 1)
            OWN = 2 + 1 + 3 + 1
            dve.wait_ge(zeroed_a, 1)
            for n in range(2 * SL):
                body(1 + n, (1 + n) % SL)
                queries(n // SL)(0, n % SL)
            rounds(dve, own, 1 + 2 * SL, 1, SL, OWN, body, lambda t, u: (row(0)(t, u), queries(2)(t, u)), (1, 1, 2))
            rounds(dve, own, 1 + 3 * SL, TILES - 3, SL, OWN, body, stage_1, (1, 1, 2))
            for n in range(2):
                rounds(dve, own, PAUSE - (2 - n) * SL, 1, SL, OWN, body, row(TILES - 2 + n), (0, 1, 0))
            join_moments(dve, own, st, mv, s1)
            own.do(dve.tensor_tensor(s1[:, :], mv[:, :, 0], mv[:, :, 0], ALU.mult))
            own.do(dve.tensor_tensor(s1[:, :], s1[:, :], mv[:, :, 1], ALU.add))
            own.do(dve.tensor_scalar(s1[:, :], s1[:, :], float(DIM), 1e-24, ALU.mult, ALU.max))
            dve.sem_inc(ss_ready, 1)
            repeat(dve, own, PAUSE, SECOND, SL, OWN, body)
            b0, c0 = bad[:, 0:BLOCKS * SUB], badc[:, 0:BLOCKS * SUB]
            own.do(dve.tensor_copy(c0, dst_raw[:, 0:BLOCKS * SUB]))
            own.do(dve.tensor_scalar(c0, c0, float(N_NODES), None, ALU.is_lt))
            dve.wait_ge(ss_sqrt, 1)
            own.do(dve.reciprocal(s1[:, :], s2[:, :]))
            own.do(dve.tensor_scalar(s1[:, :], s1[:, :], 16.0, None, ALU.mult))
            rounds(dve, own, SECOND, TILES, SL, OWN, body, stage_2, (1, 0, 0))
            own.do(dve.scalar_tensor_tensor(out=b0, in0=r0, scalar=float(WIN), in1=c0, op0=ALU.is_ge, op1=ALU.mult))
            own.do(dve.scalar_tensor_tensor(out=c0, in0=r0, scalar=0.0, in1=c0, op0=ALU.is_lt, op1=ALU.mult))
            repeat(dve, own, THIRD, THIRD + 2 * SL, SL, OWN, body)
            own.do(dve.tensor_tensor_reduce(b0, b0, c0, 1.0, 0.0, ALU.add, ALU.add, badn[:, 0:1]))
            repeat(dve, own, THIRD + 2 * SL, BLOCKS, SL, OWN, body)
            for n in range(BLOCKS - 2, BLOCKS):
                accumulate(n, n % SL)
            dve.sem_inc(span_ready, 1)
            dve.wait_ge(span_ps, 1)
            own.do(dve.tensor_copy(spans[0:1, 0:1], ps_b[0:1, 0:1]))


def any_order_stage(nc, g):
    e = g["edge_buffers"]
    acc, ident, ones, spans = (g[k] for k in ("acc", "ident", "ones", "spans"))
    table, dst_table = g["table"], g["dst_table"]
    src_idx, idx, dst_raw, rel, rows, mask, maskT, dwin, dblk, wts, wsum, lg, ex, z, lr, win, bm = (e[k] for k in (
        "src_idx", "idx", "dst_raw", "rel", "rows", "mask", "maskT", "dwin", "dblk", "wts", "wsum", "lg", "ex",
        "z", "lr", "win", "bm"))
    acc4 = acc[:, :].rearrange("p (w c) -> p w c", c=4)

    with ExitStack() as ctx:
        ps_p = ctx.enter_context(nc.psum_tensor("ps_ap", [P, 512], F32))
        ps_s = ctx.enter_context(nc.psum_tensor("ps_as", [P, 512], F32))
        (own_v, zeroed, indexed, slots_open, gathered, windowed, masked, mask_ps, mask_back, dlog_ps, lg_ready,
         ex_ready, w_ready, sum_ps, summed, shifted) = (ctx.enter_context(nc.semaphore("any_" + n)) for n in (
             "own_v", "zeroed", "indexed", "slots_open", "gathered", "windowed", "masked", "mask_ps", "mask_back",
             "dlog_ps", "lg_ready", "ex_ready", "w_ready", "sum_ps", "summed", "shifted"))
        block = ctx.enter_context(nc.Block())

        def steps(eng, body):
            outside = eng.value_load(spans[0:1, 0:1], min_val=0, max_val=N_EDGES)
            with eng.If(outside > 0):
                if eng is nc.vector or eng is nc.scalar:
                    body(None, None, None)
                with eng.Fori(0, WINDOWS) as v:
                    if eng is nc.vector:
                        body(None, v, None)
                    with eng.Fori(0, BLOCKS) as n:
                        body(v * BLOCKS + n, v, n)

        @block.sync
        def _(sp):
            def body(m, v, n):
                sp.wait_ge(summed, m + 1)
                sp.dma_start(dwin[:, 0, :], bcast(dst_table[at(v, WIN), :], 0, SUB)).then_inc(windowed, 16)
            steps(sp, body)

        @block.gpsimd
        def _(pool):
            def body(m, v, n):
                pool.wait_ge(indexed, m + 1)
                pool.sem_inc(slots_open, 1)
                for j in range(SUB):
                    pool.indirect_dma_start(
                        out=rows[:, 0, j, :], out_offset=None, in_=table[:, :],
                        in_offset=bass.IndirectOffsetOnAxis(ap=idx[:, j:j + 1], axis=0)).then_inc(gathered, 16)
            steps(pool, body)

        @block.scalar
        def _(act):
            def body(m, v, n):
                if m is None:
                    act.memzero(acc[:, ACC_W * 2:]).then_inc(zeroed, 1)
                    return
                act.wait_ge(summed, m + 1)
                act.activation(idx[:, 0:SUB], src_idx[:, at(n, SUB)], ACT.Copy).then_inc(indexed, 1)
                act.wait_ge(mask_ps, m + 1)
                act.activation(maskT[:, 0, :], ps_s[:, 0:P], ACT.Copy).then_inc(mask_back, 1)
                act.wait_ge(lg_ready, m + 1)
                act.activation(ex[:, 0], lg[:, 0], ACT.Exp).then_inc(ex_ready, 1)
            steps(act, body)

        @block.tensor
        def _(pe):
            def body(m, v, n):
                pe.wait_ge(masked, m + 1)
                pe.transpose(ps_s[:, 0:P], mask[:, 0].rearrange("p j w -> p (j w)"), ident[:, :]).then_inc(mask_ps, 1)
                pe.wait_ge(mask_back, m + 1)
                pe.matmul(ps_s[:, P:P + SUB * 8], maskT[:, 0, :], dblk[:, 0].rearrange("p j c -> p (j c)"),
                          start=True, stop=True).then_inc(dlog_ps, 1)
                pe.wait_ge(w_ready, m + 1)
                for y in range(2):
                    for j in range(SUB):
                        pe.matmul(ps_p[:, y * P:(y + 1) * P], rows[:, 0, j, y * P:(y + 1) * P], wts[:, 0, j, :],
                                  start=j == 0, stop=j == SUB - 1)
                pe.matmul(strided(ps_p, 2 * P, 192), ones[:, :], wsum[:, 0].rearrange("p (a b) -> p a b", a=2),
                          start=True, stop=True).then_inc(sum_ps, 1)
            steps(pe, body)

        @block.vector
        def _(dve):
            own = Own(dve, own_v)
            OWN = 1 + 2 + SUB + 1

            def body(m, v, n):
                if v is None:
                    dve.sem_inc(summed, 1)
                    own.do(dve.tensor_scalar(win, win, float(-WIN), None, ALU.add))
                    own.do(dve.tensor_copy(rel[:, 0:BLOCKS * SUB], dst_raw[:, 0:BLOCKS * SUB]))
                    own.do(dve.memset(acc[:, 0:ACC_W * 2], 0.0))
                    dve.wait_ge(zeroed, 1)
                    own.start = own.k
                    return
                if n is None:
                    own.base, own.k = own.start + v * (BLOCKS * OWN + 1), 0
                    own.do(dve.tensor_scalar(win, win, float(WIN), None, ALU.add))
                    own.inner = own.base + 1
                    dve.sem_inc(shifted, 1)
                    return
                own.base, own.k = own.inner + n * OWN, 0
                own.do(dve.tensor_tensor(mask[:, 0], bcast(rel[:, bass.ds(n * SUB, SUB)], 2, WIN), bcast(win, 1, SUB),
                                         ALU.is_equal))
                dve.wait_ge(windowed, m * 16 + 16)
                dve.tensor_tensor(dblk[:, 0], bm, bcast(dwin[:, 0, :], 1, SUB), ALU.mult).then_inc(masked, 1)
                dve.wait_ge(gathered, m * 64 + 64)
                dve.wait_ge(dlog_ps, m + 1)
                d8 = ps_s[:, P:P + SUB * 8].rearrange("p (j c) -> p j c", c=8)
                own.do(dve.tensor_tensor(z, rows[:, 0, :, DIM:ROW], d8[:, :, 0:4], ALU.add))
                own.do(dve.scalar_tensor_tensor(out=lr, in0=z, scalar=SLOPE, in1=z, op0=ALU.mult, op1=ALU.max))
                dve.tensor_tensor(lg[:, 0], lr, d8[:, :, 4:8], ALU.subtract).then_inc(lg_ready, 1)
                dve.wait_ge(ex_ready, m + 1)
                for j in range(SUB):
                    own.step(dve.tensor_tensor(wts[:, 0, j, :].rearrange("p (h w) -> p h w", h=G_HEADS),
                                               bcast(mask[:, 0, j, :], 1, G_HEADS), bcast(ex[:, 0, j, :], 2, WIN), ALU.mult))
                own.wait()
                dve.tensor_reduce(wsum[:, 0, :], wts[:, 0].rearrange("p j c -> p c j"), AX.X, ALU.add).then_inc(w_ready, 1)
                dve.wait_ge(sum_ps, m + 1)
                for half in range(2):
                    a = acc4[64 * half:64 * half + 64, at(v, WIN), :].rearrange("p w c -> p c w")
                    ins = dve.tensor_tensor(a, a, quads(ps_p, half), ALU.add)
                    if half == 0:
                        own.step(ins)
                ins.then_inc(summed, 1)
                assert own.k == OWN, own.k
            steps(dve, body)


def slot_count(n, s, inc, slots=3):
    return (n - s + slots) * inc // slots


def strided(ps, start, step):
    v = ps[:, start:start + 64]
    return bass.AP(v.tensor, v.offset, [list(v.ap[0]), [step, 2], [1, 64]])


def quads(ps, half):
    v = ps[64 * half:64 * half + 64, 32 * half:32 * half + 32]
    return bass.AP(v.tensor, v.offset, [list(v.ap[0]), [256, 2], [192, 2], [1, 32]])


def rows_stage(nc, g):
    acc, ident, ones, valid, w_self, region = (g[k] for k in ("acc", "ident", "ones", "valid", "w_self", "region"))
    table, base_rows, sum_rows, expert_in = (g[k] for k in ("table", "base_rows", "sum_rows", "expert_in"))
    acc4 = acc[:, :].rearrange("p (w c) -> p w c", c=4)
    w1_sb, w2_sb, b1_sb, b2_sb, affine, tile_expert, tile_start = (g[k] for k in (
        "w1_sb", "w2_sb", "b1_sb", "b2_sb", "affine", "tile_expert", "tile_start"))
    GE = GT * EXPERTS

    with ExitStack() as ctx:
        def sb(name, shape, dt=F32):
            return ctx.enter_context(nc.sbuf_tensor(name, shape, dt))

        def sem(name):
            return ctx.enter_context(nc.semaphore(name))

        def te(name):
            return sb(name, [P, GE])[:, :].rearrange("p (t e) -> p t e", e=EXPERTS)

        sent_rows = region[:, g["SENT_AT"]:g["SENT_AT"] + 2 * GT * 2 * MROW].rearrange(
            "p (s t k c) -> p s t k c", s=2, t=GT, k=2)
        free = g["SENT_AT"] + 2 * GT * 2 * MROW
        xT = region[:, free:free + 2 * DIM].rearrange("p (s c) -> p s c", s=2)
        planes = sb("planes", [P, 2, 4, P])
        h_in, b_in = sb("h_in", [P, GT, DIM]), sb("b_in", [P, GT, DIM])
        rl = sb("rl", [P, 2, G_HEADS])
        st, mv = sb("st2", [P, TILES, 6]), sb("mv2", [P, TILES, 2])
        scale, shift, sdev = sb("scale2", [P, TILES]), sb("shift2", [P, TILES]), sb("sdev2", [P, GT])
        eps = sb("eps2", [P, 1])
        wr, brow = sb("wr", [P, KC * EXPERTS]), sb("brow", [P, EXPERTS])
        pad_rows = sb("pad_rows", [P, MROW])
        token_i, token = sb("token_i", [P, TILES + 1], I32), sb("token", [P, TILES + 1])
        before = sb("before", [P, P])
        tmp = g["ye_sb"].rearrange("p (s d) -> p s d", s=2)
        rank_i, rank = sb("rank_i", [P, EXPERTS], I32), sb("rank", [P, EXPERTS])
        tau_i, tau = sb("tau_i", [1, MOE_TILES], I32), sb("tau", [1, 2, MOE_TILES])
        le = sb("le", [1, MOE_TILES * EXPERTS])
        lg, first, second, both, work, pos = (te(n) for n in ("lg2", "first", "second", "both_", "work", "pos"))
        total_et, upto_et, mask_et = (sb(n, [P, GE]) for n in ("total_et", "upto_et", "mask_et"))
        taken = sb("taken", [P, EXPERTS])
        cap_i, cap = sb("cap_i", [P, EXPERTS], I32), sb("cap", [P, EXPERTS])
        top, t1, gate = sb("top", [P, 2, GT]), sb("t1", [P, GT]), sb("gate2", [P, GT])
        place = sb("place", [P, 2, 2, GT], I32)
        cnt, cnt_i, pad_at = sb("cnt", [P, 3, EXPERTS]), sb("cnt_i", [P, EXPERTS], I32), sb("pad_at", [1, EXPERTS], I32)
        ps_t = [ctx.enter_context(nc.psum_tensor(f"ps_r{i}", [P, 512], F32)) for i in range(4)]
        ps_x = [ctx.enter_context(nc.psum_tensor(f"ps_rx{i}", [P, 512], F32)) for i in range(2)]
        ps_l = ctx.enter_context(nc.psum_tensor("ps_rl", [P, 512], F32))
        ps_c = ctx.enter_context(nc.psum_tensor("ps_rc", [P, 512], F32))

        loads, own_p, consts, sent, ring_free = (sem(n) for n in ("loads2", "own_p4", "consts4", "sent", "ring_free"))
        weights_in = g["weights_in"]
        row_in = [sem(f"row_in{i}") for i in range(GT)]
        (planes_ready, planes_ps, self_ready, x1_ready, x1_out, var_ready, dev_ready, scale_ready, n_ready, n_ps,
         nT_ready, l_ps, l_taken, picked, counted, exp_in, exp_out, routed, padded, pads_out, pads_ready) = (
             sem("rows_" + n) for n in (
                 "planes_ready", "planes_ps", "self_ready", "x1_ready", "x1_out", "var_ready", "dev_ready",
                 "scale_ready", "n_ready", "n_ps", "nT_ready", "l_ps", "l_taken", "picked", "counted", "exp_in",
                 "exp_out", "routed", "padded", "pads_out", "pads_ready"))
        block = ctx.enter_context(nc.Block())

        def x1_of(n):
            return acc[:, bass.ds(n * 4 * P + DIM, DIM)]

        @block.sync
        def _(sp):
            sp.wait_ge(pads_ready, 1)
            sp.dma_start(expert_in[EXPERTS * CAP:, :].rearrange("(t p) d -> p t d", p=P),
                         bcast(pad_rows[:, :], 1, EXPERTS)).then_inc(pads_out, 16)

            def load(gr, j):
                n = gr * GT + j
                sp.wait_ge(x1_ready, n + 1)
                sp.dma_start(h_in[:, j, :], table[at(n, P), 0:DIM]).then_inc(row_in[j], 16)
                sp.dma_start(b_in[:, j, :], base_rows[at(n, P), :]).then_inc(row_in[j], 16)

            def store(gr, j):
                n = gr * GT + j
                sp.wait_ge(x1_ready, n + 1 + GT)
                sp.dma_start(sum_rows[at(n, P), :], x1_of(n)).then_inc(x1_out, 16)

            def body(gr, s):
                for j in range(GT):
                    load(gr, j)
                    store(gr - 1, j)
            for j in range(GT):
                load(0, j)
            repeat(sp, Own(sp, None), 1, GROUPS, 2, 0, body)
            for j in range(GT):
                store(GROUPS - 1, j)
            sp.wait_ge(x1_out, 16 * TILES)
            sp.wait_ge(n_ready, (GROUPS - 1) * GT)
            sp.dma_start(b1_sb, g["b1"].rearrange("e f -> (e f)").partition_broadcast(P)).then_inc(weights_in, 16)
            for e in range(EXPERTS):
                sp.dma_start(w2_sb[:, e], g["W2"][e].rearrange("(c p) d -> p c d", p=P)).then_inc(weights_in, 16)
            sp.wait_ge(padded, 1)
            for e in range(EXPERTS):
                v = sp.value_load(pad_at[0:1, e:e + 1], min_val=0, max_val=EXPERTS * CAP - P)
                sp.dma_start(expert_in[bass.ds(v, P), :], pad_rows[:, :]).then_inc(pads_out, 16)
            sp.wait_ge(pads_out, 16 * (1 + EXPERTS))

        @block.gpsimd
        def _(pool):
            pool.memset(pad_rows[:, :], 0.0).then_inc(consts, 1)
            pool.iota(token_i[:, :], [[P, TILES + 1]], base=0, channel_multiplier=1).then_inc(consts, 1)
            pool.memset(before[:, :], 1.0).then_inc(own_p, 1)
            pool.iota(rank_i[:, :], [[-1, EXPERTS]], base=EXPERTS, channel_multiplier=0).then_inc(consts, 1)
            pool.iota(tau_i[:, :], [[1, MOE_TILES]], base=0, channel_multiplier=0).then_inc(consts, 1)
            pool.iota(cap_i[:, :], [[CAP, EXPERTS]], base=0, channel_multiplier=0).then_inc(consts, 1)
            pool.wait_ge(own_p, 1)
            pool.affine_select(out=before[:, :], in_=before[:, :], compare_op=ALU.is_gt, fill=0.0, base=0,
                               pattern=[[1, P]], channel_multiplier=-1).then_inc(consts, 1)

            def self_row(gr, j):
                n = gr * GT + j
                pool.wait_ge(row_in[j], gr * 32 + 32)
                hh = h_in[:, j, :].rearrange("p (h f) -> p h f", f=F_HEAD)
                pool.tensor_tensor(hh, hh, bcast(w_self[:, at(n, G_HEADS)], 2, F_HEAD), ALU.mult).then_inc(self_ready, 1)

            def send(gr, s, j, rows=P):
                if j == 0:
                    pool.wait_ge(routed, gr + 1)
                    pool.sem_inc(own_p, 1)
                for k in range(2):
                    pool.indirect_dma_start(
                        out=expert_in[:, :], out_offset=bass.IndirectOffsetOnAxis(ap=place[0:rows, s, k, j:j + 1], axis=0),
                        in_=sent_rows[0:rows, s, j, k, :], in_offset=None).then_inc(sent, 16)

            def group_sent(gr):
                pool.wait_ge(sent, (gr + 1) * (32 * GT))
                pool.sem_inc(ring_free, 1)

            AHEAD = 4

            def body(gr, s):
                for j in range(AHEAD):
                    self_row(gr, j)
                for j in range(GT):
                    send(gr - 2, s, j)
                    if j + AHEAD < GT:
                        self_row(gr, j + AHEAD)
                group_sent(gr - 2)
            for gr in range(2):
                for j in range(GT):
                    self_row(gr, j)
            repeat(pool, Own(pool, None), 2, GROUPS, 2, 0, body)
            for gr in range(GROUPS - 2, GROUPS):
                for j in range(GT):
                    send(gr, gr % 2, j, P if gr * GT + j < TILES - 1 else LAST)
                group_sent(gr)

        @block.scalar
        def _(act):
            act.dma_start(brow[:, :], g["br"].partition_broadcast(P)).then_inc(loads, 16)
            act.dma_start(wr[:, :].rearrange("p (c e) -> p c e", e=EXPERTS),
                          g["Wr"].rearrange("(c p) e -> p c e", p=P)).then_inc(loads, 16)
            for i, a in enumerate(("gamma", "beta")):
                act.dma_start(affine[:, i, :], g[a].rearrange("(c p) -> p c", p=P),
                              allow_slow_non_contiguous=True).then_inc(loads, 16)

            def gather_planes(n, s):
                act.wait_ge(planes_ps, n + 1)
                act.activation(planes[:, s], acc4[:, at(n, P), :].rearrange("p w c -> p c w"), ACT.Copy).then_inc(
                    planes_ready, 1)

            def norm(gr, s, j):
                n = gr * GT + j
                if j == 0:
                    act.wait_ge(scale_ready, gr + 1)
                    act.wait_ge(ring_free, gr + 1)
                act.activation(sent_rows[:, s, j, :, 0:DIM], bcast(x1_of(n), 1, 2), ACT.Identity,
                               bias=shift[:, at(n)], scale=scale[:, at(n)]).then_inc(n_ready, 1)

            def rows_back(gr, s, j):
                n, x = gr * GT + j, (s + j) % 2
                act.wait_ge(n_ps, n + 1)
                for c in range(KC):
                    m = act.activation(xT[:, x, c * P:(c + 1) * P], ps_x[x][:, c * P:(c + 1) * P], ACT.Identity,
                                       bias=affine[:, 1, c:c + 1], scale=affine[:, 0, c:c + 1])
                m.then_inc(nT_ready, 1)

            def deviation(gr):
                act.wait_ge(var_ready, gr + 1)
                act.activation(sdev[:, :], mv[:, at(gr, GT), 1], ACT.Sqrt, bias=eps[:, 0:1],
                               scale=1.0 + LN_EPS).then_inc(dev_ready, 1)

            def gates(gr):
                act.wait_ge(exp_in, gr + 1)
                act.activation(t1[:, :], t1[:, :], ACT.Exp).then_inc(exp_out, 1)

            def body(gr, s):
                gather_planes(gr * GT, s % 2)
                for j in range(GT):
                    if j < GT - 1:
                        gather_planes(gr * GT + j + 1, (s + j + 1) % 2)
                    norm(gr - 1, 1 - s, j)
                    if j:
                        rows_back(gr - 1, 1 - s, j - 1)
                rows_back(gr - 1, 1 - s, GT - 1)
                deviation(gr)
                gates(gr - 1)
            for j in range(GT):
                gather_planes(j, j % 2)
            deviation(0)
            act.dma_start(b2_sb, g["b2"].rearrange("e f -> (e f)").partition_broadcast(P)).then_inc(weights_in, 16)
            for e in range(EXPERTS):
                act.dma_start(w1_sb[:, e], g["W1"][e].rearrange("(c p) f -> p c f", p=P)).then_inc(weights_in, 16)
            act.wait_ge(loads, 64)
            repeat(act, Own(act, None), 1, GROUPS, 2, 0, body)
            last, s = GROUPS - 1, (GROUPS - 1) % 2
            for j in range(GT):
                norm(last, s, j)
                if j:
                    rows_back(last, s, j - 1)
            rows_back(last, s, GT - 1)
            gates(last)

        @block.tensor
        def _(pe):
            pe.sem_inc(planes_ps, 2)

            def sums(gr, s, j):
                n, s = gr * GT + j, (s + j) % 2
                pe.wait_ge(planes_ready, n + 1)
                pe.wait_ge(x1_ready, n + 1 + GT - (4 if j > 3 else 7 if j == 3 else 3))
                for c in range(4):
                    m = pe.transpose(ps_t[j % 4][:, c * P:(c + 1) * P], planes[:, s, c, :], ident[:, :])
                m.then_inc(planes_ps, 1)

            def rows_across(gr, s, j):
                n, x = gr * GT + j, (s + j) % 2
                pe.wait_ge(n_ready, n + 1)
                pe.wait_ge(nT_ready, n + 1)
                for c in range(KC):
                    m = pe.transpose(ps_x[x][:, c * P:(c + 1) * P], sent_rows[:, s, j, 0, c * P:(c + 1) * P], ident[:, :])
                m.then_inc(n_ps, 1)

            def router(gr, s, j):
                n, x = gr * GT + j, (s + j) % 2
                pe.wait_ge(nT_ready, n + 3)
                if j == 0:
                    pe.wait_ge(l_taken, gr + 1)
                for c in range(KC):
                    m = pe.matmul(ps_l[:, j * EXPERTS:(j + 1) * EXPERTS], xT[:, x, c * P:(c + 1) * P],
                                  wr[:, c * EXPERTS:(c + 1) * EXPERTS], start=c == 0, stop=c == KC - 1)
                if j == GT - 1:
                    m.then_inc(l_ps, 1)

            def count(gr):
                pe.wait_ge(picked, gr + 1)
                b = both.rearrange("p t e -> p (t e)")
                pe.matmul(ps_c[:, 0:GE], before[:, :], b, start=True, stop=True)
                pe.matmul(ps_c[:, DIM:DIM + GE], ones[:, :], b, start=True, stop=True).then_inc(counted, 1)

            def body(gr, s):
                sums(gr, s, 0)
                for j in range(GT):
                    if j < GT - 1:
                        sums(gr, s, j + 1)
                    rows_across(gr - 1, 1 - s, j)
                    if j:
                        router(gr - 1, 1 - s, j - 1)
                router(gr - 1, 1 - s, GT - 1)
                count(gr - 1)
            for j in range(GT):
                sums(0, 0, j)
            pe.wait_ge(loads, 64)
            pe.wait_ge(consts, 6)
            repeat(pe, Own(pe, None), 1, GROUPS, 2, 0, body)
            last, s = GROUPS - 1, (GROUPS - 1) % 2
            for j in range(GT):
                rows_across(last, s, j)
                if j:
                    router(last, s, j - 1)
            router(last, s, GT - 1)
            count(last)

        @block.vector
        def _(dve):
            own = g["dve_steps"]
            own.eng = dve
            dve.sem_inc(x1_ready, GT)
            dve.sem_inc(nT_ready, 2)
            dve.sem_inc(l_taken, 1)
            dve.sem_inc(ring_free, 2)
            own.do(dve.memset(eps[:, :], LN_EPS * LN_EPS))
            dve.wait_ge(consts, 6)
            own.do(dve.tensor_copy(token[:, :], token_i[:, :]))
            own.do(dve.tensor_copy(pad_rows[:, DIM:DIM + 1], token[:, TILES:TILES + 1]))
            dve.sem_inc(pads_ready, 1)
            own.do(dve.tensor_copy(rank[:, :], rank_i[:, :]))
            own.do(dve.tensor_copy(tau[:, 0, :], tau_i[:, :]))
            own.do(dve.tensor_copy(cap[:, :], cap_i[:, :]))
            own.do(dve.tensor_copy(taken[:, :], cap_i[:, :]))
            own.do(dve.memset(mask_et[:, :], 1.0))
            own.do(dve.memset(mask_et[:, :].rearrange("p (e t) -> p e t", t=GT)[:, :, 0:1], 0.0))

            def heads(ap):
                return ap.rearrange("p (h f) -> p h f", f=F_HEAD)

            def attended(gr, s, js):
                def tile(j):
                    return gr * GT + j, (s + j) % 2
                dve.wait_ge(planes_ps, tile(js[-1])[0] + 3)
                for j in js:
                    n, x = tile(j)
                    own.step(dve.tensor_tensor(rl[:, x, :], heads(ps_t[j % 4][:, DIM:2 * DIM])[:, :, 0],
                                               w_self[:, at(n, G_HEADS)], ALU.add))
                own.wait()
                for j in js:
                    n, x = tile(j)
                    own.step(dve.reciprocal(rl[:, x, :], rl[:, x, :]))
                dve.wait_ge(self_ready, tile(js[-1])[0] + 1)
                for j in js:
                    n, x = tile(j)
                    own.step(dve.tensor_tensor(tmp[:, x, :], h_in[:, j, :], ps_t[j % 4][:, 0:DIM], ALU.add))
                own.wait()
                for j in js:
                    n, x = tile(j)
                    own.step(dve.tensor_tensor(heads(tmp[:, x, :]), heads(tmp[:, x, :]), bcast(rl[:, x, :], 2, F_HEAD),
                                               ALU.mult))
                own.wait()
                for j in js:
                    n, x = tile(j)
                    own.step(dve.tensor_tensor(x1_of(n), tmp[:, x, :], b_in[:, j, :], ALU.add))
                own.wait()
                for j in js:
                    n, x = tile(j)
                    dve.bn_stats(st[:, at(n), :].squeeze(1), x1_of(n)).then_inc(x1_ready, 1)

            def all_attended(gr, s):
                for j in range(0, GT, 2):
                    attended(gr, s, tuple(range(j, min(j + 2, GT))))

            def moments(gr):
                dve.wait_ge(x1_ready, (gr + 2) * GT)
                join_moments(dve, own, st[:, at(gr, GT), :], mv[:, at(gr, GT), :], shift[:, at(gr, GT)])
                dve.sem_inc(var_ready, 1)

            def scales(gr):
                dve.wait_ge(dev_ready, gr + 1)
                own.do(dve.reciprocal(scale[:, at(gr, GT)], sdev[:, :]))
                own.do(dve.scalar_tensor_tensor(out=shift[:, at(gr, GT)], in0=mv[:, at(gr, GT), 0], scalar=-1.0,
                                                in1=scale[:, at(gr, GT)], op0=ALU.mult, op1=ALU.mult))
                dve.sem_inc(scale_ready, 1)

            def pick(values, k, onehot):
                own.do(dve.tensor_reduce(top[:, k, :], values, AX.X, ALU.max))
                own.do(dve.tensor_tensor(work, values, bcast(top[:, k, :], 2, EXPERTS), ALU.is_equal))
                own.do(dve.tensor_tensor(work, work, bcast(rank[:, :], 1, GT), ALU.mult))
                own.do(dve.tensor_reduce(gate[:, :], work, AX.X, ALU.max))
                own.do(dve.tensor_tensor(onehot, bcast(rank[:, :], 1, GT), bcast(gate[:, :], 2, EXPERTS), ALU.is_equal))

            def route(gr, s):
                dve.wait_ge(l_ps, gr + 1)
                own.do(dve.tensor_tensor(lg, ps_l[:, 0:GE].rearrange("p (t e) -> p t e", e=EXPERTS),
                                         bcast(brow[:, :], 1, GT), ALU.add))
                dve.sem_inc(l_taken, 1)
                pick(lg, 0, first)
                own.do(dve.scalar_tensor_tensor(out=pos, in0=first, scalar=-3e38, in1=lg, op0=ALU.mult, op1=ALU.add))
                pick(pos, 1, second)
                own.do(dve.tensor_tensor(both, first, second, ALU.add))
                own.do(dve.tensor_tensor(both, both, bcast(valid[:, at(gr, GT)], 2, EXPERTS), ALU.mult))
                dve.sem_inc(picked, 1)
                own.do(dve.tensor_tensor(t1[:, :], top[:, 1, :], top[:, 0, :], ALU.subtract))
                dve.sem_inc(exp_in, 1)
                dve.wait_ge(counted, gr + 1)
                total = ps_c[:, DIM:DIM + GE].rearrange("p (t e) -> p t e", e=EXPERTS)
                upto = upto_et[:, :].rearrange("p (e t) -> p e t", t=GT)
                own.do(dve.tensor_copy(total_et[:, :].rearrange("p (e t) -> p e t", t=GT),
                                       total.rearrange("p t e -> p e t")))
                own.do(dve.tensor_tensor_scan(upto_et[:, :], mask_et[:, :], total_et[:, :], 0.0, ALU.mult, ALU.add))
                own.do(dve.tensor_tensor(pos, upto.rearrange("p e t -> p t e"), total, ALU.subtract))
                own.do(dve.tensor_tensor(pos, pos, ps_c[:, 0:GE].rearrange("p (t e) -> p t e", e=EXPERTS), ALU.add))
                own.do(dve.tensor_tensor(pos, pos, bcast(taken[:, :], 1, GT), ALU.add))
                own.do(dve.tensor_tensor(taken[:, :], taken[:, :], upto[:, :, GT - 1], ALU.add))
                for k, oh in enumerate((first, second)):
                    own.do(dve.tensor_tensor(work, oh, pos, ALU.mult))
                    own.do(dve.tensor_reduce(top[:, k, :], work, AX.X, ALU.add))
                own.do(dve.tensor_copy(place[:, s], top[:, :, :]))
                own.do(dve.tensor_copy(sent_rows[:, s, :, :, DIM], bcast(token[:, at(gr, GT)], 2, 2)))
                dve.wait_ge(exp_out, gr + 1)
                own.do(dve.tensor_scalar(gate[:, :], t1[:, :], 1.0, None, ALU.add))
                own.do(dve.reciprocal(sent_rows[:, s, :, 0, DIM + 1], gate[:, :]))
                own.do(dve.tensor_tensor(sent_rows[:, s, :, 1, DIM + 1], sent_rows[:, s, :, 0, DIM + 1], t1[:, :],
                                         ALU.mult))
                dve.sem_inc(routed, 1)

            def body(gr, s):
                all_attended(gr, s)
                moments(gr)
                route(gr - 1, 1 - s)
                scales(gr)
            all_attended(0, 0)
            moments(0)
            scales(0)
            dve.wait_ge(loads, 64)
            STEPS = 5 * GT + 6 + 2 + 1 + 5 + 1 + 5 + 2 + 1 + 6 + 4 + 2 + 3
            repeat(dve, own, 1, GROUPS - 1, 2, STEPS, body)
            all_attended(GROUPS - 1, (GROUPS - 1) % 2)
            moments(GROUPS - 1)
            scales(GROUPS - 1)
            route(GROUPS - 2, (GROUPS - 2) % 2)
            route(GROUPS - 1, (GROUPS - 1) % 2)
            own.do(dve.tensor_copy(pad_at[0:1, :], taken[0:1, :]))
            dve.sem_inc(padded, 1)
            own.do(dve.tensor_tensor(cnt[:, 0, :], taken[:, :], cap[:, :], ALU.subtract))
            own.do(dve.tensor_scalar(cnt_i[:, :], cnt[:, 0, :], float(P - 1), None, ALU.add))
            own.do(dve.tensor_scalar(cnt_i[:, :], cnt_i[:, :], P.bit_length() - 1, None, ALU.arith_shift_right))
            own.do(dve.tensor_copy(cnt[:, 0, :], cnt_i[:, :]))
            own.do(dve.memset(work, 1.0))
            own.do(dve.tensor_tensor_scan(cnt[:, 1, :], work[:, 0, :], cnt[:, 0, :], 0.0, ALU.mult, ALU.add))
            own.do(dve.tensor_scalar(cnt[:, 2, :], cnt[:, 0, :], float(-P), float(CAP), ALU.mult, ALU.add))
            l3 = le[:, :].rearrange("p (t e) -> p t e", e=EXPERTS)
            own.do(dve.tensor_tensor(l3, bcast(cnt[0:1, 1, :], 1, MOE_TILES), bcast(tau[:, 0, :], 2, EXPERTS), ALU.is_le))
            own.do(dve.tensor_reduce(tau[:, 1, :], l3, AX.X, ALU.add))
            own.do(dve.tensor_scalar(tile_expert[0:1, :], tau[:, 1, :], float(EXPERTS - 1), None, ALU.min))
            own.do(dve.tensor_tensor(l3, l3, bcast(cnt[0:1, 2, :], 1, MOE_TILES), ALU.mult))
            own.do(dve.tensor_reduce(tau[:, 1, :], l3, AX.X, ALU.add))
            own.do(dve.scalar_tensor_tensor(out=tile_start[0:1, :], in0=tau[:, 0, :], scalar=float(P), in1=tau[:, 1, :],
                                            op0=ALU.mult, op1=ALU.add))


def expert_stage(nc, g):
    ident, affine = g["ident"], g["affine"]
    w1_sb, w2_sb, b1_sb, b2_sb, weights_in = (g[k] for k in ("w1_sb", "w2_sb", "b1_sb", "b2_sb", "weights_in"))
    tile_expert, tile_start = g["tile_expert"], g["tile_start"]
    expert_in, sum_rows, out = g["expert_in"], g["sum_rows"], g["out"]
    T = MOE_TILES
    XS = 4

    with ExitStack() as ctx:
        def sb(name, shape, dt=F32):
            return ctx.enter_context(nc.sbuf_tensor(name, shape, dt))

        def sem(name):
            return ctx.enter_context(nc.semaphore(name))

        xe = sb("xe", [P, XS, MROW])
        xeT = sb("xeT", [P, 2, DIM])
        hid = sb("hid", [P, 2, FF])
        hidT = sb("hidT", [P, 2, FF])
        y = sb("y", [P, 2, DIM])
        gates = sb("gates", [P, XS])
        rows_of = sb("rows_of", [P, XS], I32)
        ye = g["ye_sb"].rearrange("p (s d) -> p s d", s=2)
        ps_x = [ctx.enter_context(nc.psum_tensor(f"ps_ex{i}", [P, 512], F32)) for i in range(2)]
        ps_y = [ctx.enter_context(nc.psum_tensor(f"ps_ey{i}", [P, 512], F32)) for i in range(2)]
        ps_u = [ctx.enter_context(nc.psum_tensor(f"ps_eu{i}", [P, FF], F32)) for i in range(2)]
        ps_g = [ctx.enter_context(nc.psum_tensor(f"ps_eg{i}", [P, FF], F32)) for i in range(2)]
        xe_in = [sem(f"xe_in{i}") for i in range(XS)]
        (xe_ps, meta_ready, xeT_ready, up_ps, biased, hid_ready, hid_ps, hidT_ready, down_ps, ye_ready, added, add_next,
         out_done) = (sem(n) for n in ("xe_ps", "meta_ready", "xeT_ready", "up_ps", "biased", "hid_ready", "hid_ps",
                                       "hidT_ready", "down_ps", "ye_ready", "added", "add_next", "out_done"))
        block = ctx.enter_context(nc.Block())

        @block.sync
        def _(sp):
            def body(n, s):
                v = sp.value_load(tile_start[0:1, at(n)], min_val=0, max_val=(EXPERTS * CAP + (EXPERTS - 1) * P))
                sp.wait_ge(xe_ps, n + 1)
                sp.wait_ge(meta_ready, n + 1)
                sp.dma_start(xe[:, s, :], expert_in[bass.ds(v, P), :]).then_inc(xe_in[s], 16)
            repeat(sp, Own(sp, None), 0, T, XS, 0, body)
            sp.wait_ge(added, 16 * T)
            sp.dma_start(out[:, :], sum_rows[0:N_NODES, :]).then_inc(out_done, 16)
            sp.wait_ge(out_done, 16)

        @block.gpsimd
        def _(pool):
            def body(n, s):
                if not isinstance(n, int) or n:
                    pool.wait_ge(added, n * 16)
                pool.wait_ge(ye_ready, n + 1)
                pool.sem_inc(add_next, 1)
                pool.indirect_dma_start(
                    out=sum_rows[:, :], out_offset=bass.IndirectOffsetOnAxis(ap=rows_of[:, s:s + 1], axis=0),
                    in_=ye[:, s % 2, :], in_offset=None, compute_op=ALU.add).then_inc(added, 16)
            body(0, 0)
            repeat(pool, Own(pool, None), 1, T, XS, 0, body)

        @block.scalar
        def _(act):
            def hidden_back(n, s):
                act.wait_ge(hid_ps, n + 1)
                act.activation(hidT[:, s, :], ps_g[s][:, :], ACT.Copy).then_inc(hidT_ready, 1)

            def gelu(n, s):
                act.wait_ge(biased, n + 1)
                act.activation(hid[:, s, :], hid[:, s, :], ACT.Gelu).then_inc(hid_ready, 1)
            gelu(0, 0)

            def body(n, s):
                hidden_back(n - 1, 1 - s)
                gelu(n, s)
            repeat(act, Own(act, None), 1, T, 2, 0, body)
            hidden_back(T - 1, (T - 1) % 2)

        @block.tensor
        def _(pe):
            pe.sem_inc(xe_ps, XS)

            def rows_across(n, s):
                pe.wait_ge(xe_in[s], slot_count(n, s, 16, XS))
                if not isinstance(n, int) or n >= 2:
                    pe.wait_ge(xeT_ready, n - 1)
                for c in range(KC):
                    m = pe.transpose(ps_x[s % 2][:, c * P:(c + 1) * P], xe[:, s, c * P:(c + 1) * P], ident[:, :])
                m.then_inc(xe_ps, 1)

            def up(n, s):
                e = pe.value_load(tile_expert[0:1, at(n)], min_val=0, max_val=EXPERTS - 1)
                pe.wait_ge(xeT_ready, n + 1)
                for c in range(KC):
                    m = pe.matmul(ps_u[s][:, :], xeT[:, s, c * P:(c + 1) * P], w1_sb[:, at(e), c, :].squeeze(1),
                                  start=c == 0, stop=c == KC - 1)
                m.then_inc(up_ps, 1)

            def hidden_across(n, s):
                pe.wait_ge(hid_ready, n + 1)
                for c in range(FC):
                    m = pe.transpose(ps_g[s][:, c * P:(c + 1) * P], hid[:, s, c * P:(c + 1) * P], ident[:, :])
                m.then_inc(hid_ps, 1)

            def down(n, s):
                e = pe.value_load(tile_expert[0:1, at(n)], min_val=0, max_val=EXPERTS - 1)
                pe.wait_ge(hidT_ready, n + 1)
                if not isinstance(n, int) or n >= 2:
                    pe.wait_ge(ye_ready, n - 1)
                for c in range(FC):
                    m = pe.matmul(ps_y[s][:, 0:DIM], hidT[:, s, c * P:(c + 1) * P], w2_sb[:, at(e), c, :].squeeze(1),
                                  start=c == 0, stop=c == FC - 1)
                m.then_inc(down_ps, 1)

            rows_across(0, 0)
            pe.wait_ge(weights_in, 16 * (2 + 2 * EXPERTS))
            rows_across(1, 1)
            up(0, 0)
            rows_across(2, 2)
            up(1, 1)
            hidden_across(0, 0)

            def body(n, s):
                rows_across(n, s)
                up(n - 1, (s + 1) % 2)
                hidden_across(n - 2, s % 2)
                down(n - 3, (s + 1) % 2)
            body(3, 3)
            body(4, 0)
            repeat(pe, Own(pe, None), 5, T, XS, 0, body)
            up(T - 1, (T - 1) % 2)
            hidden_across(T - 2, (T - 2) % 2)
            down(T - 3, (T - 3) % 2)
            hidden_across(T - 1, (T - 1) % 2)
            down(T - 2, (T - 2) % 2)
            down(T - 1, (T - 1) % 2)

        @block.vector
        def _(dve):
            own = g["dve_steps"]
            own.eng = dve
            dve.sem_inc(meta_ready, XS)
            dve.wait_ge(weights_in, 16 * (2 + 2 * EXPERTS))

            def bias(n, s):
                e = dve.value_load(tile_expert[0:1, at(n)], min_val=0, max_val=EXPERTS - 1)
                dve.wait_ge(xe_ps, n + 1 + XS)
                if not isinstance(n, int) or n >= XS:
                    dve.wait_ge(added, (n - (XS - 1)) * 16)
                own.step(dve.tensor_copy(gates[:, s:s + 1], xe[:, s, DIM + 1:DIM + 2]))
                dve.tensor_copy(rows_of[:, s:s + 1], xe[:, s, DIM:DIM + 1]).then_inc(meta_ready, 1)
                dve.wait_ge(up_ps, n + 1)
                if not isinstance(n, int) or n >= 2:
                    dve.wait_ge(hid_ps, n - 1)
                dve.tensor_tensor(hid[:, s % 2, :], ps_u[s % 2][:, :], b1_sb[:, at(e, FF)], ALU.add).then_inc(biased, 1)

            def rows_back(n, s):
                dve.wait_ge(xe_ps, n + 1 + XS)
                for c in range(KC):
                    m = dve.tensor_scalar(xeT[:, s % 2, c * P:(c + 1) * P], ps_x[s % 2][:, c * P:(c + 1) * P],
                                          affine[:, 0, c:c + 1], affine[:, 1, c:c + 1], ALU.mult, ALU.add)
                m.then_inc(xeT_ready, 1)

            def result(n, s):
                e = dve.value_load(tile_expert[0:1, at(n)], min_val=0, max_val=EXPERTS - 1)
                dve.wait_ge(down_ps, n + 1)
                if not isinstance(n, int) or n >= 2:
                    dve.wait_ge(added, (n - 1) * 16)
                own.do(dve.tensor_tensor(y[:, s % 2, :], ps_y[s % 2][:, 0:DIM], b2_sb[:, at(e, DIM)], ALU.add))
                dve.tensor_scalar(ye[:, s % 2, :], y[:, s % 2, :], gates[:, s:s + 1], None, ALU.mult).then_inc(ye_ready, 1)
            rows_back(0, 0)
            rows_back(1, 1)
            bias(0, 0)
            rows_back(2, 2)
            bias(1, 1)

            def body(n, s):
                rows_back(n + 1, (s + 1) % XS)
                bias(n, s)
                result(n - 2, (s + 2) % XS)
            own.base, own.k = own.base + own.k, 0
            START = 5
            base = own.base
            for n in range(2, START):
                own.base, own.k = base + 2 * (n - 2), 0
                body(n, n % XS)
            own.base, own.k = base + 2 * (START - 2), 0
            repeat(dve, own, START, T - 1, XS, 2, body)
            bias(T - 1, (T - 1) % XS)
            result(T - 3, (T - 3) % XS)
            result(T - 2, (T - 2) % XS)
            result(T - 1, (T - 1) % XS)


_INS = ["x", "src", "dst", "g_W", "g_asrc", "g_adst", "g_bias", "w_qkv", "mem_kv", "w_out", "b_out", "g_out",
        "g_pre", "gamma", "beta", "Wr", "br", "W1", "b1", "W2", "b2"]


def kernel(x, src, dst, L0_gnn_W, L0_gnn_att_src, L0_gnn_att_dst, L0_gnn_bias, L0_mix_t, L0_mix_w_qkv, L0_mix_mem_kv,
           L0_mix_w_out, L0_mix_b_out, L0_mix_g_out, L0_mix_g_pre, L0_ffn_gamma, L0_ffn_beta, L0_ffn_Wr, L0_ffn_br,
           L0_ffn_W1, L0_ffn_b1, L0_ffn_W2, L0_ffn_b2):
    import numpy as _np
    import concourse.bacc as _bacc
    from concourse import mybir as _mybir
    from concourse.bass_utils import run_bass_kernel_spmd as _run

    def edges(a, fill):
        a = _np.pad(_np.asarray(a), (0, BLOCKS * BLOCK - N_EDGES), constant_values=fill)
        return _np.ascontiguousarray(a.reshape(BLOCKS, P, SUB).transpose(1, 0, 2).reshape(P, BLOCKS * SUB))

    values = dict(zip(_INS, [
        _np.pad(_np.asarray(x), ((0, N_PAD - N_NODES), (0, 0))), edges(src, 0), edges(dst, N_PAD + 2 * WIN),
        L0_gnn_W, L0_gnn_att_src, L0_gnn_att_dst, L0_gnn_bias, L0_mix_w_qkv, L0_mix_mem_kv, L0_mix_w_out, L0_mix_b_out,
        L0_mix_g_out, L0_mix_g_pre, L0_ffn_gamma, L0_ffn_beta, L0_ffn_Wr, L0_ffn_br, L0_ffn_W1, L0_ffn_b1, L0_ffn_W2,
        L0_ffn_b2]))
    nc = _bacc.Bacc("TRN2", target_bir_lowering=False, num_devices=1)
    arrays, args = {}, []
    for name in _INS:
        a = _np.ascontiguousarray(values[name])
        arrays[f"in_{name}_dram"] = a
        args.append(nc.dram_tensor(f"in_{name}_dram", a.shape, _mybir.dt.from_np(a.dtype), kind="ExternalInput").ap())
    args.append(nc.dram_tensor("out_0_dram", (N_NODES, DIM), _mybir.dt.float32, kind="ExternalOutput").ap())
    gps_layer(nc, *args)
    r = _run(nc, [arrays], core_ids=[0])
    return r.results[0]["out_0_dram"]
```
